# Optimizing a Trainium2 kernel written in Bass

```python
import numpy as np
import jax
import jax.numpy as jnp

def _softmax(x, axis=-1):
    return jax.nn.softmax(x, axis=axis)

def _gelu(x):
    return jax.nn.gelu(x, approximate=True)

def _silu(x):
    return jax.nn.silu(x)

def _sigmoid(x):
    return jax.nn.sigmoid(x)

def _layernorm(x, axis=-1, eps=1e-05):
    m = jnp.mean(x, axis=axis, keepdims=True)
    v = jnp.var(x, axis=axis, keepdims=True)
    return (x - m) / jnp.sqrt(v + eps)

def _scatter_add(tgt, idx, src, axis=0):
    return tgt.at[idx].add(src)

def _segment_sum(src, seg, n):
    return jax.ops.segment_sum(src, seg, n)
kernel_name = 'mk_perceiver_d2_seqx_r8_5147e6'

def setup_inputs(seed: int=0):
    np.random.seed(seed)
    _w = jnp.asarray

    def _rec_inputs():
        import jax
        import jax.numpy as jnp
        _rk = jax.random.key(seed)
        x = -0.0002928 + 1 * jax.random.normal(jax.random.fold_in(_rk, 1), (128, 32, 128), jnp.float32)
        _lenS = 32 - jax.random.randint(jax.random.fold_in(_rk, 7), (128,), 0, max(1, 32 // 4) + 1, jnp.int32)
        _lenS2 = 257 - jax.random.randint(jax.random.fold_in(_rk, 8), (128,), 0, max(1, 257 // 4) + 1, jnp.int32)
        _ctx_1024P = jax.random.normal(jax.random.fold_in(_rk, 11), (128, 16, 128), jnp.float32)
        _ctx_1024c = jax.random.dirichlet(jax.random.fold_in(_rk, 511), 0.3 * jnp.ones((16,), jnp.float32), (128, 257))
        _ctx_1024t = jnp.einsum('bsk,bkd->bsd', _ctx_1024c, _ctx_1024P)
        _ctx_1024t = _ctx_1024t * jax.lax.rsqrt(jnp.mean(jnp.square(_ctx_1024t)) + 1e-12) * 0.953939
        ctx_1024 = -1.39393e-06 + 0.999914 * (_ctx_1024t + 0.3 * jax.random.normal(jax.random.fold_in(_rk, 611), (128, 257, 128), jnp.float32))
        _validS = jnp.arange(32)[None, :] < _lenS[:, None]
        _validS2 = jnp.arange(257)[None, :] < _lenS2[:, None]
        _causal = jnp.tril(jnp.ones((32, 32), dtype=bool))
        mask_BxS2_ff1 = jnp.where(jnp.ones((128, 257), dtype=bool), 1.0, 0.0).astype(jnp.float32)
        return (x, ctx_1024, mask_BxS2_ff1)
    x, ctx_1024, mask_BxS2_ff1 = _rec_inputs()

    def _L0_xattn_setup():
        import jax, jax.numpy as jnp
        import numpy as np
        NUM_HEADS = 16
        D_MODEL = 128
        D_K = D_MODEL // NUM_HEADS
        B, S = (2, 256)
        key = jax.random.key(seed)
        ks = jax.random.split(key, 8)
        scale = 1.0 / np.sqrt(D_MODEL)
        return {'x': jax.random.normal(ks[0], (B, S, D_MODEL), jnp.float32), 'y': jax.random.normal(ks[1], (B, S, D_MODEL), jnp.float32), 'mask': jnp.ones((B, S), jnp.float32), 'wq': jax.random.normal(ks[2], (D_MODEL, D_MODEL), jnp.float32) * scale, 'bq': jnp.zeros((D_MODEL,), jnp.float32), 'wk': jax.random.normal(ks[3], (D_MODEL, D_MODEL), jnp.float32) * scale, 'bk': jnp.zeros((D_MODEL,), jnp.float32), 'wv': jax.random.normal(ks[4], (D_MODEL, D_MODEL), jnp.float32) * scale, 'bv': jnp.zeros((D_MODEL,), jnp.float32), 'wo': jax.random.normal(ks[5], (D_MODEL, D_MODEL), jnp.float32) * scale, 'bo': jnp.zeros((D_MODEL,), jnp.float32)}
    _L0_xattn_all = _L0_xattn_setup()
    _L0_xattn_in = {k: v for k, v in _L0_xattn_all.items() if k in ('wq', 'bq', 'wk', 'bk', 'wv', 'bv', 'wo', 'bo')}
    del _L0_xattn_all

    def _L0_attn_setup():
        import jax, jax.numpy as jnp
        import numpy as np
        import math
        DIM = 128
        NUM_HEADS = 16
        HEAD_DIM = DIM // NUM_HEADS
        B, S = (2, 256)
        key = jax.random.key(seed)
        ks = jax.random.split(key, 9)
        sc = 0.02
        return {'x': jax.random.normal(ks[0], (B, S, DIM), jnp.float32), 'Wq': jax.random.normal(ks[1], (DIM, DIM), jnp.float32) * sc, 'bq': jax.random.normal(ks[2], (DIM,), jnp.float32) * sc, 'Wk': jax.random.normal(ks[3], (DIM, DIM), jnp.float32) * sc, 'bk': jax.random.normal(ks[4], (DIM,), jnp.float32) * sc, 'Wv': jax.random.normal(ks[5], (DIM, DIM), jnp.float32) * sc, 'bv': jax.random.normal(ks[6], (DIM,), jnp.float32) * sc, 'Wo': jax.random.normal(ks[7], (DIM, DIM), jnp.float32) * sc, 'bo': jax.random.normal(ks[8], (DIM,), jnp.float32) * sc}
    _L0_attn_all = _L0_attn_setup()
    _L0_attn_in = {k: v for k, v in _L0_attn_all.items() if k in ('Wq', 'bq', 'Wk', 'bk', 'Wv', 'bv', 'Wo', 'bo')}
    del _L0_attn_all

    def _L0_ffn_setup():
        import jax, jax.numpy as jnp
        import numpy as np
        DIM = 128

        def _reference_tuple_inner(x, W_r, W_k, W_v, mu_r, mu_k):
            B, T, C = x.shape
            x_prev = jnp.concatenate([jnp.zeros((B, 1, C), x.dtype), x[:, :-1, :]], axis=1)
            xr = mu_r * x + (1.0 - mu_r) * x_prev
            xk = mu_k * x + (1.0 - mu_k) * x_prev
            r = jax.nn.sigmoid(jnp.einsum('btc,dc->btd', xr, W_r))
            k = jnp.einsum('btc,dc->btd', xk, W_k)
            k_act = jnp.square(jax.nn.relu(k))
            out = r * jnp.einsum('btc,dc->btd', k_act, W_v)
            new_state = x[:, -1, :]
            return (out, new_state)
        key = jax.random.key(seed)
        ks = jax.random.split(key, 6)
        B, T, C = (8, 256, DIM)
        x = jax.random.normal(ks[0], (B, T, C), dtype=jnp.float32)
        s = 1.0 / np.sqrt(C)
        W_r = jax.random.uniform(ks[1], (C, C), jnp.float32, -s, s)
        W_k = jax.random.uniform(ks[2], (C, C), jnp.float32, -s, s)
        W_v = jax.random.uniform(ks[3], (C, C), jnp.float32, -s, s)
        mu_r = jax.random.uniform(ks[4], (C,), jnp.float32)
        mu_k = jax.random.uniform(ks[5], (C,), jnp.float32)
        return {'x': x, 'W_r': W_r, 'W_k': W_k, 'W_v': W_v, 'mu_r': mu_r, 'mu_k': mu_k}
    _L0_ffn_all = _L0_ffn_setup()
    _L0_ffn_in = {k: v for k, v in _L0_ffn_all.items() if k in ('W_r', 'W_k', 'W_v', 'mu_r', 'mu_k')}
    del _L0_ffn_all

    def _L1_xattn_setup():
        import jax, jax.numpy as jnp
        import numpy as np
        B, L_ENC, L_DEC, D = (16, 64, 128, 128)
        key = jax.random.key(seed)
        k1, k2, k3, k4, k5, k6 = jax.random.split(key, 6)
        encoder_hc = jax.random.normal(k1, (B, L_ENC, D), dtype=jnp.float32)
        decoder_hq = jax.random.normal(k2, (B, L_DEC, D), dtype=jnp.float32)
        w_sim = jax.random.normal(k3, (3 * D,), dtype=jnp.float32) * 0.02
        b_sim = jax.random.normal(k4, (1,), dtype=jnp.float32) * 0.02
        W_qv = jax.random.normal(k5, (4 * D, D), dtype=jnp.float32) * 0.02
        b_qv = jax.random.normal(k6, (D,), dtype=jnp.float32) * 0.02
        return {'encoder_hc': encoder_hc, 'decoder_hq': decoder_hq, 'w_sim': w_sim, 'b_sim': b_sim, 'W_qv': W_qv, 'b_qv': b_qv}
    _L1_xattn_all = _L1_xattn_setup()
    _L1_xattn_in = {k: v for k, v in _L1_xattn_all.items() if k in ('w_sim', 'b_sim', 'W_qv', 'b_qv')}
    del _L1_xattn_all

    def _L1_attn_setup():
        import jax, jax.numpy as jnp
        import numpy as np
        OFFSETS = tuple(sorted(set(range(0, 33)) | {48, 64, 96, 128, 192, 32, 48, 64, 96, 128, 192}))
        B, N, D, H, FF = (1, 256, 128, 16, 512)
        HD = D // H

        def _ln(x, g, b):
            mu = x.mean(-1, keepdims=True)
            var = ((x - mu) ** 2).mean(-1, keepdims=True)
            return (x - mu) * jax.lax.rsqrt(var + 1e-05) * g + b

        def _shift(a, delta, n):
            if delta == 0:
                return a
            if delta >= n:
                return jnp.zeros_like(a)
            pad = jnp.zeros(a.shape[:2] + (delta,) + a.shape[3:], a.dtype)
            return jnp.concatenate([pad, a[:, :, :n - delta]], axis=2)

        def _block(x, ln1_g, ln1_b, qkv_w, qkv_b, gate_w, gate_b, out_w, out_b, pos_bias, ln2_g, ln2_b, fc1_w, fc1_b, fc2_w, fc2_b):
            b, n, d = x.shape
            h = pos_bias.shape[1]
            hd = d // h
            xn = _ln(x, ln1_g, ln1_b)
            qkv = xn @ qkv_w + qkv_b
            q, k, v = jnp.split(qkv, 3, axis=-1)
            q = q.reshape(b, n, h, hd).transpose(0, 2, 1, 3)
            k = k.reshape(b, n, h, hd).transpose(0, 2, 1, 3)
            v = v.reshape(b, n, h, hd).transpose(0, 2, 1, 3)
            scale = hd ** (-0.5)
            scores = jnp.stack([jnp.einsum('bhnd,bhnd->bhn', q, _shift(k, delta, n)) for delta in OFFSETS], axis=-1) * scale
            scores = scores + pos_bias.T[None, :, None, :]
            offs = jnp.asarray(OFFSETS)
            mask = jnp.arange(n)[:, None] < offs[None, :]
            scores = jnp.where(mask[None, None], -jnp.inf, scores)
            alpha = jax.nn.softmax(scores, axis=-1)
            out = jnp.zeros_like(q)
            for i, delta in enumerate(OFFSETS):
                out = out + alpha[..., i, None] * _shift(v, delta, n)
            flat = out.transpose(0, 2, 1, 3).reshape(b, n, d)
            gate = jax.nn.sigmoid(xn @ gate_w + gate_b)
            attn_out = flat * gate @ out_w + out_b
            x = x + attn_out
            xn2 = _ln(x, ln2_g, ln2_b)
            ffn = jax.nn.gelu(xn2 @ fc1_w + fc1_b, approximate=False) @ fc2_w + fc2_b
            return x + ffn
        key = jax.random.key(seed)
        ks = jax.random.split(key, 6)
        w = lambda k, sh: jax.random.normal(k, sh, jnp.float32) * 0.02
        x = jax.random.normal(ks[0], (B, N, D), jnp.float32)
        deltas = jnp.log1p(jnp.asarray(OFFSETS, dtype=jnp.float32))
        alphas = jnp.linspace(0.2, 2.0, H).astype(jnp.float32)
        pos_bias = -deltas[:, None] * alphas[None, :]
        return {'x': x, 'ln1_g': jnp.ones((D,), jnp.float32), 'ln1_b': jnp.zeros((D,), jnp.float32), 'qkv_w': w(ks[1], (D, 3 * D)), 'qkv_b': jnp.zeros((3 * D,), jnp.float32), 'gate_w': w(ks[2], (D, D)), 'gate_b': jnp.full((D,), 2.0, jnp.float32), 'out_w': w(ks[3], (D, D)), 'out_b': jnp.zeros((D,), jnp.float32), 'pos_bias': pos_bias, 'ln2_g': jnp.ones((D,), jnp.float32), 'ln2_b': jnp.zeros((D,), jnp.float32), 'fc1_w': w(ks[4], (D, FF)), 'fc1_b': jnp.zeros((FF,), jnp.float32), 'fc2_w': w(ks[5], (FF, D)), 'fc2_b': jnp.zeros((D,), jnp.float32)}
    _L1_attn_all = _L1_attn_setup()
    _L1_attn_in = {k: v for k, v in _L1_attn_all.items() if k in ('ln1_g', 'ln1_b', 'qkv_w', 'qkv_b', 'gate_w', 'gate_b', 'out_w', 'out_b', 'pos_bias', 'ln2_g', 'ln2_b', 'fc1_w', 'fc1_b', 'fc2_w', 'fc2_b')}
    del _L1_attn_all

    def _L1_ffn_setup():
        import jax, jax.numpy as jnp
        import numpy as np
        D = 128
        F = 128
        E = 8
        K = 2
        B, T = (2, 256)

        def _moe_forward(x, router_w, w1, w2, shared_gate_up, shared_down, shared_gate_w):
            b, t, d = x.shape
            xf = x.reshape(-1, d)
            n = xf.shape[0]
            logits = xf @ router_w
            probs = jax.nn.softmax(logits, axis=-1)
            topw, topi = jax.lax.top_k(probs, K)
            combine = jnp.zeros((n, E), dtype=probs.dtype).at[jnp.arange(n)[:, None], topi].add(topw)
            h = jax.nn.silu(jnp.einsum('nd,edf->nef', xf, w1))
            ye = jnp.einsum('nef,efd->ned', h, w2)
            routed = jnp.einsum('ne,ned->nd', combine, ye)
            gu = xf @ shared_gate_up
            gate, up = (gu[:, :F], gu[:, F:])
            shared = jax.nn.silu(gate) * up @ shared_down
            shared = jax.nn.sigmoid(xf @ shared_gate_w) * shared
            return (routed + shared).reshape(b, t, d)
        key = jax.random.key(seed)
        ks = jax.random.split(key, 7)
        std = 0.02
        x = jax.random.normal(ks[0], (B, T, D), dtype=jnp.float32)
        router_w = jax.random.normal(ks[1], (D, E), dtype=jnp.float32) * std
        w1 = jax.random.normal(ks[2], (E, D, F), dtype=jnp.float32) * std
        w2 = jax.random.normal(ks[3], (E, F, D), dtype=jnp.float32) * std
        shared_gate_up = jax.random.normal(ks[4], (D, 2 * F), dtype=jnp.float32) * std
        shared_down = jax.random.normal(ks[5], (F, D), dtype=jnp.float32) * std
        shared_gate_w = jax.random.normal(ks[6], (D, 1), dtype=jnp.float32) * std
        return {'x': x, 'router_w': router_w, 'w1': w1, 'w2': w2, 'shared_gate_up': shared_gate_up, 'shared_down': shared_down, 'shared_gate_w': shared_gate_w}
    _L1_ffn_all = _L1_ffn_setup()
    _L1_ffn_in = {k: v for k, v in _L1_ffn_all.items() if k in ('router_w', 'w1', 'w2', 'shared_gate_up', 'shared_down', 'shared_gate_w')}
    del _L1_ffn_all
    return {'x': x, 'ctx_1024': ctx_1024, 'mask_BxS2_ff1': mask_BxS2_ff1, 'L0_xattn_wq': _L0_xattn_in['wq'], 'L0_xattn_bq': _L0_xattn_in['bq'], 'L0_xattn_wk': _L0_xattn_in['wk'], 'L0_xattn_bk': _L0_xattn_in['bk'], 'L0_xattn_wv': _L0_xattn_in['wv'], 'L0_xattn_bv': _L0_xattn_in['bv'], 'L0_xattn_wo': _L0_xattn_in['wo'], 'L0_xattn_bo': _L0_xattn_in['bo'], 'L0_attn_Wq': _L0_attn_in['Wq'], 'L0_attn_bq': _L0_attn_in['bq'], 'L0_attn_Wk': _L0_attn_in['Wk'], 'L0_attn_bk': _L0_attn_in['bk'], 'L0_attn_Wv': _L0_attn_in['Wv'], 'L0_attn_bv': _L0_attn_in['bv'], 'L0_attn_Wo': _L0_attn_in['Wo'], 'L0_attn_bo': _L0_attn_in['bo'], 'L0_ffn_W_r': _L0_ffn_in['W_r'], 'L0_ffn_W_k': _L0_ffn_in['W_k'], 'L0_ffn_W_v': _L0_ffn_in['W_v'], 'L0_ffn_mu_r': _L0_ffn_in['mu_r'], 'L0_ffn_mu_k': _L0_ffn_in['mu_k'], 'L1_xattn_w_sim': _L1_xattn_in['w_sim'], 'L1_xattn_b_sim': _L1_xattn_in['b_sim'], 'L1_xattn_W_qv': _L1_xattn_in['W_qv'], 'L1_xattn_b_qv': _L1_xattn_in['b_qv'], 'L1_attn_ln1_g': _L1_attn_in['ln1_g'], 'L1_attn_ln1_b': _L1_attn_in['ln1_b'], 'L1_attn_qkv_w': _L1_attn_in['qkv_w'], 'L1_attn_qkv_b': _L1_attn_in['qkv_b'], 'L1_attn_gate_w': _L1_attn_in['gate_w'], 'L1_attn_gate_b': _L1_attn_in['gate_b'], 'L1_attn_out_w': _L1_attn_in['out_w'], 'L1_attn_out_b': _L1_attn_in['out_b'], 'L1_attn_pos_bias': _L1_attn_in['pos_bias'], 'L1_attn_ln2_g': _L1_attn_in['ln2_g'], 'L1_attn_ln2_b': _L1_attn_in['ln2_b'], 'L1_attn_fc1_w': _L1_attn_in['fc1_w'], 'L1_attn_fc1_b': _L1_attn_in['fc1_b'], 'L1_attn_fc2_w': _L1_attn_in['fc2_w'], 'L1_attn_fc2_b': _L1_attn_in['fc2_b'], 'L1_ffn_router_w': _L1_ffn_in['router_w'], 'L1_ffn_w1': _L1_ffn_in['w1'], 'L1_ffn_w2': _L1_ffn_in['w2'], 'L1_ffn_shared_gate_up': _L1_ffn_in['shared_gate_up'], 'L1_ffn_shared_down': _L1_ffn_in['shared_down'], 'L1_ffn_shared_gate_w': _L1_ffn_in['shared_gate_w']}

def reference(x, ctx_1024, mask_BxS2_ff1, L0_xattn_wq, L0_xattn_bq, L0_xattn_wk, L0_xattn_bk, L0_xattn_wv, L0_xattn_bv, L0_xattn_wo, L0_xattn_bo, L0_attn_Wq, L0_attn_bq, L0_attn_Wk, L0_attn_bk, L0_attn_Wv, L0_attn_bv, L0_attn_Wo, L0_attn_bo, L0_ffn_W_r, L0_ffn_W_k, L0_ffn_W_v, L0_ffn_mu_r, L0_ffn_mu_k, L1_xattn_w_sim, L1_xattn_b_sim, L1_xattn_W_qv, L1_xattn_b_qv, L1_attn_ln1_g, L1_attn_ln1_b, L1_attn_qkv_w, L1_attn_qkv_b, L1_attn_gate_w, L1_attn_gate_b, L1_attn_out_w, L1_attn_out_b, L1_attn_pos_bias, L1_attn_ln2_g, L1_attn_ln2_b, L1_attn_fc1_w, L1_attn_fc1_b, L1_attn_fc2_w, L1_attn_fc2_b, L1_ffn_router_w, L1_ffn_w1, L1_ffn_w2, L1_ffn_shared_gate_up, L1_ffn_shared_down, L1_ffn_shared_gate_w):
    import jax
    import jax.numpy as jnp

    def _L0_xattn_ref(x, y, mask, wq, bq, wk, bk, wv, bv, wo, bo):
        import jax, jax.numpy as jnp
        import numpy as np
        NUM_HEADS = 16
        D_MODEL = 128
        D_K = D_MODEL // NUM_HEADS
        B, S = (2, 256)
        b, s, d = x.shape

        def split_heads(t):
            return t.reshape(b, -1, NUM_HEADS, D_K).transpose(0, 2, 1, 3)
        q = split_heads(x @ wq.T + bq)
        k = split_heads(y @ wk.T + bk)
        v = split_heads(y @ wv.T + bv)
        scores = jnp.einsum('bhqd,bhkd->bhqk', q, k) / np.sqrt(D_K)
        scores = scores + (1.0 - mask[:, None, None, :]) * -10000.0
        attn = jax.nn.softmax(scores, axis=-1)
        z = jnp.einsum('bhqk,bhkd->bhqd', attn, v)
        z = z.transpose(0, 2, 1, 3).reshape(b, -1, d)
        return z @ wo.T + bo

    def _L0_attn_ref(x, Wq, bq, Wk, bk, Wv, bv, Wo, bo):
        import jax, jax.numpy as jnp
        import numpy as np
        import math
        DIM = 128
        NUM_HEADS = 16
        HEAD_DIM = DIM // NUM_HEADS
        B, S = (2, 256)
        b, s, d = x.shape
        h, hd = (NUM_HEADS, HEAD_DIM)

        def split_heads(t):
            return t.reshape(b, s, h, hd).transpose(0, 2, 1, 3)
        q = split_heads(x @ Wq + bq)
        k = split_heads(x @ Wk + bk)
        v = split_heads(x @ Wv + bv)
        scores = jnp.einsum('bhqd,bhkd->bhqk', q, k) / math.sqrt(hd)
        causal = jnp.tril(jnp.ones((s, s), dtype=bool))
        scores = jnp.where(causal[None, None], scores, jnp.asarray(-10000.0, scores.dtype))
        probs = jax.nn.softmax(scores, axis=-1)
        ctx = jnp.einsum('bhqk,bhkd->bhqd', probs, v)
        ctx = ctx.transpose(0, 2, 1, 3).reshape(b, s, d)
        return ctx @ Wo + bo

    def _L0_ffn_ref(x, W_r, W_k, W_v, mu_r, mu_k):
        import jax, jax.numpy as jnp
        import numpy as np
        DIM = 128

        def _reference_tuple_inner(x, W_r, W_k, W_v, mu_r, mu_k):
            B, T, C = x.shape
            x_prev = jnp.concatenate([jnp.zeros((B, 1, C), x.dtype), x[:, :-1, :]], axis=1)
            xr = mu_r * x + (1.0 - mu_r) * x_prev
            xk = mu_k * x + (1.0 - mu_k) * x_prev
            r = jax.nn.sigmoid(jnp.einsum('btc,dc->btd', xr, W_r))
            k = jnp.einsum('btc,dc->btd', xk, W_k)
            k_act = jnp.square(jax.nn.relu(k))
            out = r * jnp.einsum('btc,dc->btd', k_act, W_v)
            new_state = x[:, -1, :]
            return (out, new_state)
        return _reference_tuple_inner(x, W_r, W_k, W_v, mu_r, mu_k)[0]

    def _L1_xattn_ref(encoder_hc, decoder_hq, w_sim, b_sim, W_qv, b_qv):
        import jax, jax.numpy as jnp
        import numpy as np
        B, L_ENC, L_DEC, D = (16, 64, 128, 128)
        d = encoder_hc.shape[-1]
        w1, w2, w3 = (w_sim[:d], w_sim[d:2 * d], w_sim[2 * d:])
        Sim = (encoder_hc @ w1)[:, :, None] + (decoder_hq @ w2)[:, None, :] + jnp.einsum('bid,bjd->bij', encoder_hc * w3, decoder_hq) + b_sim[0]
        A = jax.nn.softmax(Sim, axis=2)
        hq_hat = jnp.einsum('bij,bjd->bid', A, decoder_hq)
        Batt = jax.nn.softmax(jnp.max(Sim, axis=2), axis=1)
        hc_bar = jnp.einsum('bi,bid->bd', Batt, encoder_hc)[:, None, :]
        hc_hat = jnp.broadcast_to(hc_bar, encoder_hc.shape)
        feats = jnp.concatenate([encoder_hc, hq_hat, encoder_hc * hq_hat, encoder_hc * hc_hat], axis=-1)
        hcq = feats @ W_qv + b_qv
        return hcq

    def _L1_attn_ref(x, ln1_g, ln1_b, qkv_w, qkv_b, gate_w, gate_b, out_w, out_b, pos_bias, ln2_g, ln2_b, fc1_w, fc1_b, fc2_w, fc2_b):
        import jax, jax.numpy as jnp
        import numpy as np
        OFFSETS = tuple(sorted(set(range(0, 33)) | {48, 64, 96, 128, 192, 32, 48, 64, 96, 128, 192}))
        B, N, D, H, FF = (1, 256, 128, 16, 512)
        HD = D // H

        def _ln(x, g, b):
            mu = x.mean(-1, keepdims=True)
            var = ((x - mu) ** 2).mean(-1, keepdims=True)
            return (x - mu) * jax.lax.rsqrt(var + 1e-05) * g + b

        def _shift(a, delta, n):
            if delta == 0:
                return a
            if delta >= n:
                return jnp.zeros_like(a)
            pad = jnp.zeros(a.shape[:2] + (delta,) + a.shape[3:], a.dtype)
            return jnp.concatenate([pad, a[:, :, :n - delta]], axis=2)

        def _block(x, ln1_g, ln1_b, qkv_w, qkv_b, gate_w, gate_b, out_w, out_b, pos_bias, ln2_g, ln2_b, fc1_w, fc1_b, fc2_w, fc2_b):
            b, n, d = x.shape
            h = pos_bias.shape[1]
            hd = d // h
            xn = _ln(x, ln1_g, ln1_b)
            qkv = xn @ qkv_w + qkv_b
            q, k, v = jnp.split(qkv, 3, axis=-1)
            q = q.reshape(b, n, h, hd).transpose(0, 2, 1, 3)
            k = k.reshape(b, n, h, hd).transpose(0, 2, 1, 3)
            v = v.reshape(b, n, h, hd).transpose(0, 2, 1, 3)
            scale = hd ** (-0.5)
            scores = jnp.stack([jnp.einsum('bhnd,bhnd->bhn', q, _shift(k, delta, n)) for delta in OFFSETS], axis=-1) * scale
            scores = scores + pos_bias.T[None, :, None, :]
            offs = jnp.asarray(OFFSETS)
            mask = jnp.arange(n)[:, None] < offs[None, :]
            scores = jnp.where(mask[None, None], -jnp.inf, scores)
            alpha = jax.nn.softmax(scores, axis=-1)
            out = jnp.zeros_like(q)
            for i, delta in enumerate(OFFSETS):
                out = out + alpha[..., i, None] * _shift(v, delta, n)
            flat = out.transpose(0, 2, 1, 3).reshape(b, n, d)
            gate = jax.nn.sigmoid(xn @ gate_w + gate_b)
            attn_out = flat * gate @ out_w + out_b
            x = x + attn_out
            xn2 = _ln(x, ln2_g, ln2_b)
            ffn = jax.nn.gelu(xn2 @ fc1_w + fc1_b, approximate=False) @ fc2_w + fc2_b
            return x + ffn
        return _block(x, ln1_g, ln1_b, qkv_w, qkv_b, gate_w, gate_b, out_w, out_b, pos_bias, ln2_g, ln2_b, fc1_w, fc1_b, fc2_w, fc2_b)

    def _L1_ffn_ref(x, router_w, w1, w2, shared_gate_up, shared_down, shared_gate_w):
        import jax, jax.numpy as jnp
        import numpy as np
        D = 128
        F = 128
        E = 8
        K = 2
        B, T = (2, 256)

        def _moe_forward(x, router_w, w1, w2, shared_gate_up, shared_down, shared_gate_w):
            b, t, d = x.shape
            xf = x.reshape(-1, d)
            n = xf.shape[0]
            logits = xf @ router_w
            probs = jax.nn.softmax(logits, axis=-1)
            topw, topi = jax.lax.top_k(probs, K)
            combine = jnp.zeros((n, E), dtype=probs.dtype).at[jnp.arange(n)[:, None], topi].add(topw)
            h = jax.nn.silu(jnp.einsum('nd,edf->nef', xf, w1))
            ye = jnp.einsum('nef,efd->ned', h, w2)
            routed = jnp.einsum('ne,ned->nd', combine, ye)
            gu = xf @ shared_gate_up
            gate, up = (gu[:, :F], gu[:, F:])
            shared = jax.nn.silu(gate) * up @ shared_down
            shared = jax.nn.sigmoid(xf @ shared_gate_w) * shared
            return (routed + shared).reshape(b, t, d)
        return _moe_forward(x, router_w, w1, w2, shared_gate_up, shared_down, shared_gate_w)
    x = x + _L0_xattn_ref(_layernorm(x, axis=-1), ctx_1024, mask_BxS2_ff1, L0_xattn_wq, L0_xattn_bq, L0_xattn_wk, L0_xattn_bk, L0_xattn_wv, L0_xattn_bv, L0_xattn_wo, L0_xattn_bo)
    x = x + _L0_attn_ref(_layernorm(x, axis=-1), L0_attn_Wq, L0_attn_bq, L0_attn_Wk, L0_attn_bk, L0_attn_Wv, L0_attn_bv, L0_attn_Wo, L0_attn_bo)
    x = x + _L0_ffn_ref(_layernorm(x, axis=-1), L0_ffn_W_r, L0_ffn_W_k, L0_ffn_W_v, L0_ffn_mu_r, L0_ffn_mu_k)
    x = x + _L1_xattn_ref(_layernorm(x, axis=-1), ctx_1024, L1_xattn_w_sim, L1_xattn_b_sim, L1_xattn_W_qv, L1_xattn_b_qv)
    x = x + _L1_attn_ref(_layernorm(x, axis=-1), L1_attn_ln1_g, L1_attn_ln1_b, L1_attn_qkv_w, L1_attn_qkv_b, L1_attn_gate_w, L1_attn_gate_b, L1_attn_out_w, L1_attn_out_b, L1_attn_pos_bias, L1_attn_ln2_g, L1_attn_ln2_b, L1_attn_fc1_w, L1_attn_fc1_b, L1_attn_fc2_w, L1_attn_fc2_b)
    x = x + _L1_ffn_ref(_layernorm(x, axis=-1), L1_ffn_router_w, L1_ffn_w1, L1_ffn_w2, L1_ffn_shared_gate_up, L1_ffn_shared_down, L1_ffn_shared_gate_w)
    return x

_drawn_inputs = setup_inputs


def setup_inputs(seed=0):
    import zlib

    import numpy as np

    out = dict(_drawn_inputs(seed))
    spreads = {'L0_xattn_bq': (0.0, 0.354),
     'L0_xattn_bk': (0.0, 2.0),
     'L0_xattn_bv': (0.0, 0.1),
     'L0_xattn_bo': (0.0, 0.1),
     'L1_attn_ln1_g': (1.0, 0.6),
     'L1_attn_ln1_b': (0.0, 0.8),
     'L1_attn_qkv_b': (0.0, 0.8),
     'L1_attn_gate_b': (2.0, 0.6),
     'L1_attn_out_b': (0.0, 0.1),
     'L1_attn_ln2_g': (1.0, 0.6),
     'L1_attn_ln2_b': (0.0, 0.8),
     'L1_attn_fc1_b': (0.0, 0.8),
     'L1_attn_fc2_b': (0.0, 0.1)}
    factors = {'L0_attn_Wq': 8.0,
     'L0_attn_bq': 64.0,
     'L0_attn_Wk': 8.0,
     'L0_attn_bk': 64.0,
     'L0_attn_bv': 8.0,
     'L0_attn_bo': 3.032,
     'L0_ffn_W_r': 3.202,
     'L0_ffn_mu_r': 7.44,
     'L1_xattn_w_sim': 2.902,
     'L1_xattn_b_qv': 2.887,
     'L1_attn_qkv_w': 4.156,
     'L1_attn_gate_w': 8.0,
     'L1_attn_out_w': 3.472,
     'L1_attn_pos_bias': 8.0,
     'L1_ffn_router_w': 8.0,
     'L1_ffn_w1': 8.0,
     'L1_ffn_w2': 8.0,
     'L1_ffn_shared_gate_up': 8.0,
     'L1_ffn_shared_down': 8.0,
     'L1_ffn_shared_gate_w': 8.0}
    for name, (base, spread) in spreads.items():
        noise = np.random.default_rng([zlib.crc32(name.encode()), seed]).standard_normal(out[name].shape)
        drawn = base * np.exp(spread * noise) if base else spread * noise
        out[name] = jnp.asarray(drawn.astype(out[name].dtype))
    for name, factor in factors.items():
        out[name] = (out[name] * factor).astype(out[name].dtype)
    return out
```

```python
from contextlib import ExitStack

import concourse.bass as bass
import numpy as np
from concourse import mybir

F32 = mybir.dt.float32
ACT = mybir.ActivationFunctionType
ALU = mybir.AluOpType
AXIS_X = mybir.AxisListType.X

P = 128
B, S, D = 128, 32, 128
KEYS = 257
H, DH = 16, 8
BG = P // S
GROUPS = B // BG
CHUNKS = KEYS // P
LAST = CHUNKS * P
HG = P // S
NHG = H // HG
FF = 512
EXPERTS = 8
BIG = 3.0e38
LN_EPS = 1e-5
QK_SCALE = DH ** -0.5


def shape_constants():
    row = np.arange(P)[:, None]
    col = np.arange(P)[None, :]
    sixteen = row < BG * NHG
    tables = {
        "identity": row == col,
        "head": row // DH == np.arange(H)[None, :],
        "head_in_group": (row // DH) % HG == np.arange(HG)[None, :],
        "group_of_d": sixteen & (row % NHG == col // (HG * DH)),
        "sequence_of_row": sixteen & (row // NHG == np.arange(BG)[None, :]),
        "head_block": row // S == (col // DH) % HG,
        "head_of_row": row // S == np.arange(HG)[None, :],
        "same_sequence": row // S == col // S,
        "other_sequence": np.where(row // S == col // S, 0.0, -BIG),
        "causal_bound": np.where(np.arange(S)[None, :] <= row % S, BIG, -10000.0),
        "causal_sum": np.where(np.arange(S)[None, :] <= row % S, 0.0, -1.0e30),
        "expert_rank": EXPERTS - np.arange(EXPERTS)[None, :],
    }
    return {k: np.broadcast_to(v, (P, v.shape[1])).astype(np.float32) for k, v in tables.items()}


CONSTANTS = ["identity", "head", "head_in_group", "group_of_d", "sequence_of_row", "head_block",
             "head_of_row", "same_sequence", "other_sequence", "causal_bound", "causal_sum", "expert_rank"]
CONST_WIDTH = {"identity": P, "head": H, "head_in_group": HG, "group_of_d": P, "sequence_of_row": BG,
               "head_block": P, "head_of_row": HG, "same_sequence": P, "other_sequence": P,
               "causal_bound": S, "causal_sum": S, "expert_rank": EXPERTS}
MATRICES = {"xa_q": D, "xa_k": D, "xa_v": D, "xa_o": D,
            "sa_q": D, "sa_k": D, "sa_v": D, "sa_o": D,
            "cm_r": D, "cm_k": D, "cm_v": D,
            "bi_qv": 4 * D,
            "wa_qkv": 3 * D, "wa_gate": D, "wa_o": D, "wa_fc1": FF, "wa_fc2": (FF // P) * D,
            "moe_router": EXPERTS, "moe_gate_w": 1, "moe_w1": EXPERTS * D, "moe_w2": EXPERTS * D,
            "moe_gate_up": 2 * D, "moe_down": D}
COLUMNS = {"xa_bq": 1, "xa_bk": 1, "xa_bv": 1, "sa_bq": 1, "sa_bk": 1, "sa_bv": 1,
           "cm_mu_r": 1, "cm_mu_k": 1, "bi_w2": 1, "bi_w3": 1,
           "wa_g1": 1, "wa_b1": 1, "wa_bqkv": 3, "wa_bgate": 1, "wa_g2": 1, "wa_b2": 1,
           "wa_bfc1": FF // P}
ROWS = {"xa_bo": D, "sa_bo": D, "bi_w1": D, "bi_bqv": D, "wa_bo": D, "wa_bfc2": D, "bi_b": 1}


def offsets(widths):
    out, at = {}, 0
    for name, width in widths.items():
        out[name] = (at, width)
        at += width
    return out, at


class Group:

    def __init__(self, n, slot, lap):
        self.n, self.slot, self.parity, self.lap = n, slot, slot % 2, lap


class Step:

    def __init__(self, j, base, count, body):
        self.j, self.base, self.count, self.body = j, base, count, body

    def group(self, lag):
        at = self.base - lag
        if isinstance(self.j, int):
            if not 0 <= at < self.count:
                return None
            return Group(at, at % self.body, at // self.body)
        return Group(self.j * self.body + at, at % self.body, self.j + at // self.body)


def steps(engine, count, peel, deepest, body=2):
    assert peel % body == 0 and peel > deepest and (count - peel) % body == 0
    for t in range(peel):
        yield Step(0, t, count, body)
    with engine.Fori(0, (count - peel) // body) as j:
        for u in range(body):
            yield Step(j, peel + u, count, body)
    for t in range(count, count + deepest):
        yield Step(0, t, count, body)


def past(value):
    return not isinstance(value, int) or value > 0


def in_register(engine, value):
    return value if isinstance(value, int) else engine.to_reg(value)


class Memory:

    def __init__(self, nc, stack, prefix):
        self.nc, self.stack, self.prefix, self.semaphores = nc, stack, prefix, []

    def sbuf(self, name, shape):
        return self.stack.enter_context(self.nc.sbuf_tensor(f"{self.prefix}_{name}", shape, F32))

    def psum(self, name, shape):
        return self.stack.enter_context(self.nc.psum_tensor(f"{self.prefix}_{name}", shape, F32))

    def sem(self, name):
        self.semaphores.append(self.nc.alloc_semaphore(f"{self.prefix}_{name}"))
        return self.semaphores[-1]


def clear_finished(nc, shared, mem):
    if shared["finished"]:
        nc.clear_and_free_semaphores(shared["finished"])
    shared["finished"] = mem.semaphores


def cross_attention(nc, shared, ctx_t, mask):
    with ExitStack() as stack:
        mem = Memory(nc, stack, "xa")
        UNITS = BG * NHG // 2
        KCOLS = BG * KEYS
        KPART = [(0, 343), (343, 343), (686, 342)]
        LAG_LN, LAG_FRONT, LAG_STREAM, LAG_TAIL = 0, 1, 2, 3
        PEEL, DEEPEST = 4, 3
        x, const, weight, column, row = (shared[k] for k in ("x", "const", "weight", "column", "row"))

        ctx = [mem.sbuf(f"ctx{i}", [P, KCOLS]) for i in range(2)]
        mask_raw = [mem.sbuf(f"mask_raw{i}", [P, KCOLS]) for i in range(2)]
        mask_add = [mem.sbuf(f"mask_add{i}", [P, KCOLS]) for i in range(2)]
        stats = mem.sbuf("stats", [P, 2, 6])
        moments = mem.sbuf("moments", [P, 2, 2])
        var_eps = mem.sbuf("var_eps", [P, 2])
        rstd = mem.sbuf("rstd", [P, 2])
        xn = mem.sbuf("xn", [P, 2, D])
        xn_t = mem.sbuf("xn_t", [P, 2, P])
        q_t = mem.sbuf("q_t", [P, 2, P])
        q_blocks = [mem.sbuf(f"q_blocks{i}", [P, BG, H, S]) for i in range(2)]
        k_t = [mem.sbuf(f"k_t{i}", [P, KCOLS]) for i in range(2)]
        v = [mem.sbuf(f"v{i}", [P, BG, CHUNKS, D]) for i in range(2)]
        last_ctx = mem.sbuf("last_ctx", [P, 2, BG, NHG])
        last_v = [mem.sbuf(f"last_v{i}", [P, D]) for i in range(2)]
        last_p = mem.sbuf("last_p", [P, BG, P])
        probs = [mem.sbuf(f"probs{i}", [P, BG * NHG, KEYS]) for i in range(2)]
        neg_max = mem.sbuf("neg_max", [P, 2, BG * NHG])
        den = mem.sbuf("den", [P, 2, BG * NHG])
        inv_den = mem.sbuf("inv_den", [P, 2, BG * NHG])
        probs_t = mem.sbuf("probs_t", [P, 4, 2, CHUNKS, P])
        z_heads = mem.sbuf("z_heads", [P, BG, HG, S])
        z_t = mem.sbuf("z_t", [P, BG, S])
        x_bias = mem.sbuf("x_bias", [P, 2, D])
        bias = mem.sbuf("bias", [P, D])

        scores = [mem.psum(f"scores{i}", [P, 2, 512]) for i in range(2)]
        turned = [mem.psum(f"turned{i}", [P, 2, CHUNKS, P]) for i in range(2)]
        z = mem.psum("z", [P, BG, P])
        front = mem.psum("front", [P, 512])

        ctx_loaded = [mem.sem(f"ctx_loaded{i}") for i in range(2)]
        mask_loaded = [mem.sem(f"mask_loaded{i}") for i in range(2)]
        stats_done, moments_done, var_done, rstd_done, xn_done = (
            mem.sem(k) for k in ("stats_done", "moments_done", "var_done", "rstd_done", "xn_done"))
        bias_product, bias_ready, zeroed = mem.sem("bias_product"), mem.sem("bias_ready"), mem.sem("zeroed")
        xn_turned, xn_copied = mem.sem("xn_turned"), mem.sem("xn_copied")
        q_product, q_copied, q_spread = mem.sem("q_product"), mem.sem("q_copied"), mem.sem("q_spread")
        k_product, k_copied = mem.sem("k_product"), mem.sem("k_copied")
        v_product, v_copied = mem.sem("v_product"), mem.sem("v_copied")
        last_ctx_copied = mem.sem("last_ctx_copied")
        last_v_product, last_v_copied = mem.sem("last_v_product"), mem.sem("last_v_copied")
        last_p_turned, last_p_spread = mem.sem("last_p_turned"), mem.sem("last_p_spread")
        mask_ready = mem.sem("mask_ready")
        scored, maxed, exped, inverted, normed = (
            mem.sem(k) for k in ("scored", "maxed", "exped", "inverted", "normed"))
        p_turned, p_copied, pv_done, z_done = (
            mem.sem(k) for k in ("p_turned", "p_copied", "pv_done", "z_done"))
        z_masked, z_summed, o_product = mem.sem("z_masked"), mem.sem("z_summed"), mem.sem("o_product")
        x_biased, x_updated = mem.sem("x_biased"), mem.sem("x_updated")

        def unit_count(g, u):
            return g.n * UNITS + (u + 1)

        def unit_before(tail, stream, u, back):
            return (stream, u - back) if u >= back else (tail, u - back + UNITS)

        block = stack.enter_context(nc.Block())

        @block.sync
        def _(sp):
            def load(n, parity, wait):
                if wait:
                    sp.wait_ge(last_v_product, n - 1)
                    sp.wait_ge(last_ctx_copied, n - 1)
                sp.dma_start(ctx[parity][:, :], ctx_t[:, bass.ds(n * KCOLS, KCOLS)]).then_inc(
                    ctx_loaded[parity], 16)
                if wait:
                    sp.wait_ge(mask_ready, n - 1)
                sp.dma_start(mask_raw[parity][:, :],
                             mask[:, bass.ds(n * KCOLS, KCOLS)].broadcast_to([P, KCOLS])).then_inc(
                    mask_loaded[parity], 16)

            for n in range(2):
                load(n, n, False)
            with sp.Fori(0, (GROUPS - 2) // 2) as j:
                for parity in range(2):
                    load(j * 2 + (2 + parity), parity, True)

        @block.gpsimd
        def _(pool):
            clear_finished(nc, shared, mem)
            pool.wait_ge(shared["loaded"], shared["loaded_count"])
            pool.wait_ge(shared["params"], shared["params_count"])
            for step in steps(pool, GROUPS, PEEL, DEEPEST):
                g = step.group(LAG_LN)
                if g:
                    pool.wait_ge(var_done, g.n + 1)
                    pool.wait_ge(zeroed, 1)
                    nc.gpsimd.tensor_tensor(rstd[:, g.parity:g.parity + 1], var_eps[:, g.parity:g.parity + 1],
                                            shared["minus_half"][:, 0:1], ALU.pow).then_inc(rstd_done, 1)
                f = step.group(LAG_FRONT)
                if f:
                    loads = in_register(pool, (f.lap + 1) * 16)
                    units = in_register(pool, (f.n - 1) * UNITS)
                    pool.wait_ge(zeroed, 1)
                    pool.wait_ge(mask_loaded[f.parity], loads)
                    if past(units):
                        pool.wait_ge(maxed, units)
                    nc.gpsimd.tensor_scalar(mask_add[f.parity][:, :], mask_raw[f.parity][:, :],
                                            -10000.0, 10000.0, ALU.mult, ALU.add).then_inc(mask_ready, 1)
                    pool.wait_ge(q_copied, f.n + 1)
                    if past(f.n - 1):
                        pool.wait_ge(scored, (f.n - 1) * UNITS)
                    for b in range(BG):
                        last = nc.gpsimd.tensor_tensor(
                            q_blocks[f.parity][:, b, :, :],
                            q_t[:, f.parity, b * S:(b + 1) * S].rearrange("p (o q) -> p o q", o=1).broadcast_to([P, H, S]),
                            const["head"].rearrange("p (h o) -> p h o", o=1).broadcast_to([P, H, S]),
                            ALU.mult)
                    last.then_inc(q_spread, 1)
                m = step.group(LAG_TAIL)
                if m:
                    if past(m.n - 1):
                        pool.wait_ge(x_updated, m.n - 1)
                    pool.wait_ge(bias_ready, 1)
                    nc.gpsimd.tensor_tensor(x_bias[:, m.parity, :], x[:, bass.ds(m.n * D, D)], bias[:, :],
                                            ALU.add).then_inc(x_biased, 1)

        @block.tensor
        def _(pe):
            pe.wait_ge(shared["loaded"], shared["loaded_count"])
            pe.wait_ge(shared["params"], shared["params_count"])
            nc.tensor.matmul(front[:, 0:D], column("xa_bv").broadcast_to([P, P]), weight("xa_o"),
                             start=True, stop=True).then_inc(bias_product, 1)
            pe.wait_ge(bias_ready, 1)
            for step in steps(pe, GROUPS, PEEL, DEEPEST):
                f, n, m = step.group(LAG_FRONT), step.group(LAG_STREAM), step.group(LAG_TAIL)
                for u in range(UNITS):
                    if n:
                        b, gp = u // 2, u % 2
                        if u == 0:
                            pe.wait_ge(q_spread, n.n + 1)
                            pe.wait_ge(k_copied, (n.n + 1) * 3)
                        if past(unit_count(n, u) - 2):
                            pe.wait_ge(exped, unit_count(n, u) - 2)
                        for i in range(2):
                            g = gp * 2 + i
                            mm = nc.tensor.matmul(
                                scores[u % 2][:, i, 0:KEYS],
                                q_blocks[n.parity][:, b, g * HG:(g + 1) * HG, :].rearrange("p h q -> p (h q)"),
                                k_t[n.parity][:, b * KEYS:(b + 1) * KEYS], start=True, stop=True)
                        mm.then_inc(scored, 1)
                    w, wu = unit_before(m, n, u, 2)
                    if w:
                        pe.wait_ge(normed, unit_count(w, wu))
                        if past(unit_count(w, wu) - 2):
                            pe.wait_ge(p_copied, unit_count(w, wu) - 2)
                        for i in range(2):
                            for c in range(CHUNKS):
                                mm = nc.tensor.transpose(
                                    turned[u % 2][:, i, c, :],
                                    probs[w.parity][:, wu * 2 + i, c * P:(c + 1) * P], const["identity"])
                        mm.then_inc(p_turned, 1)
                    w, wu = unit_before(m, n, u, 4)
                    if u % 2 == 0 and w:
                        b = wu // 2
                        pe.wait_ge(p_copied, unit_count(w, wu + 1))
                        if b == 0:
                            pe.wait_ge(v_copied, (w.n + 1) * 2)
                            if past(w.n):
                                pe.wait_ge(z_masked, w.n)
                        for c in range(CHUNKS):
                            for g in range(NHG):
                                rows = slice(g * HG * DH, (g + 1) * HG * DH)
                                mm = nc.tensor.matmul(
                                    z[rows, b, :], v[w.parity][:, b, c, rows],
                                    probs_t[:, (wu + g // 2) % 4, g % 2, c, :],
                                    start=(b == 0 and c == 0), stop=False, skip_group_check=True)
                        mm.then_inc(pv_done, 1)
                        if b == BG - 1:
                            pe.wait_ge(last_v_copied, w.n + 1)
                            pe.wait_ge(last_p_spread, w.n + 1)
                            nc.tensor.matmul(z[:, :, :].rearrange("p b k -> p (b k)"), last_v[w.parity][:, :],
                                             last_p[:, :, :].rearrange("p b k -> p (b k)"),
                                             start=False, stop=True, skip_group_check=True).then_inc(z_done, 1)
                    if f and u == 0:
                        pe.wait_ge(xn_done, f.n + 1)
                        if past(f.n):
                            pe.wait_ge(last_v_copied, f.n)
                        if m and past(m.n):
                            pe.wait_ge(x_updated, m.n)
                        nc.tensor.transpose(front[:, 0:P], xn[:, f.parity, :], const["identity"]).then_inc(xn_turned, 1)
                    if m and u == 1:
                        pe.wait_ge(normed, (m.n + 1) * UNITS)
                        if f:
                            pe.wait_ge(xn_copied, f.n + 1)
                        elif past(m.n):
                            pe.wait_ge(x_updated, m.n)
                        nc.tensor.transpose(front[0:BG * NHG, 256:256 + P], probs[m.parity][:, :, LAST],
                                            const["identity"]).then_inc(last_p_turned, 1)
                    if f and u == 1:
                        pe.wait_ge(xn_copied, f.n + 1)
                        nc.tensor.matmul(front[:, P:2 * P], weight("xa_q"), xn_t[:, f.parity, :],
                                         start=True, stop=True).then_inc(q_product, 1)
                    if f and 2 <= u < 5:
                        at, width = KPART[u - 2]
                        if u == 2:
                            pe.wait_ge(ctx_loaded[f.parity], (f.lap + 1) * 16)
                            pe.wait_ge(q_copied, f.n + 1)
                            if m:
                                pe.wait_ge(last_p_spread, m.n + 1)
                        else:
                            pe.wait_ge(k_copied, f.n * 3 + (u - 2))
                        nc.tensor.matmul(front[:, 0:width], weight("xa_k"), ctx[f.parity][:, at:at + width],
                                         start=True, stop=True).then_inc(k_product, 1)
                    if f and 5 <= u < 7:
                        if u == 5:
                            pe.wait_ge(k_copied, (f.n + 1) * 3)
                        else:
                            pe.wait_ge(v_copied, f.n * 2 + 1)
                        for i in range(2):
                            for c in range(CHUNKS):
                                at = (2 * (u - 5) + i) * KEYS + c * P
                                mm = nc.tensor.matmul(front[:, (2 * i + c) * D:(2 * i + c + 1) * D],
                                                      ctx[f.parity][:, at:at + P], weight("xa_v"),
                                                      start=True, stop=True)
                        mm.then_inc(v_product, 1)
                    if f and u == 7:
                        pe.wait_ge(v_copied, (f.n + 1) * 2)
                        pe.wait_ge(last_ctx_copied, f.n + 1)
                        nc.tensor.matmul(front[0:BG * NHG, 0:D],
                                         last_ctx[:, f.parity, :, :].rearrange("p b g -> p (b g)"), weight("xa_v"),
                                         start=True, stop=True).then_inc(last_v_product, 1)
                    if m and u == 7:
                        pe.wait_ge(z_summed, m.n + 1)
                        nc.tensor.matmul(front[:, 384:384 + D], z_t[:, :, :].rearrange("p b q -> p (b q)"),
                                         weight("xa_o"), start=True, stop=True).then_inc(o_product, 1)

        @block.scalar
        def _(act):
            act.wait_ge(shared["loaded"], shared["loaded_count"])
            act.wait_ge(shared["params"], shared["params_count"])
            for step in steps(act, GROUPS, PEEL, DEEPEST):
                f, n, m = step.group(LAG_FRONT), step.group(LAG_STREAM), step.group(LAG_TAIL)
                for u in range(UNITS):
                    w, wu = unit_before(m, n, u, 2)
                    if w:
                        act.wait_ge(p_turned, unit_count(w, wu))
                        if past(w.n * BG + (wu // 2 - 1)):
                            act.wait_ge(pv_done, w.n * BG + (wu // 2 - 1))
                        nc.scalar.activation(probs_t[:, wu % 4, :, :, :], turned[u % 2][:, :, :, :],
                                             ACT.Copy).then_inc(p_copied, 1)
                    if n:
                        act.wait_ge(maxed, unit_count(n, u))
                        if u == 0 and past(n.n - 1):
                            act.wait_ge(last_p_turned, n.n - 1)
                        for i in range(2):
                            k = u * 2 + i
                            last = nc.scalar.activation(
                                probs[n.parity][:, k, :], scores[u % 2][:, i, 0:KEYS], ACT.Exp,
                                bias=neg_max[:, n.parity, k:k + 1], scale=-1.0,
                                accum_out=den[:, n.parity, k:k + 1])
                        last.then_inc(exped, 1)
                    if f and u == 0:
                        act.wait_ge(xn_turned, f.n + 1)
                        nc.scalar.activation(xn_t[:, f.parity, :], front[:, 0:P], ACT.Copy).then_inc(xn_copied, 1)
                    if f and u == 1:
                        act.wait_ge(ctx_loaded[f.parity], (f.lap + 1) * 16)
                        if past(f.n - 1):
                            act.wait_ge(last_v_product, f.n - 1)
                        nc.scalar.activation(
                            last_ctx[:, f.parity, :, :],
                            ctx[f.parity][:, :].rearrange("p (b k) -> p b k", b=BG)[:, :, LAST:KEYS].broadcast_to([P, BG, NHG]),
                            ACT.Copy).then_inc(last_ctx_copied, 1)
                    if f and 2 <= u < 5:
                        at, width = KPART[u - 2]
                        act.wait_ge(k_product, f.n * 3 + (u - 1))
                        if u == 2 and past(f.n - 1):
                            act.wait_ge(scored, (f.n - 1) * UNITS)
                        nc.scalar.activation(k_t[f.parity][:, at:at + width], front[:, 0:width], ACT.Identity,
                                             bias=column("xa_bk")).then_inc(k_copied, 1)
                    if f and 5 <= u < 7:
                        act.wait_ge(v_product, f.n * 2 + (u - 4))
                        if u == 5 and past(f.n - 1):
                            act.wait_ge(pv_done, (f.n - 1) * BG)
                        nc.scalar.activation(
                            v[f.parity][:, 2 * (u - 5):2 * (u - 4), :, :].rearrange("p b c d -> p (b c d)"),
                            front[:, 0:512], ACT.Copy).then_inc(v_copied, 1)

        @block.vector
        def _(dve):
            dve.wait_ge(shared["loaded"], shared["loaded_count"])
            dve.wait_ge(shared["params"], shared["params_count"])
            for t in (last_p[:, :, :], last_v[0][:, :], last_v[1][:, :]):
                last = nc.vector.memset(t, 0.0)
            last.then_inc(zeroed, 1)
            dve.wait_ge(zeroed, 1)
            dve.wait_ge(bias_product, 1)
            nc.vector.tensor_tensor(bias[:, :], front[:, 0:D], row("xa_bo"), ALU.add).then_inc(bias_ready, 1)
            for step in steps(dve, GROUPS, PEEL, DEEPEST):
                g = step.group(LAG_LN)
                f, n, m = step.group(LAG_FRONT), step.group(LAG_STREAM), step.group(LAG_TAIL)
                for u in range(UNITS):
                    w, wu = unit_before(m, n, u, 1)
                    if w:
                        dve.wait_ge(exped, unit_count(w, wu))
                        nc.vector.reciprocal(inv_den[:, w.parity, wu * 2:wu * 2 + 2],
                                             den[:, w.parity, wu * 2:wu * 2 + 2]).then_inc(inverted, 1)
                        dve.wait_ge(inverted, unit_count(w, wu))
                        for i in range(2):
                            k = wu * 2 + i
                            last = nc.vector.tensor_scalar(probs[w.parity][:, k, :], probs[w.parity][:, k, :],
                                                           inv_den[:, w.parity, k:k + 1], None, ALU.mult)
                        last.then_inc(normed, 1)
                    if n:
                        b = u // 2
                        units = in_register(dve, unit_count(n, u))
                        masks = in_register(dve, n.n + 1)
                        dve.wait_ge(zeroed, 1)
                        dve.wait_ge(scored, units)
                        if u == 0:
                            dve.wait_ge(mask_ready, masks)
                        for i in range(2):
                            k = u * 2 + i
                            last = nc.vector.tensor_tensor_reduce(
                                scores[u % 2][:, i, 0:KEYS], scores[u % 2][:, i, 0:KEYS],
                                mask_add[n.parity][:, b * KEYS:(b + 1) * KEYS], 1.0, BIG, ALU.add, ALU.min,
                                neg_max[:, n.parity, k:k + 1])
                        last.then_inc(maxed, 1)
                    if m and u == 1:
                        dve.wait_ge(last_p_turned, m.n + 1)
                        if f:
                            dve.wait_ge(q_product, f.n + 1)
                        if past(m.n):
                            dve.wait_ge(z_done, m.n)
                        nc.vector.tensor_tensor(
                            last_p[0:BG * NHG, :, :],
                            front[0:BG * NHG, 256:256 + P].rearrange("p (o k) -> p o k", o=1).broadcast_to([BG * NHG, BG, P]),
                            const["sequence_of_row"][0:BG * NHG, :].rearrange("p (b o) -> p b o", o=1).broadcast_to([BG * NHG, BG, P]),
                            ALU.mult).then_inc(last_p_spread, 1)
                    if f and u == 1:
                        dve.wait_ge(q_product, f.n + 1)
                        if past(f.n - 1):
                            dve.wait_ge(q_spread, f.n - 1)
                        nc.vector.tensor_scalar(q_t[:, f.parity, :], front[:, P:2 * P], column("xa_bq"), -QK_SCALE,
                                                ALU.add, ALU.mult).then_inc(q_copied, 1)
                    if m and u == 3:
                        dve.wait_ge(z_done, m.n + 1)
                        nc.vector.tensor_tensor(
                            z_heads[:, :, :, :], z[:, :, :].rearrange("p b (h q) -> p b h q", h=HG),
                            const["head_in_group"].rearrange("p (o h i) -> p o h i", o=1, i=1).broadcast_to([P, BG, HG, S]),
                            ALU.mult).then_inc(z_masked, 1)
                        dve.wait_ge(z_masked, m.n + 1)
                        if past(m.n):
                            dve.wait_ge(o_product, m.n)
                        nc.vector.tensor_reduce(z_t[:, :, :], z_heads[:, :, :, :].rearrange("p b h q -> p b q h"),
                                                AXIS_X, ALU.add).then_inc(z_summed, 1)
                    if f and u == 7:
                        dve.wait_ge(last_v_product, f.n + 1)
                        if m:
                            dve.wait_ge(o_product, m.n + 1)
                        if past(f.n - 1):
                            dve.wait_ge(z_done, f.n - 1)
                        nc.vector.tensor_tensor(last_v[f.parity][0:BG * NHG, :], front[0:BG * NHG, 0:D],
                                                const["group_of_d"][0:BG * NHG, :], ALU.mult).then_inc(last_v_copied, 1)
                    if m and u == 7:
                        dve.wait_ge(o_product, m.n + 1)
                        dve.wait_ge(x_biased, m.n + 1)
                        nc.vector.tensor_tensor(x[:, bass.ds(m.n * D, D)], front[:, 384:384 + D],
                                                x_bias[:, m.parity, :], ALU.add).then_inc(x_updated, 1)
                    if g and u == 4:
                        if past(g.n - 1):
                            dve.wait_ge(rstd_done, g.n - 1)
                        k = g.parity
                        nc.vector.bn_stats(stats[:, k, :], x[:, bass.ds(g.n * D, D)]).then_inc(stats_done, 1)
                        groups_done = in_register(dve, g.n + 1)
                        dve.wait_ge(zeroed, 1)
                        dve.wait_ge(stats_done, groups_done)
                        nc.vector.bn_aggr(moments[:, k, :], stats[:, k, :]).then_inc(moments_done, 1)
                        dve.wait_ge(moments_done, g.n + 1)
                        nc.vector.tensor_scalar(var_eps[:, k:k + 1], moments[:, k, 1:2], LN_EPS, None,
                                                ALU.add).then_inc(var_done, 1)
                    if g and u == 7:
                        dve.wait_ge(rstd_done, g.n + 1)
                        if past(g.n - 1):
                            dve.wait_ge(xn_turned, g.n - 1)
                        nc.vector.tensor_scalar(xn[:, g.parity, :], x[:, bass.ds(g.n * D, D)],
                                                moments[:, g.parity, 0:1], rstd[:, g.parity:g.parity + 1],
                                                ALU.subtract, ALU.mult).then_inc(xn_done, 1)


def self_attention(nc, shared, name, windowed, window_bias=None, inner=None):
    with ExitStack() as stack:
        mem = Memory(nc, stack, name)
        LAG_LN, LAG_QK, LAG_BLOCK, LAG_SCORE, LAG_VALUE, LAG_OUT = 0, 1, 2, 3, 4, 5
        PEEL, DEEPEST = 6, 5
        VW = HG * DH + HG
        KEY_BLOCKS_ON_POOL = 3
        x, const, weight, column, row = (shared[k] for k in ("x", "const", "weight", "column", "row"))
        if windowed:
            w_q, w_k, w_v = (weight("wa_qkv", i) for i in range(3))
            b_q, b_k, b_v = (column("wa_bqkv", i, 1) for i in range(3))
            w_o, bias = weight("wa_o"), row("wa_bo")
        else:
            w_q, w_k, w_v = (weight(k) for k in ("sa_q", "sa_k", "sa_v"))
            b_q, b_k, b_v = (column(k) for k in ("sa_bq", "sa_bk", "sa_bv"))
            w_o, bias = weight("sa_o"), row("sa_bo")

        stats = mem.sbuf("stats", [P, 2, 6])
        moments = mem.sbuf("moments", [P, 2, 2])
        NORMS = 2 if windowed else 1
        var_eps = mem.sbuf("var_eps", [P, 2, NORMS])
        rstd = mem.sbuf("rstd", [P, 2, NORMS])
        xn = mem.sbuf("xn", [P, 2, D])
        xn_t = [mem.sbuf(f"xn_t{i}", [P, BG, HG, S]) for i in range(2)]
        q_t = mem.sbuf("q_t", [P, 2, BG, S])
        k_t = mem.sbuf("k_t", [P, 2, BG, S])
        k_blocks = [mem.sbuf(f"k_blocks{i}", [P, BG, H, S]) for i in range(2)]
        v_blocks = [mem.sbuf(f"v_blocks{i}", [P, BG, NHG, VW]) for i in range(2)]
        shifted = mem.sbuf("shifted", [P, 2, H, S])
        maxima = mem.sbuf("maxima", [P, 2, H])
        probs = mem.sbuf("probs", [P, 2, H, S])
        probs_t = mem.sbuf("probs_t", [P, 2, NHG, P])
        inv_den = mem.sbuf("inv_den", [P, 2, NHG, HG])
        z_rows = mem.sbuf("z_rows", [P, 2, D])
        z_t = mem.sbuf("z_t", [P, 2, P])
        x_bias = mem.sbuf("x_bias", [P, 2, D])
        scaled = mem.sbuf("scaled", [P, 3])
        if windowed:
            distance_bias = mem.sbuf("distance_bias", [P, H, S])
            gate = mem.sbuf("gate", [P, GROUPS * P])
            z_gated = mem.sbuf("z_gated", [P, 2, P])

        xt_bank = mem.psum("xt_bank", [P, 512])
        qk_bank = mem.psum("qk_bank", [P, 512])
        v_bank = mem.psum("v_bank", [P, BG, NHG, HG * DH])
        score_bank = mem.psum("score_bank", [P, H, S])
        pt_bank = mem.psum("pt_bank", [P, NHG, P])
        z_bank = mem.psum("z_bank", [P, 512])
        zt_bank = mem.psum("zt_bank", [P, 512])
        o_bank = mem.psum("o_bank", [P, 512])

        (prepared, bias_loaded, stats_done, moments_done, var_done, rstd_done, xn_done, xn_turned, xn_copied,
         qk_product, q_copied, k_copied, pool_blocks, dve_blocks, v_product, v_blocked, scored, bounded,
         maxed, shift_done, exped, p_turned, p_copied, pv_done, inverted, z_normed, z_turned, z_copied,
         gate_done, gated, o_product, x_biased, x_updated) = (mem.sem(k) for k in (
             "prepared", "bias_loaded", "stats_done", "moments_done", "var_done", "rstd_done", "xn_done",
             "xn_turned", "xn_copied", "qk_product", "q_copied", "k_copied", "pool_blocks", "dve_blocks",
             "v_product", "v_blocked", "scored", "bounded", "maxed", "shift_done", "exped", "p_turned",
             "p_copied", "pv_done", "inverted", "z_normed", "z_turned", "z_copied", "gate_done", "gated",
             "o_product", "x_biased", "x_updated"))
        PREPARED = 6 if windowed else 3
        y_done = mem.sem("y_done") if windowed else None
        residual = inner if windowed else x

        def key_block(engine, parity, b):
            return engine.tensor_tensor(
                k_blocks[parity][:, b, :, :],
                k_t[:, parity, b, :].rearrange("p (o k) -> p o k", o=1).broadcast_to([P, H, S]),
                const["head"].rearrange("p (h o) -> p h o", o=1).broadcast_to([P, H, S]), ALU.mult)

        block = stack.enter_context(nc.Block())

        if windowed:
            @block.sync
            def _(sp):
                for b in range(BG):
                    sp.dma_start(distance_bias[b * S:(b + 1) * S, :, :].rearrange("p h k -> p (h k)"),
                                 window_bias).then_inc(bias_loaded, 16)

        @block.gpsimd
        def _(pool):
            clear_finished(nc, shared, mem)
            for step in steps(pool, GROUPS, PEEL, DEEPEST):
                g, f, m = step.group(LAG_LN), step.group(LAG_BLOCK), step.group(LAG_OUT)
                if g:
                    pool.wait_ge(var_done, g.n + 1)
                    pool.wait_ge(prepared, PREPARED)
                    nc.gpsimd.tensor_tensor(rstd[:, g.parity, :], var_eps[:, g.parity, :],
                                            shared["minus_half"][:, 0:NORMS], ALU.pow).then_inc(rstd_done, 1)
                if m:
                    if windowed:
                        pool.wait_ge(y_done, m.n + 1)
                    if past(m.n - 1):
                        pool.wait_ge(x_updated, m.n - 1)
                    pool.wait_ge(prepared, PREPARED)
                    nc.gpsimd.tensor_tensor(x_bias[:, m.parity, :], residual[:, bass.ds(m.n * D, D)], bias,
                                            ALU.add).then_inc(x_biased, 1)
                if f:
                    pool.wait_ge(k_copied, f.n + 1)
                    if past(f.n - 1):
                        pool.wait_ge(scored, f.n - 1)
                    for b in range(KEY_BLOCKS_ON_POOL):
                        last = key_block(nc.gpsimd, f.parity, b)
                    last.then_inc(pool_blocks, 1)

        @block.tensor
        def _(pe):
            pe.wait_ge(prepared, PREPARED)
            for step in steps(pe, GROUPS, PEEL, DEEPEST):
                f, v, n, w, m = (step.group(k) for k in (LAG_QK, LAG_BLOCK, LAG_SCORE, LAG_VALUE, LAG_OUT))
                if f:
                    pe.wait_ge(xn_done, f.n + 1)
                    if past(f.n):
                        pe.wait_ge(xn_copied, f.n)
                    nc.tensor.transpose(xt_bank[:, 0:P], xn[:, f.parity, :], const["identity"]).then_inc(xn_turned, 1)
                if n:
                    pe.wait_ge(q_copied, n.n + 1)
                    pe.wait_ge(pool_blocks, n.n + 1)
                    pe.wait_ge(dve_blocks, n.n + 1)
                    if past(n.n):
                        pe.wait_ge(bounded, n.n)
                    for b in range(BG):
                        mm = nc.tensor.matmul(score_bank[b * S:(b + 1) * S, :, :].rearrange("p h k -> p (h k)"),
                                              q_t[:, n.parity, b, :],
                                              k_blocks[n.parity][:, b, :, :].rearrange("p h k -> p (h k)"),
                                              start=True, stop=True)
                    mm.then_inc(scored, 1)
                if w:
                    pe.wait_ge(exped, w.n + 1)
                    if past(w.n):
                        pe.wait_ge(p_copied, w.n)
                    for g in range(NHG):
                        mm = nc.tensor.transpose(
                            pt_bank[:, g, :],
                            probs[:, w.parity, g * HG:(g + 1) * HG, :].rearrange("p h k -> p (h k)"),
                            const["identity"])
                    mm.then_inc(p_turned, 1)
                if v:
                    if past(v.n):
                        pe.wait_ge(v_blocked, v.n)
                    for b in range(BG):
                        mm = nc.tensor.matmul(v_bank[:, b, :, :].rearrange("p g d -> p (g d)"),
                                              xn_t[v.parity][:, b, :, :].rearrange("p r k -> p (r k)"), w_v,
                                              start=True, stop=True)
                    mm.then_inc(v_product, 1)
                if f:
                    pe.wait_ge(xn_copied, f.n + 1)
                    if past(f.n):
                        pe.wait_ge(gate_done if windowed else k_copied, f.n)
                    tokens = xn_t[f.parity][:, :, 0, :]
                    products = [w_q, w_k] + ([weight("wa_gate")] if windowed else [])
                    for i, w_i in enumerate(products):
                        mm = nc.tensor.matmul(qk_bank[:, i * P:(i + 1) * P].rearrange("p (b k) -> p b k", b=BG),
                                              w_i, tokens, start=True, stop=True)
                    mm.then_inc(qk_product, 1)
                if m:
                    pe.wait_ge(z_normed, m.n + 1)
                    if past(m.n):
                        pe.wait_ge(z_copied, m.n)
                    nc.tensor.transpose(zt_bank[:, 0:P], z_rows[:, m.parity, :], const["identity"]).then_inc(z_turned, 1)
                if w:
                    pe.wait_ge(p_copied, w.n + 1)
                    pe.wait_ge(v_blocked, w.n + 1)
                    if past(w.n):
                        pe.wait_ge(z_normed, w.n)
                    for g in range(NHG):
                        for b in range(BG):
                            mm = nc.tensor.matmul(z_bank[b * S:(b + 1) * S, g * VW:(g + 1) * VW],
                                                  probs_t[:, w.parity, g, b * S:(b + 1) * S],
                                                  v_blocks[w.parity][:, b, g, :], start=True, stop=True)
                    mm.then_inc(pv_done, 1)
                if m:
                    pe.wait_ge(gated if windowed else z_copied, m.n + 1)
                    if past(m.n):
                        pe.wait_ge(x_updated, m.n)
                    nc.tensor.matmul(o_bank[:, 0:D], (z_gated if windowed else z_t)[:, m.parity, :], w_o,
                                     start=True, stop=True).then_inc(o_product, 1)

        @block.scalar
        def _(act):
            act.wait_ge(prepared, PREPARED)
            for step in steps(act, GROUPS, PEEL, DEEPEST):
                f, n, w, m = (step.group(k) for k in (LAG_QK, LAG_SCORE, LAG_VALUE, LAG_OUT))
                if f:
                    act.wait_ge(xn_turned, f.n + 1)
                    if past(f.n - 1):
                        act.wait_ge(v_product, f.n - 1)
                    turned = xt_bank[:, 0:P].rearrange("p (b o k) -> p b o k", b=BG, o=1).broadcast_to([P, BG, HG, S])
                    if windowed:
                        last = nc.scalar.activation(xn_t[f.parity][:, :, :, :], turned, ACT.Identity,
                                                    bias=column("wa_b1"), scale=column("wa_g1"))
                    else:
                        last = nc.scalar.activation(xn_t[f.parity][:, :, :, :], turned, ACT.Copy)
                    last.then_inc(xn_copied, 1)
                if w:
                    act.wait_ge(p_turned, w.n + 1)
                    if past(w.n - 1):
                        act.wait_ge(pv_done, w.n - 1)
                    nc.scalar.activation(probs_t[:, w.parity, :, :], pt_bank[:, :, :], ACT.Copy).then_inc(p_copied, 1)
                if f:
                    act.wait_ge(qk_product, f.n + 1)
                    if past(f.n - 1):
                        act.wait_ge(dve_blocks, f.n - 1)
                        act.wait_ge(pool_blocks, f.n - 1)
                    nc.scalar.activation(k_t[:, f.parity, :, :], qk_bank[:, P:2 * P], ACT.Identity,
                                         bias=b_k).then_inc(k_copied, 1)
                    if past(f.n - 1):
                        act.wait_ge(scored, f.n - 1)
                    nc.scalar.activation(q_t[:, f.parity, :, :], qk_bank[:, 0:P], ACT.Identity,
                                         bias=scaled[:, 0:1], scale=QK_SCALE).then_inc(q_copied, 1)
                    if windowed:
                        act.wait_ge(prepared, PREPARED)
                        nc.scalar.activation(gate[:, bass.ds(f.n * P, P)], qk_bank[:, 2 * P:3 * P], ACT.Tanh,
                                             bias=scaled[:, 1:2], scale=0.5).then_inc(gate_done, 1)
                if m:
                    act.wait_ge(z_turned, m.n + 1)
                    if past(m.n - 1):
                        act.wait_ge(gated if windowed else o_product, m.n - 1)
                    if windowed:
                        last = nc.scalar.activation(z_t[:, m.parity, :], zt_bank[:, 0:P], ACT.Identity,
                                                    bias=scaled[:, 2:3], scale=0.5)
                    else:
                        last = nc.scalar.activation(z_t[:, m.parity, :], zt_bank[:, 0:P], ACT.Identity, bias=b_v)
                    last.then_inc(z_copied, 1)
                if n:
                    act.wait_ge(shift_done, n.n + 1)
                    if past(n.n - 1):
                        act.wait_ge(p_turned, n.n - 1)
                    nc.scalar.activation(probs[:, n.parity, :, :], shifted[:, n.parity, :, :],
                                         ACT.Exp).then_inc(exped, 1)

        @block.vector
        def _(dve):
            dve.wait_ge(shared["loaded"], shared["loaded_count"])
            dve.wait_ge(shared["params"], shared["params_count"])
            for i in range(2):
                nc.vector.tensor_copy(
                    v_blocks[i][:, :, :, HG * DH:VW],
                    const["head_of_row"].rearrange("p (a c h) -> p a c h", a=1, c=1).broadcast_to([P, BG, NHG, HG])
                ).then_inc(prepared, 1)
            nc.vector.tensor_scalar(scaled[:, 0:1], b_q, QK_SCALE, None, ALU.mult).then_inc(prepared, 1)
            if windowed:
                nc.vector.tensor_scalar(scaled[:, 1:2], column("wa_bgate"), 0.5, None, ALU.mult).then_inc(prepared, 1)
                nc.vector.tensor_scalar(scaled[:, 2:3], b_v, 0.5, None, ALU.mult).then_inc(prepared, 1)
                dve.wait_ge(bias_loaded, 16 * BG)
                nc.vector.tensor_tensor(
                    distance_bias[:, :, :], distance_bias[:, :, :],
                    const["causal_sum"].rearrange("p (o k) -> p o k", o=1).broadcast_to([P, H, S]),
                    ALU.add).then_inc(prepared, 1)
                dve.wait_ge(prepared, PREPARED)
            for step in steps(dve, GROUPS, PEEL, DEEPEST):
                g, v, n, w, m = (step.group(k) for k in (LAG_LN, LAG_BLOCK, LAG_SCORE, LAG_VALUE, LAG_OUT))
                if g:
                    k = g.parity
                    if past(g.n - 1):
                        dve.wait_ge(rstd_done, g.n - 1)
                    nc.vector.bn_stats(stats[:, k, :], x[:, bass.ds(g.n * D, D)]).then_inc(stats_done, 1)
                if n:
                    dve.wait_ge(scored, n.n + 1)
                    if past(n.n - 1):
                        dve.wait_ge(exped, n.n - 1)
                    if windowed:
                        last = nc.vector.tensor_tensor(shifted[:, n.parity, :, :], score_bank[:, :, :],
                                                       distance_bias[:, :, :], ALU.add)
                    else:
                        last = nc.vector.tensor_tensor(
                            shifted[:, n.parity, :, :], score_bank[:, :, :],
                            const["causal_bound"].rearrange("p (o k) -> p o k", o=1).broadcast_to([P, H, S]),
                            ALU.min)
                    last.then_inc(bounded, 1)
                if g:
                    groups_done = in_register(dve, g.n + 1)
                    dve.wait_ge(prepared, 2)
                    dve.wait_ge(stats_done, groups_done)
                    nc.vector.bn_aggr(moments[:, g.parity, :], stats[:, g.parity, :]).then_inc(moments_done, 1)
                if n:
                    dve.wait_ge(bounded, n.n + 1)
                    nc.vector.tensor_reduce(maxima[:, n.parity, :], shifted[:, n.parity, :, :], AXIS_X,
                                            ALU.max).then_inc(maxed, 1)
                if g:
                    k = g.parity
                    dve.wait_ge(moments_done, g.n + 1)
                    last = nc.vector.tensor_scalar(var_eps[:, k, 0:1], moments[:, k, 1:2], LN_EPS, None, ALU.add)
                    if windowed:
                        last = nc.vector.tensor_scalar(var_eps[:, k, 1:2], moments[:, k, 1:2], 1.0 + LN_EPS,
                                                       LN_EPS * LN_EPS, ALU.mult, ALU.add)
                    last.then_inc(var_done, 1)
                if n:
                    dve.wait_ge(maxed, n.n + 1)
                    nc.vector.tensor_tensor(
                        shifted[:, n.parity, :, :], shifted[:, n.parity, :, :],
                        maxima[:, n.parity, :].rearrange("p (h o) -> p h o", o=1).broadcast_to([P, H, S]),
                        ALU.subtract).then_inc(shift_done, 1)
                if v:
                    dve.wait_ge(k_copied, v.n + 1)
                    if past(v.n - 1):
                        dve.wait_ge(scored, v.n - 1)
                    for b in range(KEY_BLOCKS_ON_POOL, BG):
                        last = key_block(nc.vector, v.parity, b)
                    last.then_inc(dve_blocks, 1)
                if windowed and m:
                    dve.wait_ge(z_copied, m.n + 1)
                    if past(m.n - 1):
                        dve.wait_ge(o_product, m.n - 1)
                    nc.vector.scalar_tensor_tensor(out=z_gated[:, m.parity, :], in0=gate[:, bass.ds(m.n * P, P)],
                                                   scalar=1.0, in1=z_t[:, m.parity, :], op0=ALU.add,
                                                   op1=ALU.mult).then_inc(gated, 1)
                if w:
                    z_of = z_bank[:, 0:NHG * VW].rearrange("p (g c) -> p g c", g=NHG)
                    dve.wait_ge(pv_done, w.n + 1)
                    nc.vector.reciprocal(inv_den[:, w.parity, :, :], z_of[:, :, HG * DH:VW]).then_inc(inverted, 1)
                    dve.wait_ge(inverted, w.n + 1)
                    if past(w.n - 1):
                        dve.wait_ge(z_turned, w.n - 1)
                    nc.vector.tensor_tensor(
                        z_rows[:, w.parity, :].rearrange("p (g h d) -> p g h d", g=NHG, h=HG),
                        z_of[:, :, 0:HG * DH].rearrange("p g (h d) -> p g h d", h=HG),
                        inv_den[:, w.parity, :, :].rearrange("p g (h o) -> p g h o", o=1).broadcast_to([P, NHG, HG, DH]),
                        ALU.mult).then_inc(z_normed, 1)
                if m:
                    dve.wait_ge(o_product, m.n + 1)
                    dve.wait_ge(x_biased, m.n + 1)
                    nc.vector.tensor_tensor(residual[:, bass.ds(m.n * D, D)], o_bank[:, 0:D], x_bias[:, m.parity, :],
                                            ALU.add).then_inc(x_updated, 1)
                if v:
                    dve.wait_ge(v_product, v.n + 1)
                    if past(v.n - 1):
                        dve.wait_ge(pv_done, v.n - 1)
                    nc.vector.tensor_tensor(
                        v_blocks[v.parity][:, :, :, 0:HG * DH], v_bank[:, :, :, :],
                        const["head_block"].rearrange("p (o g d) -> p o g d", o=1, g=NHG).broadcast_to([P, BG, NHG, HG * DH]),
                        ALU.mult).then_inc(v_blocked, 1)
                if g:
                    dve.wait_ge(rstd_done, g.n + 1)
                    if past(g.n - 1):
                        dve.wait_ge(xn_turned, g.n - 1)
                    nc.vector.tensor_scalar(xn[:, g.parity, :], x[:, bass.ds(g.n * D, D)],
                                            moments[:, g.parity, 0:1], rstd[:, g.parity, NORMS - 1:NORMS],
                                            ALU.subtract, ALU.mult).then_inc(xn_done, 1)
                if g and windowed:
                    nc.vector.tensor_scalar(inner[:, bass.ds(g.n * D, D)], x[:, bass.ds(g.n * D, D)],
                                            moments[:, g.parity, 0:1], rstd[:, g.parity, 0:1],
                                            ALU.subtract, ALU.mult).then_inc(y_done, 1)


class Norm:

    def __init__(self, nc, mem, shared, ring=2):
        self.nc, self.x, self.minus_half, self.ring = nc, shared["x"], shared["minus_half"], ring
        self.stats = mem.sbuf("stats", [P, 2, 6])
        self.moments = mem.sbuf("moments", [P, 2, 2])
        self.var_eps = mem.sbuf("var_eps", [P, 2])
        self.rstd = mem.sbuf("rstd", [P, 2])
        self.rows = mem.sbuf("xn", [P, ring, D])
        (self.stats_done, self.moments_done, self.var_done, self.rstd_done, self.done) = (
            mem.sem(k) for k in ("stats_done", "moments_done", "var_done", "rstd_done", "xn_done"))

    def moments_on_vector(self, dve, g, constants_made):
        k, nc = g.parity, self.nc
        if past(g.n - 1):
            dve.wait_ge(self.rstd_done, g.n - 1)
        nc.vector.bn_stats(self.stats[:, k, :], self.x[:, bass.ds(g.n * D, D)]).then_inc(self.stats_done, 1)
        groups_done = in_register(dve, g.n + 1)
        dve.wait_ge(*constants_made)
        dve.wait_ge(self.stats_done, groups_done)
        nc.vector.bn_aggr(self.moments[:, k, :], self.stats[:, k, :]).then_inc(self.moments_done, 1)
        dve.wait_ge(self.moments_done, g.n + 1)
        nc.vector.tensor_scalar(self.var_eps[:, k:k + 1], self.moments[:, k, 1:2], LN_EPS, None,
                                ALU.add).then_inc(self.var_done, 1)

    def rstd_on_gpsimd(self, pool, g, constants_made):
        k, nc = g.parity, self.nc
        pool.wait_ge(self.var_done, g.n + 1)
        pool.wait_ge(*constants_made)
        nc.gpsimd.tensor_tensor(self.rstd[:, k:k + 1], self.var_eps[:, k:k + 1], self.minus_half[:, 0:1],
                                ALU.pow).then_inc(self.rstd_done, 1)

    def rows_on_vector(self, dve, g, last_reader):
        k, nc = g.parity, self.nc
        dve.wait_ge(self.rstd_done, g.n + 1)
        if past(g.n - (self.ring - 1)):
            dve.wait_ge(last_reader, g.n - (self.ring - 1))
        nc.vector.tensor_scalar(self.rows[:, g.slot % self.ring, :], self.x[:, bass.ds(g.n * D, D)],
                                self.moments[:, k, 0:1], self.rstd[:, k:k + 1],
                                ALU.subtract, ALU.mult).then_inc(self.done, 1)


def channel_mix(nc, shared):
    with ExitStack() as stack:
        mem = Memory(nc, stack, "cm")
        LAG_LN, LAG_TURN, LAG_MIX, LAG_OUT = 0, 1, 2, 3
        PEEL, DEEPEST = 4, 3
        x, const, weight, column = (shared[k] for k in ("x", "const", "weight", "column"))
        norm = Norm(nc, mem, shared)
        now_t = mem.sbuf("now_t", [P, 2, BG, S])
        before_t = mem.sbuf("before_t", [P, 2, BG, S])
        weights = mem.sbuf("weights", [P, 4, D])
        half_v = mem.sbuf("half_v", [P, D])
        gate = mem.sbuf("gate", [P, 2, D])
        relu_t = mem.sbuf("relu_t", [P, 2, P])
        key_t = mem.sbuf("key_t", [P, 2, P])
        mixed = mem.sbuf("mixed", [P, 2, D])
        xt_bank, r_bank, k_bank, v_bank = (mem.psum(k, [P, 512]) for k in ("xt_bank", "r_bank", "k_bank", "v_bank"))
        (made, turned, now_copied, before_copied, r_product, k_product, gate_done, relu_done, key_done, v_product,
         mixed_done, x_updated) = (mem.sem(k) for k in (
             "made", "turned", "now_copied", "before_copied", "r_product", "k_product", "gate_done",
             "relu_done", "key_done", "v_product", "mixed_done", "x_updated"))
        MADE = 8
        block = stack.enter_context(nc.Block())

        @block.gpsimd
        def _(pool):
            clear_finished(nc, shared, mem)
            pool.wait_ge(made, MADE)
            for step in steps(pool, GROUPS, PEEL, DEEPEST):
                g, f = step.group(LAG_LN), step.group(LAG_TURN)
                if g:
                    norm.rstd_on_gpsimd(pool, g, (made, MADE))
                if f:
                    copies, products = in_register(pool, f.n + 1), in_register(pool, f.n - 1)
                    pool.wait_ge(made, MADE)
                    pool.wait_ge(now_copied, copies)
                    if past(products):
                        pool.wait_ge(k_product, products)
                    nc.gpsimd.tensor_copy(before_t[:, f.parity, :, 1:S],
                                          now_t[:, f.parity, :, 0:S - 1]).then_inc(before_copied, 1)

        @block.tensor
        def _(pe):
            pe.wait_ge(made, MADE)
            for step in steps(pe, GROUPS, PEEL, DEEPEST):
                f, n, m = (step.group(k) for k in (LAG_TURN, LAG_MIX, LAG_OUT))
                if f:
                    pe.wait_ge(norm.done, f.n + 1)
                    if past(f.n):
                        pe.wait_ge(now_copied, f.n)
                    nc.tensor.transpose(xt_bank[:, 0:P], norm.rows[:, f.parity, :], const["identity"]).then_inc(turned, 1)
                if n:
                    now = now_t[:, n.parity, :, :].rearrange("p b s -> p (b s)")
                    before = before_t[:, n.parity, :, :].rearrange("p b s -> p (b s)")
                    pe.wait_ge(before_copied, n.n + 1)
                    if past(n.n):
                        pe.wait_ge(gate_done, n.n)
                    nc.tensor.matmul(r_bank[:, 0:D], now, weights[:, 0, :], start=True, stop=False)
                    nc.tensor.matmul(r_bank[:, 0:D], before, weights[:, 1, :], start=False, stop=True).then_inc(r_product, 1)
                    if past(n.n):
                        pe.wait_ge(relu_done, n.n)
                    nc.tensor.matmul(k_bank[:, 0:P], weights[:, 2, :], now, start=True, stop=False)
                    nc.tensor.matmul(k_bank[:, 0:P], weights[:, 3, :], before, start=False, stop=True).then_inc(k_product, 1)
                if m:
                    pe.wait_ge(key_done, m.n + 1)
                    if past(m.n):
                        pe.wait_ge(mixed_done, m.n)
                    nc.tensor.matmul(v_bank[:, 0:D], key_t[:, m.parity, :], half_v[:, :], start=True,
                                     stop=True).then_inc(v_product, 1)

        @block.scalar
        def _(act):
            act.wait_ge(made, MADE)
            for step in steps(act, GROUPS, PEEL, DEEPEST):
                f, n = step.group(LAG_TURN), step.group(LAG_MIX)
                if f:
                    act.wait_ge(turned, f.n + 1)
                    if past(f.n - 1):
                        act.wait_ge(k_product, f.n - 1)
                    nc.scalar.activation(now_t[:, f.parity, :, :], xt_bank[:, 0:P], ACT.Copy).then_inc(now_copied, 1)
                if n:
                    act.wait_ge(r_product, n.n + 1)
                    if past(n.n - 1):
                        act.wait_ge(mixed_done, n.n - 1)
                    nc.scalar.activation(gate[:, n.parity, :], r_bank[:, 0:D], ACT.Tanh, scale=0.5).then_inc(gate_done, 1)
                    act.wait_ge(k_product, n.n + 1)
                    if past(n.n - 1):
                        act.wait_ge(key_done, n.n - 1)
                    nc.scalar.activation(relu_t[:, n.parity, :], k_bank[:, 0:P], ACT.Relu).then_inc(relu_done, 1)

        @block.vector
        def _(dve):
            dve.wait_ge(shared["loaded"], shared["loaded_count"])
            dve.wait_ge(shared["params"], shared["params_count"])
            for i, (w, mu) in enumerate((("cm_r", "cm_mu_r"), ("cm_k", "cm_mu_k"))):
                nc.vector.tensor_scalar(weights[:, 2 * i, :], weight(w), column(mu), None, ALU.mult).then_inc(made, 1)
                dve.wait_ge(made, 3 * i + 1)
                nc.vector.tensor_scalar(weights[:, 2 * i + 1, :], weight(w), column(mu), None, ALU.mult).then_inc(made, 1)
                dve.wait_ge(made, 3 * i + 2)
                nc.vector.tensor_tensor(weights[:, 2 * i + 1, :], weight(w), weights[:, 2 * i + 1, :],
                                        ALU.subtract).then_inc(made, 1)
            nc.vector.tensor_scalar(half_v[:, :], weight("cm_v"), 0.5, None, ALU.mult).then_inc(made, 1)
            nc.vector.memset(before_t[:, :, :, 0:1], 0.0).then_inc(made, 1)
            for step in steps(dve, GROUPS, PEEL, DEEPEST):
                g, n, m = (step.group(k) for k in (LAG_LN, LAG_MIX, LAG_OUT))
                if g:
                    norm.moments_on_vector(dve, g, (made, 1))
                if n:
                    dve.wait_ge(relu_done, n.n + 1)
                    if past(n.n - 1):
                        dve.wait_ge(v_product, n.n - 1)
                    nc.vector.tensor_tensor(key_t[:, n.parity, :], relu_t[:, n.parity, :], relu_t[:, n.parity, :],
                                            ALU.mult).then_inc(key_done, 1)
                if m:
                    dve.wait_ge(v_product, m.n + 1)
                    dve.wait_ge(gate_done, m.n + 1)
                    nc.vector.scalar_tensor_tensor(out=mixed[:, m.parity, :], in0=gate[:, m.parity, :], scalar=1.0,
                                                   in1=v_bank[:, 0:D], op0=ALU.add, op1=ALU.mult).then_inc(mixed_done, 1)
                    dve.wait_ge(mixed_done, m.n + 1)
                    nc.vector.tensor_tensor(x[:, bass.ds(m.n * D, D)], x[:, bass.ds(m.n * D, D)],
                                            mixed[:, m.parity, :], ALU.add).then_inc(x_updated, 1)
                if g:
                    norm.rows_on_vector(dve, g, turned)


def similarity_attention(nc, shared, ctx_t, ctx_rows, ctx_last):
    with ExitStack() as stack:
        mem = Memory(nc, stack, "bi")
        LAG_LN, LAG_TURN, LAG_SIM, LAG_MIX, LAG_FEATURE, LAG_OUT = 0, 1, 2, 3, 4, 5
        PEEL, DEEPEST, BODY = 8, 5, 4
        KCOLS = BG * KEYS
        x, const, weight, column, row = (shared[k] for k in ("x", "const", "weight", "column", "row"))
        norm = Norm(nc, mem, shared, ring=4)
        keys_t = [mem.sbuf(f"keys_t{i}", [P, KCOLS]) for i in range(2)]
        keys = [mem.sbuf(f"keys{i}", [P, BG, CHUNKS, D]) for i in range(2)]
        last_key = mem.sbuf("last_key", [P, GROUPS, D])
        x_t = mem.sbuf("x_t", [P, 4, P])
        sim_rows = mem.sbuf("sim_rows", [P, 2, P])
        negated = mem.sbuf("negated", [P, 2])
        x_w1 = mem.sbuf("x_w1", [P, 2, D])
        x_part = mem.sbuf("x_part", [P, 4])
        neg_max = mem.sbuf("neg_max", [P, 2])
        row_max = mem.sbuf("row_max", [P, 4])
        probs = mem.sbuf("probs", [P, 2, KEYS])
        den = mem.sbuf("den", [P, 2])
        inv_den = mem.sbuf("inv_den", [P, 2])
        probs_t = mem.sbuf("probs_t", [P, 2, CHUNKS, P])
        maxima = mem.sbuf("maxima", [P, 2, P])
        neg_top = mem.sbuf("neg_top", [P, 2, 2])
        token_exp = mem.sbuf("token_exp", [P, 2, P])
        token_sum = mem.sbuf("token_sum", [P, 2, 2])
        own_exp = mem.sbuf("own_exp", [P, 2, 2])
        token_weights = mem.sbuf("token_weights", [P, 2, P])
        mix_rows = mem.sbuf("mix_rows", [P, 2, D])
        last_part = mem.sbuf("last_part", [P, 2, D])
        mix_t = mem.sbuf("mix_t", [P, 2, P])
        x_mix_t = mem.sbuf("x_mix_t", [P, 2, P])
        x_mean_t = mem.sbuf("x_mean_t", [P, 2, P])
        x_bias = mem.sbuf("x_bias", [P, 2, D])
        (xt_bank, sim_bank, pt_bank, max_bank, mix_bank, mixt_bank, mean_bank, o_bank) = (
            mem.psum(k, [P, 512]) for k in ("xt_bank", "sim_bank", "pt_bank", "max_bank", "mix_bank",
                                            "mixt_bank", "mean_bank", "o_bank"))
        keys_t_loaded = [mem.sem(f"keys_t_loaded{i}") for i in range(2)]
        keys_loaded = [mem.sem(f"keys_loaded{i}") for i in range(2)]
        (made, last_loaded, turned, x_copied, sim_rows_done, x_part_done, sim_done, min_done, exped,
         inverted, normed, row_max_done, p_turned, p_copied, max_spread, top_done, top_negated, token_exped,
         own_exped, sum_inverted, weight_scaled, weights_done, last_part_done, mix_product, mix_done,
         mix_turned, mix_copied, mean_product, x_mixed, x_meaned, o_product, x_biased, x_updated) = (
             mem.sem(k) for k in (
                 "made", "last_loaded", "turned", "x_copied", "sim_rows_done", "x_part_done", "sim_done",
                 "min_done", "exped", "inverted", "normed", "row_max_done", "p_turned", "p_copied",
                 "max_spread", "top_done", "top_negated", "token_exped", "own_exped", "sum_inverted",
                 "weight_scaled", "weights_done", "last_part_done", "mix_product", "mix_done", "mix_turned",
                 "mix_copied", "mean_product", "x_mixed", "x_meaned", "o_product", "x_biased", "x_updated"))
        MADE = 2

        def past_loads(g):
            return (g.lap * 2 + (g.slot // 2 + 1)) * 16

        block = stack.enter_context(nc.Block())

        @block.sync
        def _(sp):
            rows_of = ctx_last.rearrange("(n b) d -> b n d", b=BG)

            def load(n, parity, wait):
                if wait:
                    sp.wait_ge(sim_done, n - 1)
                sp.dma_start(keys_t[parity][:, :], ctx_t[:, bass.ds(n * KCOLS, KCOLS)]).then_inc(
                    keys_t_loaded[parity], 16)
                if wait:
                    sp.wait_ge(mix_product, n - 1)
                sp.dma_start(keys[parity][:, :, :, :].rearrange("p b c d -> p (b c d)"),
                             ctx_rows[:, bass.ds(n * BG * CHUNKS * D, BG * CHUNKS * D)]).then_inc(
                    keys_loaded[parity], 16)

            load(0, 0, False)
            for b in range(BG):
                sp.dma_start(last_key[b * S:(b + 1) * S, :, :],
                             rows_of[b:b + 1, :, :].broadcast_to([S, GROUPS, D])).then_inc(last_loaded, 16)
            load(1, 1, False)
            with sp.Fori(0, (GROUPS - 2) // 2) as j:
                for parity in range(2):
                    load(j * 2 + (2 + parity), parity, True)

        @block.gpsimd
        def _(pool):
            clear_finished(nc, shared, mem)
            pool.wait_ge(made, MADE)
            pool.wait_ge(last_loaded, 16 * BG)
            for step in steps(pool, GROUPS, PEEL, DEEPEST, BODY):
                g, m = step.group(LAG_LN), step.group(LAG_OUT)
                if g:
                    norm.rstd_on_gpsimd(pool, g, (made, MADE))
                if m:
                    if past(m.n - 1):
                        pool.wait_ge(x_updated, m.n - 1)
                    pool.wait_ge(made, MADE)
                    nc.gpsimd.tensor_tensor(x_bias[:, m.parity, :], x[:, bass.ds(m.n * D, D)], row("bi_bqv"),
                                            ALU.add).then_inc(x_biased, 1)

        @block.tensor
        def _(pe):
            pe.wait_ge(made, MADE)
            for step in steps(pe, GROUPS, PEEL, DEEPEST, BODY):
                f, n, w, v, m = (step.group(k) for k in (LAG_TURN, LAG_SIM, LAG_MIX, LAG_FEATURE, LAG_OUT))
                if m:
                    pe.wait_ge(x_mixed, m.n + 1)
                    pe.wait_ge(x_meaned, m.n + 1)
                    if past(m.n):
                        pe.wait_ge(x_updated, m.n)
                    features = (x_t[:, m.slot, :], mix_t[:, m.parity, :], x_mix_t[:, m.parity, :],
                                x_mean_t[:, m.parity, :])
                    for i, feature in enumerate(features):
                        mm = nc.tensor.matmul(o_bank[:, 0:D], feature, weight("bi_qv", i), start=(i == 0),
                                              stop=(i == 3))
                    mm.then_inc(o_product, 1)
                if f:
                    pe.wait_ge(norm.done, f.n + 1)
                    if past(f.n):
                        pe.wait_ge(sim_rows_done, f.n)
                    nc.tensor.transpose(xt_bank[:, 0:P], norm.rows[:, f.slot, :], const["identity"]).then_inc(turned, 1)
                if n:
                    pe.wait_ge(sim_rows_done, n.n + 1)
                    pe.wait_ge(keys_t_loaded[n.parity], past_loads(n))
                    if past(n.n):
                        pe.wait_ge(exped, n.n)
                    for b in range(BG):
                        mm = nc.tensor.matmul(sim_bank[b * S:(b + 1) * S, 0:KEYS],
                                              sim_rows[:, n.parity, b * S:(b + 1) * S],
                                              keys_t[n.parity][:, b * KEYS:(b + 1) * KEYS], start=True, stop=True)
                    mm.then_inc(sim_done, 1)
                if w:
                    pe.wait_ge(normed, w.n + 1)
                    if past(w.n):
                        pe.wait_ge(p_copied, w.n)
                    for c in range(CHUNKS):
                        mm = nc.tensor.transpose(pt_bank[:, c * P:(c + 1) * P],
                                                 probs[:, w.parity, c * P:(c + 1) * P], const["identity"])
                    mm.then_inc(p_turned, 1)
                    pe.wait_ge(row_max_done, w.n + 1)
                    if past(w.n):
                        pe.wait_ge(top_done, w.n)
                    nc.tensor.matmul(max_bank[:, 0:P], row_max[:, w.slot:w.slot + 1].broadcast_to([P, P]),
                                     const["identity"], start=True, stop=True).then_inc(max_spread, 1)
                if v:
                    pe.wait_ge(mix_done, v.n + 1)
                    if past(v.n):
                        pe.wait_ge(mix_copied, v.n)
                    nc.tensor.transpose(mixt_bank[:, 0:P], mix_rows[:, v.parity, :], const["identity"]).then_inc(mix_turned, 1)
                    pe.wait_ge(weights_done, v.n + 1)
                    if past(v.n):
                        pe.wait_ge(x_meaned, v.n)
                    nc.tensor.matmul(mean_bank[:, 0:P], norm.rows[:, v.slot, :], token_weights[:, v.parity, :],
                                     start=True, stop=True).then_inc(mean_product, 1)
                if w:
                    pe.wait_ge(p_copied, w.n + 1)
                    pe.wait_ge(keys_loaded[w.parity], past_loads(w))
                    if past(w.n):
                        pe.wait_ge(mix_done, w.n)
                    for c in range(CHUNKS):
                        for b in range(BG):
                            mm = nc.tensor.matmul(mix_bank[b * S:(b + 1) * S, 0:D],
                                                  probs_t[:, w.parity, c, b * S:(b + 1) * S],
                                                  keys[w.parity][:, b, c, :], start=(c == 0),
                                                  stop=(c == CHUNKS - 1), skip_group_check=True)
                    mm.then_inc(mix_product, 1)

        @block.scalar
        def _(act):
            act.wait_ge(made, MADE)
            for step in steps(act, GROUPS, PEEL, DEEPEST, BODY):
                f, n, w, v = (step.group(k) for k in (LAG_TURN, LAG_SIM, LAG_MIX, LAG_FEATURE))
                if f:
                    act.wait_ge(turned, f.n + 1)
                    if past(f.n - 3):
                        act.wait_ge(o_product, f.n - 3)
                        act.wait_ge(x_meaned, f.n - 3)
                    nc.scalar.activation(x_t[:, f.slot, :], xt_bank[:, 0:P], ACT.Copy).then_inc(x_copied, 1)
                    if past(f.n - 1):
                        act.wait_ge(sim_done, f.n - 1)
                    nc.scalar.activation(sim_rows[:, f.parity, :], xt_bank[:, 0:P], ACT.Identity,
                                         bias=negated[:, 0:1], scale=negated[:, 1:2]).then_inc(sim_rows_done, 1)
                if w:
                    act.wait_ge(p_turned, w.n + 1)
                    if past(w.n - 1):
                        act.wait_ge(mix_product, w.n - 1)
                    nc.scalar.activation(probs_t[:, w.parity, :, :].rearrange("p c k -> p (c k)"),
                                         pt_bank[:, 0:CHUNKS * P], ACT.Copy).then_inc(p_copied, 1)
                if n:
                    act.wait_ge(min_done, n.n + 1)
                    if past(n.n - 1):
                        act.wait_ge(p_turned, n.n - 1)
                        act.wait_ge(last_part_done, n.n - 1)
                    nc.scalar.activation(probs[:, n.parity, :], sim_bank[:, 0:KEYS], ACT.Exp,
                                         bias=neg_max[:, n.parity:n.parity + 1], scale=-1.0,
                                         accum_out=den[:, n.parity:n.parity + 1]).then_inc(exped, 1)
                if v:
                    act.wait_ge(mix_turned, v.n + 1)
                    if past(v.n - 1):
                        act.wait_ge(o_product, v.n - 1)
                    nc.scalar.activation(mix_t[:, v.parity, :], mixt_bank[:, 0:P], ACT.Copy).then_inc(mix_copied, 1)
                if w:
                    act.wait_ge(top_negated, w.n + 1)
                    if past(w.n - 1):
                        act.wait_ge(weight_scaled, w.n - 1)
                    nc.scalar.activation(token_exp[:, w.parity, :], maxima[:, w.parity, :], ACT.Exp,
                                         bias=neg_top[:, w.parity, 1:2],
                                         accum_out=token_sum[:, w.parity, 0:1]).then_inc(token_exped, 1)
                    nc.scalar.activation(own_exp[:, w.parity, 0:1], row_max[:, w.slot:w.slot + 1], ACT.Exp,
                                         bias=neg_top[:, w.parity, 1:2]).then_inc(own_exped, 1)

        @block.vector
        def _(dve):
            dve.wait_ge(shared["loaded"], shared["loaded_count"])
            dve.wait_ge(shared["params"], shared["params_count"])
            nc.vector.tensor_scalar(negated[:, 0:1], column("bi_w2"), -1.0, None, ALU.mult).then_inc(made, 1)
            nc.vector.tensor_scalar(negated[:, 1:2], column("bi_w3"), -1.0, None, ALU.mult).then_inc(made, 1)
            dve.wait_ge(last_loaded, 16 * BG)
            for step in steps(dve, GROUPS, PEEL, DEEPEST, BODY):
                g, f, n, w, v, m = (step.group(k) for k in (LAG_LN, LAG_TURN, LAG_SIM, LAG_MIX, LAG_FEATURE, LAG_OUT))
                if g:
                    norm.moments_on_vector(dve, g, (made, MADE))
                if f:
                    k = f.slot
                    dve.wait_ge(norm.done, f.n + 1)
                    if past(f.n - 3):
                        dve.wait_ge(row_max_done, f.n - 3)
                    nc.vector.tensor_tensor_reduce(x_w1[:, f.parity, :], norm.rows[:, k, :], row("bi_w1"), 1.0,
                                                   row("bi_b"), ALU.mult, ALU.add,
                                                   x_part[:, k:k + 1]).then_inc(x_part_done, 1)
                if w:
                    k = w.parity
                    spreads, exps = in_register(dve, w.n + 1), in_register(dve, w.n - 1)
                    dve.wait_ge(made, MADE)
                    dve.wait_ge(max_spread, spreads)
                    if past(exps):
                        dve.wait_ge(token_exped, exps)
                    nc.vector.tensor_tensor_reduce(maxima[:, k, :], max_bank[:, 0:P], const["other_sequence"],
                                                   1.0, -BIG, ALU.add, ALU.max, neg_top[:, k, 0:1]).then_inc(top_done, 1)
                if n:
                    k = n.parity
                    dve.wait_ge(sim_done, n.n + 1)
                    if past(n.n - 1):
                        dve.wait_ge(exped, n.n - 1)
                    nc.vector.tensor_reduce(neg_max[:, k:k + 1], sim_bank[:, 0:KEYS], AXIS_X, ALU.min).then_inc(min_done, 1)
                if w:
                    k = w.parity
                    dve.wait_ge(top_done, w.n + 1)
                    if past(w.n - 1):
                        dve.wait_ge(own_exped, w.n - 1)
                    nc.vector.tensor_scalar(neg_top[:, k, 1:2], neg_top[:, k, 0:1], -1.0, None,
                                            ALU.mult).then_inc(top_negated, 1)
                    dve.wait_ge(normed, w.n + 1)
                    nc.vector.tensor_scalar(last_part[:, k, :], last_key[:, bass.ds(w.n, 1), :].rearrange("p n d -> p (n d)"),
                                            probs[:, k, LAST:KEYS], None, ALU.mult).then_inc(last_part_done, 1)
                if n:
                    dve.wait_ge(min_done, n.n + 1)
                    dve.wait_ge(x_part_done, n.n + 1)
                    if past(n.n - 3):
                        dve.wait_ge(max_spread, n.n - 3)
                        dve.wait_ge(own_exped, n.n - 3)
                    nc.vector.tensor_tensor(row_max[:, n.slot:n.slot + 1], x_part[:, n.slot:n.slot + 1],
                                            neg_max[:, n.parity:n.parity + 1], ALU.subtract).then_inc(row_max_done, 1)
                    k = n.parity
                    dve.wait_ge(exped, n.n + 1)
                    nc.vector.reciprocal(inv_den[:, k:k + 1], den[:, k:k + 1]).then_inc(inverted, 1)
                    dve.wait_ge(inverted, n.n + 1)
                    nc.vector.tensor_scalar(probs[:, k, :], probs[:, k, :], inv_den[:, k:k + 1], None,
                                            ALU.mult).then_inc(normed, 1)
                if v:
                    k = v.parity
                    dve.wait_ge(mix_copied, v.n + 1)
                    if past(v.n - 1):
                        dve.wait_ge(o_product, v.n - 1)
                    nc.vector.tensor_tensor(x_mix_t[:, k, :], x_t[:, v.slot, :], mix_t[:, k, :],
                                            ALU.mult).then_inc(x_mixed, 1)
                    dve.wait_ge(mean_product, v.n + 1)
                    nc.vector.tensor_tensor(x_mean_t[:, k, :], mean_bank[:, 0:P], x_t[:, v.slot, :],
                                            ALU.mult).then_inc(x_meaned, 1)
                if w:
                    k = w.parity
                    dve.wait_ge(token_exped, w.n + 1)
                    nc.vector.reciprocal(token_sum[:, k, 1:2], token_sum[:, k, 0:1]).then_inc(sum_inverted, 1)
                    dve.wait_ge(own_exped, w.n + 1)
                    dve.wait_ge(sum_inverted, w.n + 1)
                    nc.vector.tensor_tensor(own_exp[:, k, 1:2], own_exp[:, k, 0:1], token_sum[:, k, 1:2],
                                            ALU.mult).then_inc(weight_scaled, 1)
                    dve.wait_ge(weight_scaled, w.n + 1)
                    if past(w.n - 1):
                        dve.wait_ge(mean_product, w.n - 1)
                    nc.vector.tensor_scalar(token_weights[:, k, :], const["same_sequence"], own_exp[:, k, 1:2], None,
                                            ALU.mult).then_inc(weights_done, 1)
                    dve.wait_ge(mix_product, w.n + 1)
                    dve.wait_ge(last_part_done, w.n + 1)
                    if past(w.n - 1):
                        dve.wait_ge(mix_turned, w.n - 1)
                    nc.vector.tensor_tensor(mix_rows[:, k, :], mix_bank[:, 0:D], last_part[:, k, :],
                                            ALU.add).then_inc(mix_done, 1)
                if m:
                    dve.wait_ge(o_product, m.n + 1)
                    dve.wait_ge(x_biased, m.n + 1)
                    nc.vector.tensor_tensor(x[:, bass.ds(m.n * D, D)], o_bank[:, 0:D], x_bias[:, m.parity, :],
                                            ALU.add).then_inc(x_updated, 1)
                if g:
                    norm.rows_on_vector(dve, g, mean_product)


def gelu_block(nc, shared, inner):
    with ExitStack() as stack:
        mem = Memory(nc, stack, "gelu")
        LAG_LN, LAG_TURN, LAG_UP, LAG_DOWN = 0, 1, 2, 3
        PEEL, DEEPEST = 4, 3
        PARTS = FF // P
        x, const, weight, column, row = (shared[k] for k in ("x", "const", "weight", "column", "row"))
        norm = Norm(nc, mem, {**shared, "x": inner})
        x_t = mem.sbuf("x_t", [P, 2, P])
        hidden = mem.sbuf("hidden", [P, 2, PARTS, P])
        x_inner = mem.sbuf("x_inner", [P, 2, D])
        x_summed = mem.sem("x_summed")
        x_bias = mem.sbuf("x_bias", [P, 2, D])
        xt_bank, o_bank = (mem.psum(k, [P, 512]) for k in ("xt_bank", "o_bank"))
        up_bank = [mem.psum(f"up_bank{i}", [P, PARTS, P]) for i in range(2)]
        (made, turned, x_copied, up_product, hidden_done, o_product, x_biased, x_updated) = (
            mem.sem(k) for k in ("made", "turned", "x_copied", "up_product", "hidden_done", "o_product",
                                 "x_biased", "x_updated"))
        block = stack.enter_context(nc.Block())

        @block.gpsimd
        def _(pool):
            clear_finished(nc, shared, mem)
            pool.wait_ge(made, 1)
            for step in steps(pool, GROUPS, PEEL, DEEPEST):
                g, m = step.group(LAG_LN), step.group(LAG_DOWN)
                if g:
                    norm.rstd_on_gpsimd(pool, g, (made, 1))
                if m:
                    if past(m.n - 1):
                        pool.wait_ge(x_updated, m.n - 1)
                    pool.wait_ge(made, 1)
                    nc.gpsimd.tensor_tensor(x_inner[:, m.parity, :], x[:, bass.ds(m.n * D, D)],
                                            inner[:, bass.ds(m.n * D, D)], ALU.add).then_inc(x_summed, 1)
                    pool.wait_ge(x_summed, m.n + 1)
                    pool.wait_ge(made, 1)
                    nc.gpsimd.tensor_tensor(x_bias[:, m.parity, :], x_inner[:, m.parity, :], row("wa_bfc2"),
                                            ALU.add).then_inc(x_biased, 1)

        @block.tensor
        def _(pe):
            pe.wait_ge(made, 1)
            for step in steps(pe, GROUPS, PEEL, DEEPEST):
                f, n, m = (step.group(k) for k in (LAG_TURN, LAG_UP, LAG_DOWN))
                if f:
                    pe.wait_ge(norm.done, f.n + 1)
                    if past(f.n):
                        pe.wait_ge(x_copied, f.n)
                    nc.tensor.transpose(xt_bank[:, 0:P], norm.rows[:, f.parity, :], const["identity"]).then_inc(turned, 1)
                if n:
                    pe.wait_ge(x_copied, n.n + 1)
                    if past(n.n - 1):
                        pe.wait_ge(hidden_done, n.n - 1)
                    for c in range(PARTS):
                        mm = nc.tensor.matmul(up_bank[n.parity][:, c, :], weight("wa_fc1", c), x_t[:, n.parity, :],
                                              start=True, stop=True)
                    mm.then_inc(up_product, 1)
                if m:
                    pe.wait_ge(hidden_done, m.n + 1)
                    if past(m.n):
                        pe.wait_ge(x_updated, m.n)
                    for c in range(PARTS):
                        mm = nc.tensor.matmul(o_bank[:, 0:D], hidden[:, m.parity, c, :], weight("wa_fc2", c),
                                              start=(c == 0), stop=(c == PARTS - 1))
                    mm.then_inc(o_product, 1)

        @block.scalar
        def _(act):
            act.wait_ge(made, 1)
            for step in steps(act, GROUPS, PEEL, DEEPEST):
                f, n = step.group(LAG_TURN), step.group(LAG_UP)
                if f:
                    act.wait_ge(turned, f.n + 1)
                    if past(f.n - 1):
                        act.wait_ge(up_product, f.n - 1)
                    nc.scalar.activation(x_t[:, f.parity, :], xt_bank[:, 0:P], ACT.Identity,
                                         bias=column("wa_b2"), scale=column("wa_g2")).then_inc(x_copied, 1)
                if n:
                    act.wait_ge(up_product, n.n + 1)
                    if past(n.n - 1):
                        act.wait_ge(o_product, n.n - 1)
                    for c in range(PARTS):
                        last = nc.scalar.activation(hidden[:, n.parity, c, :], up_bank[n.parity][:, c, :], ACT.Gelu,
                                                    bias=column("wa_bfc1", c, 1))
                    last.then_inc(hidden_done, 1)

        @block.vector
        def _(dve):
            dve.wait_ge(shared["loaded"], shared["loaded_count"])
            dve.wait_ge(shared["params"], shared["params_count"])
            dve.sem_inc(made, 1)
            for step in steps(dve, GROUPS, PEEL, DEEPEST):
                g, m = step.group(LAG_LN), step.group(LAG_DOWN)
                if g:
                    norm.moments_on_vector(dve, g, (made, 1))
                if m:
                    dve.wait_ge(o_product, m.n + 1)
                    dve.wait_ge(x_biased, m.n + 1)
                    nc.vector.tensor_tensor(x[:, bass.ds(m.n * D, D)], o_bank[:, 0:D], x_bias[:, m.parity, :],
                                            ALU.add).then_inc(x_updated, 1)
                if g:
                    norm.rows_on_vector(dve, g, turned)


def mixture(nc, shared):
    with ExitStack() as stack:
        mem = Memory(nc, stack, "moe")
        x, const, weight = (shared[k] for k in ("x", "const", "weight"))
        OUTS = EXPERTS + 1
        x_t = mem.sbuf("x_t", [P, GROUPS * P])
        share = mem.sbuf("share", [P, GROUPS, OUTS])

        with ExitStack() as router:
            route_tokens(nc, shared, Memory(nc, router, "route"), x_t, share)

        TILES = 4
        CHUNK = TILES * P
        N_CHUNKS = GROUPS // TILES
        HIDDEN = EXPERTS + 2
        RING = 3
        hidden = mem.sbuf("hidden", [P, RING, CHUNK])
        gate = mem.sbuf("gate", [P, 2, CHUNK])
        up = mem.sbuf("up", [P, CHUNK])
        hidden_bank = [mem.psum(f"hidden_bank{i}", [P, CHUNK]) for i in range(2)]
        out_bank = [mem.psum(f"out_bank{i}", [P, TILES, D]) for i in range(RING)]
        (hidden_product, silu_done, up_copied, gate_done, shared_done, out_product, added) = (
            mem.sem(k) for k in ("hidden_product", "silu_done", "up_copied", "gate_done", "shared_done",
                                 "out_product", "added"))
        block = stack.enter_context(nc.Block())

        def chunks_of(engine):
            yield 0
            with engine.Fori(1, N_CHUNKS) as c:
                yield c

        def expert_of(k):
            return EXPERTS if k == 0 else k - 1

        @block.tensor
        def _(pe):
            for c in chunks_of(pe):
                for i in range(HIDDEN + 1):
                    if i < HIDDEN:
                        w = weight("moe_gate_up", 1 - i) if i < 2 else weight("moe_w1", i - 2)
                        if past(c * HIDDEN + (i - 1)):
                            pe.wait_ge(silu_done, c * HIDDEN + (i - 1))
                        nc.tensor.matmul(hidden_bank[i % 2][:, :], w, x_t[:, bass.ds(c * CHUNK, CHUNK)],
                                         start=True, stop=True).then_inc(hidden_product, 1)
                    if i >= 2:
                        k = i - 2
                        if k == 0:
                            pe.wait_ge(shared_done, c + 1)
                        else:
                            pe.wait_ge(silu_done, c * HIDDEN + (k + 2))
                        if past(c * OUTS + (k - 2)):
                            pe.wait_ge(added, c * OUTS + (k - 2))
                        w = weight("moe_down") if k == 0 else weight("moe_w2", k - 1)
                        for j in range(TILES):
                            mm = nc.tensor.matmul(out_bank[k % RING][:, j, :], hidden[:, k % RING, j * P:(j + 1) * P],
                                                  w, start=True, stop=True)
                        mm.then_inc(out_product, 1)

        @block.scalar
        def _(act):
            for c in chunks_of(act):
                for i in range(HIDDEN):
                    act.wait_ge(hidden_product, c * HIDDEN + (i + 1))
                    if i == 0:
                        if past(c):
                            act.wait_ge(shared_done, c)
                        last = nc.scalar.activation(up[:, :], hidden_bank[i % 2][:, :], ACT.Copy)
                    elif i == 1:
                        last = nc.scalar.activation(gate[:, 0, :], hidden_bank[i % 2][:, :], ACT.Silu)
                    else:
                        k = i - 1
                        if past(c * OUTS + (k - 2)):
                            act.wait_ge(out_product, c * OUTS + (k - 2))
                        last = nc.scalar.activation(hidden[:, k % RING, :], hidden_bank[i % 2][:, :], ACT.Silu)
                    last.then_inc(silu_done, 1)

        @block.vector
        def _(dve):
            for c in chunks_of(dve):
                dve.wait_ge(silu_done, c * HIDDEN + 2)
                if past(c * OUTS - 2):
                    dve.wait_ge(out_product, c * OUTS - 2)
                nc.vector.tensor_tensor(hidden[:, 0, :], gate[:, 0, :], up[:, :], ALU.mult).then_inc(shared_done, 1)
                for k in range(OUTS):
                    dve.wait_ge(out_product, c * OUTS + (k + 1))
                    if past(c * OUTS + k):
                        dve.wait_ge(added, c * OUTS + k)
                    for j in range(TILES):
                        rows = x[:, bass.ds((c * TILES + j) * D, D)]
                        last = nc.vector.scalar_tensor_tensor(
                            out=rows, in0=out_bank[k % RING][:, j, :],
                            scalar=share[:, bass.ds(c * TILES + j, 1), expert_of(k):expert_of(k) + 1].rearrange("p n e -> p (n e)"),
                            in1=rows, op0=ALU.mult, op1=ALU.add)
                    last.then_inc(added, 1)


def route_tokens(nc, shared, mem, x_t, share):
    x, const, weight = (shared[k] for k in ("x", "const", "weight"))
    LAG_LN, LAG_TURN, LAG_LOGIT = 0, 1, 2
    PEEL, DEEPEST = 4, 2
    norm = Norm(nc, mem, shared)
    own_t = mem.sbuf("own_t", [P, 2, P])
    logits = mem.sbuf("logits", [P, GROUPS, EXPERTS + 1])
    probs = mem.sbuf("probs", [P, GROUPS, EXPERTS])
    rest = mem.sbuf("rest", [P, GROUPS, EXPERTS])
    ranks = mem.sbuf("ranks", [P, GROUPS, EXPERTS])
    chosen = mem.sbuf("chosen", [P, GROUPS, EXPERTS])
    one = mem.sbuf("one", [P, GROUPS])
    half_tanh = mem.sbuf("half_tanh", [P, GROUPS])
    xt_bank, logit_bank = (mem.psum(k, [P, 512]) for k in ("xt_bank", "logit_bank"))
    (made, turned, own_copied, kept, logit_product, logit_copied, chain, exped, tanh_done) = (
        mem.sem(k) for k in ("made", "turned", "own_copied", "kept", "logit_product", "logit_copied",
                             "chain", "exped", "tanh_done"))
    with nc.Block() as block:

        @block.gpsimd
        def _(pool):
            clear_finished(nc, shared, mem)
            pool.wait_ge(made, 1)
            for step in steps(pool, GROUPS, PEEL, DEEPEST):
                g, f = step.group(LAG_LN), step.group(LAG_TURN)
                if g:
                    norm.rstd_on_gpsimd(pool, g, (made, 1))
                if f:
                    pool.wait_ge(own_copied, f.n + 1)
                    pool.wait_ge(made, 1)
                    nc.gpsimd.tensor_copy(x_t[:, bass.ds(f.n * P, P)], own_t[:, f.parity, :]).then_inc(kept, 1)

        @block.tensor
        def _(pe):
            pe.wait_ge(made, 1)
            for step in steps(pe, GROUPS, PEEL, DEEPEST):
                f, n = step.group(LAG_TURN), step.group(LAG_LOGIT)
                if f:
                    pe.wait_ge(norm.done, f.n + 1)
                    if past(f.n):
                        pe.wait_ge(own_copied, f.n)
                    nc.tensor.transpose(xt_bank[:, 0:P], norm.rows[:, f.parity, :], const["identity"]).then_inc(turned, 1)
                if n:
                    pe.wait_ge(own_copied, n.n + 1)
                    if past(n.n):
                        pe.wait_ge(logit_copied, n.n)
                    nc.tensor.matmul(logit_bank[:, 0:EXPERTS + 1], own_t[:, n.parity, :], shared["router"],
                                     start=True, stop=True).then_inc(logit_product, 1)

        @block.scalar
        def _(act):
            act.wait_ge(made, 1)
            for step in steps(act, GROUPS, PEEL, DEEPEST):
                f, n = step.group(LAG_TURN), step.group(LAG_LOGIT)
                if f:
                    act.wait_ge(turned, f.n + 1)
                    if past(f.n - 1):
                        act.wait_ge(logit_product, f.n - 1)
                        act.wait_ge(kept, f.n - 1)
                    nc.scalar.activation(own_t[:, f.parity, :], xt_bank[:, 0:P], ACT.Copy).then_inc(own_copied, 1)
                if n:
                    act.wait_ge(logit_product, n.n + 1)
                    act.wait_ge(made, 1)
                    nc.scalar.activation(logits[:, bass.ds(n.n, 1), :].rearrange("p n e -> p (n e)"),
                                         logit_bank[:, 0:EXPERTS + 1], ACT.Copy).then_inc(logit_copied, 1)
            act.wait_ge(logit_copied, GROUPS)
            nc.scalar.activation(half_tanh[:, :], logits[:, :, EXPERTS], ACT.Tanh, scale=0.5).then_inc(tanh_done, 1)
            act.wait_ge(chain, 2)
            nc.scalar.activation(probs[:, :, :], rest[:, :, :], ACT.Exp).then_inc(exped, 1)

        @block.vector
        def _(dve):
            dve.wait_ge(shared["loaded"], shared["loaded_count"])
            dve.wait_ge(shared["params"], shared["params_count"])
            dve.sem_inc(made, 1)
            for step in steps(dve, GROUPS, PEEL, DEEPEST):
                g = step.group(LAG_LN)
                if g:
                    norm.moments_on_vector(dve, g, (made, 1))
                    norm.rows_on_vector(dve, g, turned)
            whole = [P, GROUPS, EXPERTS]
            count = [0]

            def then(instruction):
                count[0] += 1
                instruction.then_inc(chain, 1)
                dve.wait_ge(chain, count[0])

            def wide(column_per_group):
                return column_per_group.rearrange("p (n o) -> p n o", o=1).broadcast_to(whole)

            rank = const["expert_rank"].rearrange("p (o e) -> p o e", o=1).broadcast_to(whole)
            dve.wait_ge(logit_copied, GROUPS)
            then(nc.vector.tensor_reduce(one[:, :], logits[:, :, 0:EXPERTS], AXIS_X, ALU.max))
            then(nc.vector.tensor_tensor(rest[:, :, :], logits[:, :, 0:EXPERTS], wide(one[:, :]), ALU.subtract))
            dve.wait_ge(exped, 1)
            then(nc.vector.tensor_reduce(one[:, :], probs[:, :, :], AXIS_X, ALU.add))
            then(nc.vector.reciprocal(one[:, :], one[:, :]))
            then(nc.vector.tensor_tensor(probs[:, :, :], probs[:, :, :], wide(one[:, :]), ALU.mult))
            then(nc.vector.tensor_copy(rest[:, :, :], probs[:, :, :]))
            for turn in range(2):
                then(nc.vector.tensor_reduce(one[:, :], rest[:, :, :], AXIS_X, ALU.max))
                then(nc.vector.tensor_tensor(ranks[:, :, :], rest[:, :, :], wide(one[:, :]), ALU.is_equal))
                then(nc.vector.tensor_tensor(ranks[:, :, :], ranks[:, :, :], rank, ALU.mult))
                then(nc.vector.tensor_reduce(one[:, :], ranks[:, :, :], AXIS_X, ALU.max))
                then(nc.vector.tensor_tensor(chosen[:, :, :], ranks[:, :, :], wide(one[:, :]), ALU.is_equal))
                if turn == 0:
                    then(nc.vector.tensor_tensor(share[:, :, 0:EXPERTS], chosen[:, :, :], probs[:, :, :], ALU.mult))
                    then(nc.vector.scalar_tensor_tensor(out=rest[:, :, :], in0=chosen[:, :, :], scalar=-2.0,
                                                        in1=rest[:, :, :], op0=ALU.mult, op1=ALU.add))
                else:
                    then(nc.vector.tensor_tensor(chosen[:, :, :], chosen[:, :, :], probs[:, :, :], ALU.mult))
                    then(nc.vector.tensor_tensor(share[:, :, 0:EXPERTS], share[:, :, 0:EXPERTS], chosen[:, :, :],
                                                 ALU.add))
            dve.wait_ge(tanh_done, 1)
            then(nc.vector.tensor_scalar(share[:, :, EXPERTS], half_tanh[:, :], 0.5, 0.5, ALU.mult, ALU.add))


PHASES = range(6)


def program(nc, x_in, ctx_t, ctx_rows, ctx_last, mask, constants, matrices, columns, rows, window_bias, out):
    with ExitStack() as stack:
        mem = Memory(nc, stack, "all")
        matrix_at, matrix_width = offsets(MATRICES)
        column_at, column_width = offsets(COLUMNS)
        row_at, row_width = offsets(ROWS)
        const_at, const_width = offsets({k: CONST_WIDTH[k] for k in CONSTANTS})
        x = mem.sbuf("x", [P, GROUPS * D])
        const_sb = mem.sbuf("constants", [P, const_width])
        matrix_sb = mem.sbuf("matrices", [P, matrix_width])
        column_sb = mem.sbuf("columns", [P, column_width])
        row_sb = mem.sbuf("rows", [P, row_width])
        minus_half = mem.sbuf("minus_half", [P, 2])
        loaded, params, stored = mem.sem("loaded"), mem.sem("params"), mem.sem("stored")

        def piece(tile, where):
            def get(name, part=None, width=D):
                at, whole = where[name]
                return tile[:, at:at + whole] if part is None else tile[:, at + part * width:at + (part + 1) * width]
            return get

        shared = {"finished": [], "x": x, "weight": piece(matrix_sb, matrix_at), "column": piece(column_sb, column_at),
                  "row": piece(row_sb, row_at), "minus_half": minus_half,
                  "const": {k: const_sb[:, at:at + w] for k, (at, w) in const_at.items()},
                  "router": matrix_sb[:, matrix_at["moe_router"][0]:matrix_at["moe_gate_w"][0] + 1],
                  "loaded": loaded, "loaded_count": 16, "params": params, "params_count": 16 * 4 + 1}
        x_rows = x_in.rearrange("(n b) q d -> (b q) n d", b=BG)
        out_rows = out.rearrange("(n b) q d -> (b q) n d", b=BG)

        block = nc.Block()
        with block:
            @block.sync
            def _(sp):
                sp.dma_start(column_sb[:, :], columns).then_inc(params, 16)
                sp.dma_start(row_sb[:, :], rows.broadcast_to([P, row_width])).then_inc(params, 16)
                sp.dma_start(const_sb[:, :], constants).then_inc(params, 16)
                sp.dma_start(x[:, :].rearrange("p (n d) -> p n d", d=D), x_rows).then_inc(loaded, 16)
                sp.dma_start(matrix_sb[:, :], matrices).then_inc(params, 16)

            @block.vector
            def _(dve):
                nc.vector.memset(minus_half[:, :], -0.5).then_inc(params, 1)

        if 0 in PHASES:
            cross_attention(nc, shared, ctx_t, mask)
        if 1 in PHASES:
            self_attention(nc, shared, "sa", windowed=False)
        if 2 in PHASES:
            channel_mix(nc, shared)
        if 3 in PHASES:
            similarity_attention(nc, shared, ctx_t, ctx_rows, ctx_last)
        if 4 in PHASES:
            inner = mem.sbuf("inner", [P, GROUPS * D])
            self_attention(nc, shared, "wa", windowed=True, window_bias=window_bias, inner=inner)
            gelu_block(nc, shared, inner)
        if 5 in PHASES:
            mixture(nc, shared)

        block = nc.Block()
        with block:
            @block.sync
            def _(sp):
                sp.dma_start(out_rows, x[:, :].rearrange("p (n d) -> p n d", d=D)).then_inc(stored, 16)
                sp.wait_ge(stored, 16)


def kernel(**inputs):
    import numpy as _np
    import concourse.bacc as _bacc
    from concourse import mybir as _mybir
    from concourse.bass_utils import run_bass_kernel_spmd as _run

    a = {k: _np.asarray(v) for k, v in inputs.items()}

    def chunks(w):
        return w.reshape(-1, P, w.shape[-1]).transpose(1, 0, 2).reshape(P, -1)

    matrices = {
        "xa_q": a["L0_xattn_wq"].T, "xa_k": a["L0_xattn_wk"].T, "xa_v": a["L0_xattn_wv"].T,
        "xa_o": a["L0_xattn_wo"].T,
        "sa_q": a["L0_attn_Wq"], "sa_k": a["L0_attn_Wk"], "sa_v": a["L0_attn_Wv"], "sa_o": a["L0_attn_Wo"],
        "cm_r": a["L0_ffn_W_r"].T, "cm_k": a["L0_ffn_W_k"].T, "cm_v": a["L0_ffn_W_v"].T,
        "bi_qv": chunks(a["L1_xattn_W_qv"]),
        "wa_qkv": a["L1_attn_qkv_w"], "wa_gate": a["L1_attn_gate_w"], "wa_o": a["L1_attn_out_w"],
        "wa_fc1": a["L1_attn_fc1_w"], "wa_fc2": chunks(a["L1_attn_fc2_w"]),
        "moe_router": a["L1_ffn_router_w"], "moe_gate_w": a["L1_ffn_shared_gate_w"],
        "moe_w1": a["L1_ffn_w1"].transpose(1, 0, 2).reshape(P, -1),
        "moe_w2": a["L1_ffn_w2"].transpose(1, 0, 2).reshape(P, -1),
        "moe_gate_up": a["L1_ffn_shared_gate_up"], "moe_down": a["L1_ffn_shared_down"],
    }
    w_sim = a["L1_xattn_w_sim"].reshape(3, D)
    columns = {
        "xa_bq": a["L0_xattn_bq"], "xa_bk": a["L0_xattn_bk"], "xa_bv": a["L0_xattn_bv"],
        "sa_bq": a["L0_attn_bq"], "sa_bk": a["L0_attn_bk"], "sa_bv": a["L0_attn_bv"],
        "cm_mu_r": a["L0_ffn_mu_r"], "cm_mu_k": a["L0_ffn_mu_k"], "bi_w2": w_sim[1], "bi_w3": w_sim[2],
        "wa_g1": a["L1_attn_ln1_g"], "wa_b1": a["L1_attn_ln1_b"], "wa_bqkv": a["L1_attn_qkv_b"],
        "wa_bgate": a["L1_attn_gate_b"], "wa_g2": a["L1_attn_ln2_g"], "wa_b2": a["L1_attn_ln2_b"],
        "wa_bfc1": a["L1_attn_fc1_b"],
    }
    rows = {"xa_bo": a["L0_xattn_bo"], "sa_bo": a["L0_attn_bo"], "bi_w1": w_sim[0],
            "bi_bqv": a["L1_xattn_b_qv"], "wa_bo": a["L1_attn_out_b"], "wa_bfc2": a["L1_attn_fc2_b"],
            "bi_b": a["L1_xattn_b_sim"]}
    ctx = a["ctx_1024"]
    distance = _np.maximum(_np.arange(S)[:, None] - _np.arange(S)[None, :], 0)
    toeplitz = a["L1_attn_pos_bias"][distance].transpose(0, 2, 1).reshape(S, H * S)
    constants = shape_constants()
    arrays = {
        "x": a["x"],
        "ctx_t": ctx.transpose(2, 0, 1).reshape(D, B * KEYS),
        "ctx_rows": ctx[:, :LAST].reshape(B, CHUNKS, P, D).transpose(2, 0, 1, 3).reshape(P, B * CHUNKS * D),
        "ctx_last": ctx[:, LAST],
        "mask": a["mask_BxS2_ff1"].reshape(1, B * KEYS),
        "constants": _np.concatenate([constants[k] for k in CONSTANTS], axis=1),
        "matrices": _np.concatenate([matrices[k] for k in MATRICES], axis=1),
        "columns": _np.concatenate([columns[k].reshape(-1, P) for k in COLUMNS], axis=0).T,
        "rows": _np.concatenate([rows[k] for k in ROWS]).reshape(1, -1),
        "window_bias": toeplitz,
    }
    arrays = {f"in_{k}_dram": _np.ascontiguousarray(v) for k, v in arrays.items()}
    nc = _bacc.Bacc("TRN2", target_bir_lowering=False, num_devices=1)
    args = [nc.dram_tensor(k, v.shape, _mybir.dt.from_np(v.dtype), kind="ExternalInput").ap()
            for k, v in arrays.items()]
    out = nc.dram_tensor("out_dram", a["x"].shape, F32, kind="ExternalOutput").ap()
    program(nc, *args, out)
    r = _run(nc, [arrays], core_ids=[0])
    return r.results[0]["out_dram"]
```

```python
from contextlib import ExitStack

import concourse.bass as bass
import numpy as np
from concourse import mybir

F32 = mybir.dt.float32
ACT = mybir.ActivationFunctionType
ALU = mybir.AluOpType
AXIS_X = mybir.AxisListType.X

P = 128
B, S, D = 128, 32, 128
KEYS = 257
H, DH = 16, 8
BG = P // S
GROUPS = B // BG
CHUNKS = KEYS // P
LAST = CHUNKS * P
HG = P // S
NHG = H // HG
FF = 512
EXPERTS = 8
BIG = 3.0e38
LN_EPS = 1e-5
QK_SCALE = DH ** -0.5


def shape_constants():
    row = np.arange(P)[:, None]
    col = np.arange(P)[None, :]
    sixteen = row < BG * NHG
    tables = {
        "identity": row == col,
        "head": row // DH == np.arange(H)[None, :],
        "head_in_group": (row // DH) % HG == np.arange(HG)[None, :],
        "group_of_d": sixteen & (row % NHG == col // (HG * DH)),
        "sequence_of_row": sixteen & (row // NHG == np.arange(BG)[None, :]),
        "head_block": row // S == (col // DH) % HG,
        "head_of_row": row // S == np.arange(HG)[None, :],
        "same_sequence": row // S == col // S,
        "other_sequence": np.where(row // S == col // S, 0.0, -BIG),
        "causal_bound": np.where(np.arange(S)[None, :] <= row % S, BIG, -10000.0),
        "causal_sum": np.where(np.arange(S)[None, :] <= row % S, 0.0, -1.0e30),
        "expert_rank": EXPERTS - np.arange(EXPERTS)[None, :],
    }
    return {k: np.broadcast_to(v, (P, v.shape[1])).astype(np.float32) for k, v in tables.items()}


CONSTANTS = ["identity", "head", "head_in_group", "group_of_d", "sequence_of_row", "head_block",
             "head_of_row", "same_sequence", "other_sequence", "causal_bound", "causal_sum", "expert_rank"]
CONST_WIDTH = {"identity": P, "head": H, "head_in_group": HG, "group_of_d": P, "sequence_of_row": BG,
               "head_block": P, "head_of_row": HG, "same_sequence": P, "other_sequence": P,
               "causal_bound": S, "causal_sum": S, "expert_rank": EXPERTS}
MATRICES = {"xa_q": D, "xa_k": D, "xa_v": D, "xa_o": D,
            "sa_q": D, "sa_k": D, "sa_v": D, "sa_o": D,
            "cm_r": D, "cm_k": D, "cm_v": D,
            "bi_qv": 4 * D,
            "wa_qkv": 3 * D, "wa_gate": D, "wa_o": D, "wa_fc1": FF, "wa_fc2": (FF // P) * D,
            "moe_router": EXPERTS, "moe_gate_w": 1, "moe_w1": EXPERTS * D, "moe_w2": EXPERTS * D,
            "moe_gate_up": 2 * D, "moe_down": D}
COLUMNS = {"xa_bq": 1, "xa_bk": 1, "xa_bv": 1, "sa_bq": 1, "sa_bk": 1, "sa_bv": 1,
           "cm_mu_r": 1, "cm_mu_k": 1, "bi_w2": 1, "bi_w3": 1,
           "wa_g1": 1, "wa_b1": 1, "wa_bqkv": 3, "wa_bgate": 1, "wa_g2": 1, "wa_b2": 1,
           "wa_bfc1": FF // P}
ROWS = {"xa_bo": D, "sa_bo": D, "bi_w1": D, "bi_bqv": D, "wa_bo": D, "wa_bfc2": D, "bi_b": 1}


def offsets(widths):
    out, at = {}, 0
    for name, width in widths.items():
        out[name] = (at, width)
        at += width
    return out, at


class Group:

    def __init__(self, n, slot, lap):
        self.n, self.slot, self.parity, self.lap = n, slot, slot % 2, lap


class Step:

    def __init__(self, j, base, count, body):
        self.j, self.base, self.count, self.body = j, base, count, body

    def group(self, lag):
        at = self.base - lag
        if isinstance(self.j, int):
            if not 0 <= at < self.count:
                return None
            return Group(at, at % self.body, at // self.body)
        return Group(self.j * self.body + at, at % self.body, self.j + at // self.body)


def steps(engine, count, peel, deepest, body=2):
    assert body % 2 == 0 and peel > deepest and (count - peel) % body == 0
    for t in range(peel):
        yield Step(0, t, count, body)
    with engine.Fori(0, (count - peel) // body) as j:
        for u in range(body):
            yield Step(j, peel + u, count, body)
    for t in range(count, count + deepest):
        yield Step(0, t, count, body)


def past(value):
    return not isinstance(value, int) or value > 0


def in_register(engine, value):
    return value if isinstance(value, int) else engine.to_reg(value)


class Memory:

    def __init__(self, nc, stack, prefix):
        self.nc, self.stack, self.prefix, self.semaphores = nc, stack, prefix, []

    def sbuf(self, name, shape):
        return self.stack.enter_context(self.nc.sbuf_tensor(f"{self.prefix}_{name}", shape, F32))

    def psum(self, name, shape):
        return self.stack.enter_context(self.nc.psum_tensor(f"{self.prefix}_{name}", shape, F32))

    def sem(self, name):
        self.semaphores.append(self.nc.alloc_semaphore(f"{self.prefix}_{name}"))
        return self.semaphores[-1]


def clear_finished(nc, shared, mem):
    if shared["finished"]:
        nc.clear_and_free_semaphores(shared["finished"])
    shared["finished"] = mem.semaphores


class Norm:
    FOLDS = 8
    FIRST = 2

    def __init__(self, nc, mem):
        self.nc = nc
        self.stats = mem.sbuf("stats", [P, GROUPS, 2, 3])
        self.mean = mem.sbuf("mean", [P, GROUPS])
        self.part = mem.sbuf("part", [P, 3, GROUPS])
        self.variance = mem.sbuf("variance", [P, 2, GROUPS])
        self.rstd = mem.sbuf("rstd", [P, 2, GROUPS])
        self.stats_done, self.folded, self.rstd_done = (mem.sem(k) for k in ("stats_done", "folded", "rstd_done"))
        self.layer = 0

    def next_layer(self):
        self.layer += 1

    def stats_on_vector(self, rows, n):
        self.nc.vector.bn_stats(self.stats[:, bass.ds(n, 1), :, :].rearrange("p n h s -> p (n h s)"),
                                rows[:, bass.ds(n * D, D)]).then_inc(self.stats_done, 1)

    def fold_on_vector(self, dve):
        v, part = self.nc.vector, self.part
        count = [self.layer * self.FOLDS]

        def then(instruction):
            count[0] += 1
            instruction.then_inc(self.folded, 1)
            dve.wait_ge(self.folded, count[0])

        dve.wait_ge(self.stats_done, GROUPS * (self.layer + 1))
        means, squares = self.stats[:, :, :, 1], self.stats[:, :, :, 2]
        then(v.tensor_tensor(part[:, 0, :], means[:, :, 0], means[:, :, 1], ALU.subtract))
        then(v.tensor_tensor(part[:, 1, :], squares[:, :, 0], squares[:, :, 1], ALU.add))
        then(v.tensor_tensor(part[:, 2, :], part[:, 0, :], part[:, 0, :], ALU.mult))
        then(v.tensor_scalar(part[:, 1, :], part[:, 1, :], 1.0 / D, None, ALU.mult))
        then(v.scalar_tensor_tensor(out=part[:, 0, :], in0=part[:, 2, :], scalar=0.25, in1=part[:, 1, :],
                                    op0=ALU.mult, op1=ALU.add))
        v.tensor_scalar(self.variance[:, 1, :], part[:, 0, :], 1.0 + LN_EPS, LN_EPS * LN_EPS, ALU.mult, ALU.add)
        then(v.tensor_scalar(self.variance[:, 0, :], part[:, 0, :], LN_EPS, None, ALU.add))
        then(v.tensor_tensor(part[:, 0, :], means[:, :, 0], means[:, :, 1], ALU.add))
        then(v.tensor_scalar(self.mean[:, :], part[:, 0, :], 0.5, None, ALU.mult))

    def rstd_on_gpsimd(self, pool, minus_half, twice=False):
        pool.wait_ge(self.folded, self.layer * self.FOLDS + 6)
        kinds = 2 if twice else 1
        for groups in (slice(0, self.FIRST), slice(self.FIRST, GROUPS)):
            shape = [P, kinds, groups.stop - groups.start]
            self.nc.gpsimd.tensor_tensor(self.rstd[:, 0:kinds, groups], self.variance[:, 0:kinds, groups],
                                         minus_half[:, 0:1].rearrange("p (k g) -> p k g", k=1).broadcast_to(shape),
                                         ALU.pow).then_inc(self.rstd_done, 1)

    def rows_on_vector(self, dve, out, rows, n, twice=False):
        if isinstance(n, int) and n in (0, self.FIRST):
            dve.wait_ge(self.rstd_done, 2 * self.layer + (1 if n == 0 else 2))
        k = 1 if twice else 0
        return self.nc.vector.tensor_scalar(
            out, rows[:, bass.ds(n * D, D)], self.mean[:, bass.ds(n, 1)],
            self.rstd[:, k, bass.ds(n, 1)], ALU.subtract, ALU.mult)


def cross_attention(nc, shared, ctx_t, mask, rest_loaded):
    with ExitStack() as stack:
        mem = Memory(nc, stack, "xa")
        UNITS = BG * NHG // 2
        KCOLS = BG * KEYS
        KPART = [(0, 343), (343, 343), (686, 342)]
        LAG_LN, LAG_FRONT, LAG_STREAM, LAG_TAIL, LAG_STATS = 0, 1, 2, 3, 4
        PEEL, DEEPEST = 6, 4
        norm = shared["norm"]
        x, const, weight, column, row = (shared[k] for k in ("x", "const", "weight", "column", "row"))

        ctx = [mem.sbuf(f"ctx{i}", [P, KCOLS]) for i in range(2)]
        mask_raw = [mem.sbuf(f"mask_raw{i}", [P, KCOLS]) for i in range(2)]
        mask_add = [mem.sbuf(f"mask_add{i}", [P, KCOLS]) for i in range(2)]
        xn = mem.sbuf("xn", [P, 2, D])
        xn_t = mem.sbuf("xn_t", [P, 2, P])
        q_t = mem.sbuf("q_t", [P, 2, P])
        q_blocks = [mem.sbuf(f"q_blocks{i}", [P, BG, H, S]) for i in range(2)]
        k_t = [mem.sbuf(f"k_t{i}", [P, KCOLS]) for i in range(2)]
        v = [mem.sbuf(f"v{i}", [P, BG, CHUNKS, D]) for i in range(2)]
        last_ctx = mem.sbuf("last_ctx", [P, 2, BG, NHG])
        last_v = [mem.sbuf(f"last_v{i}", [P, D]) for i in range(2)]
        last_p = mem.sbuf("last_p", [P, BG, P])
        probs = [mem.sbuf(f"probs{i}", [P, BG * NHG, KEYS]) for i in range(2)]
        neg_max = mem.sbuf("neg_max", [P, 2, BG * NHG])
        den = mem.sbuf("den", [P, 2, BG * NHG])
        inv_den = mem.sbuf("inv_den", [P, 2, BG * NHG])
        probs_t = mem.sbuf("probs_t", [P, 4, 2, CHUNKS, P])
        z_heads = mem.sbuf("z_heads", [P, BG, HG, S])
        z_t = mem.sbuf("z_t", [P, BG, S])
        x_bias = mem.sbuf("x_bias", [P, 2, D])
        bias = mem.sbuf("bias", [P, D])

        scores = [mem.psum(f"scores{i}", [P, 2, 512]) for i in range(2)]
        turned = [mem.psum(f"turned{i}", [P, 2, CHUNKS, P]) for i in range(2)]
        z = mem.psum("z", [P, BG, P])
        front = mem.psum("front", [P, 512])

        ctx_loaded = [mem.sem(f"ctx_loaded{i}") for i in range(2)]
        mask_loaded = [mem.sem(f"mask_loaded{i}") for i in range(2)]
        stats_done, moments_done, var_done, rstd_done, xn_done = (
            mem.sem(k) for k in ("stats_done", "moments_done", "var_done", "rstd_done", "xn_done"))
        bias_product, bias_ready, zeroed = mem.sem("bias_product"), mem.sem("bias_ready"), mem.sem("zeroed")
        xn_turned, xn_copied = mem.sem("xn_turned"), mem.sem("xn_copied")
        q_product, q_copied, q_spread = mem.sem("q_product"), mem.sem("q_copied"), mem.sem("q_spread")
        k_product, k_copied = mem.sem("k_product"), mem.sem("k_copied")
        v_product, v_copied = mem.sem("v_product"), mem.sem("v_copied")
        last_ctx_copied = mem.sem("last_ctx_copied")
        last_v_product, last_v_copied = mem.sem("last_v_product"), mem.sem("last_v_copied")
        last_p_turned, last_p_spread = mem.sem("last_p_turned"), mem.sem("last_p_spread")
        mask_ready = mem.sem("mask_ready")
        scored, maxed, exped, inverted, normed = (
            mem.sem(k) for k in ("scored", "maxed", "exped", "inverted", "normed"))
        p_turned, p_copied, pv_done, z_done = (
            mem.sem(k) for k in ("p_turned", "p_copied", "pv_done", "z_done"))
        z_masked, z_summed, o_product = mem.sem("z_masked"), mem.sem("z_summed"), mem.sem("o_product")
        x_biased, x_updated = mem.sem("x_biased"), mem.sem("x_updated")

        def unit_count(g, u):
            return g.n * UNITS + (u + 1)

        def unit_before(tail, stream, u, back):
            return (stream, u - back) if u >= back else (tail, u - back + UNITS)

        block = stack.enter_context(nc.Block())

        @block.sync
        def _(sp):
            def load(n, parity, wait):
                if wait:
                    sp.wait_ge(last_v_product, n - 1)
                    sp.wait_ge(last_ctx_copied, n - 1)
                sp.dma_start(ctx[parity][:, :], ctx_t[:, bass.ds(n * KCOLS, KCOLS)]).then_inc(
                    ctx_loaded[parity], 16)
                if wait:
                    sp.wait_ge(mask_ready, n - 1)
                sp.dma_start(mask_raw[parity][:, :],
                             mask[:, bass.ds(n * KCOLS, KCOLS)].broadcast_to([P, KCOLS])).then_inc(
                    mask_loaded[parity], 16)

            for n in range(2):
                load(n, n, False)
            with sp.Fori(0, (GROUPS - 2) // 2) as j:
                for parity in range(2):
                    load(j * 2 + (2 + parity), parity, True)
            sp.wait_ge(rest_loaded, 16)

        @block.gpsimd
        def _(pool):
            clear_finished(nc, shared, mem)
            pool.wait_ge(shared["loaded"], shared["loaded_count"])
            pool.wait_ge(shared["params"], shared["params_count"])
            norm.rstd_on_gpsimd(pool, shared["minus_half"])
            for step in steps(pool, GROUPS, PEEL, DEEPEST):
                f = step.group(LAG_FRONT)
                if f:
                    loads = in_register(pool, (f.lap + 1) * 16)
                    units = in_register(pool, (f.n - 1) * UNITS)
                    pool.wait_ge(zeroed, 1)
                    pool.wait_ge(mask_loaded[f.parity], loads)
                    if past(units):
                        pool.wait_ge(maxed, units)
                    nc.gpsimd.tensor_scalar(mask_add[f.parity][:, :], mask_raw[f.parity][:, :],
                                            -10000.0, 10000.0, ALU.mult, ALU.add).then_inc(mask_ready, 1)
                    pool.wait_ge(q_copied, f.n + 1)
                    if past(f.n - 1):
                        pool.wait_ge(scored, (f.n - 1) * UNITS)
                    for b in range(BG):
                        last = nc.gpsimd.tensor_tensor(
                            q_blocks[f.parity][:, b, :, :],
                            q_t[:, f.parity, b * S:(b + 1) * S].rearrange("p (o q) -> p o q", o=1).broadcast_to([P, H, S]),
                            const["head"].rearrange("p (h o) -> p h o", o=1).broadcast_to([P, H, S]),
                            ALU.mult)
                    last.then_inc(q_spread, 1)
                m = step.group(LAG_TAIL)
                if m:
                    if past(m.n - 1):
                        pool.wait_ge(x_updated, m.n - 1)
                    pool.wait_ge(bias_ready, 1)
                    nc.gpsimd.tensor_tensor(x_bias[:, m.parity, :], x[:, bass.ds(m.n * D, D)], bias[:, :],
                                            ALU.add).then_inc(x_biased, 1)

        @block.tensor
        def _(pe):
            pe.wait_ge(shared["loaded"], shared["loaded_count"])
            pe.wait_ge(shared["params"], shared["params_count"])
            nc.tensor.matmul(front[:, 0:D], column("xa_bv").broadcast_to([P, P]), weight("xa_o"),
                             start=True, stop=True).then_inc(bias_product, 1)
            pe.wait_ge(bias_ready, 1)
            for step in steps(pe, GROUPS, PEEL, DEEPEST):
                f, n, m = step.group(LAG_FRONT), step.group(LAG_STREAM), step.group(LAG_TAIL)
                for u in range(UNITS):
                    if n:
                        b, gp = u // 2, u % 2
                        if u == 0:
                            pe.wait_ge(q_spread, n.n + 1)
                            pe.wait_ge(k_copied, (n.n + 1) * 3)
                        if past(unit_count(n, u) - 2):
                            pe.wait_ge(exped, unit_count(n, u) - 2)
                        for i in range(2):
                            g = gp * 2 + i
                            mm = nc.tensor.matmul(
                                scores[u % 2][:, i, 0:KEYS],
                                q_blocks[n.parity][:, b, g * HG:(g + 1) * HG, :].rearrange("p h q -> p (h q)"),
                                k_t[n.parity][:, b * KEYS:(b + 1) * KEYS], start=True, stop=True)
                        mm.then_inc(scored, 1)
                    w, wu = unit_before(m, n, u, 2)
                    if w:
                        pe.wait_ge(normed, unit_count(w, wu))
                        if past(unit_count(w, wu) - 2):
                            pe.wait_ge(p_copied, unit_count(w, wu) - 2)
                        for i in range(2):
                            for c in range(CHUNKS):
                                mm = nc.tensor.transpose(
                                    turned[u % 2][:, i, c, :],
                                    probs[w.parity][:, wu * 2 + i, c * P:(c + 1) * P], const["identity"])
                        mm.then_inc(p_turned, 1)
                    w, wu = unit_before(m, n, u, 4)
                    if u % 2 == 0 and w:
                        b = wu // 2
                        pe.wait_ge(p_copied, unit_count(w, wu + 1))
                        if b == 0:
                            pe.wait_ge(v_copied, (w.n + 1) * 2)
                            if past(w.n):
                                pe.wait_ge(z_masked, w.n)
                        for c in range(CHUNKS):
                            for g in range(NHG):
                                rows = slice(g * HG * DH, (g + 1) * HG * DH)
                                mm = nc.tensor.matmul(
                                    z[rows, b, :], v[w.parity][:, b, c, rows],
                                    probs_t[:, (wu + g // 2) % 4, g % 2, c, :],
                                    start=(b == 0 and c == 0), stop=False, skip_group_check=True)
                        mm.then_inc(pv_done, 1)
                        if b == BG - 1:
                            pe.wait_ge(last_v_copied, w.n + 1)
                            pe.wait_ge(last_p_spread, w.n + 1)
                            nc.tensor.matmul(z[:, :, :].rearrange("p b k -> p (b k)"), last_v[w.parity][:, :],
                                             last_p[:, :, :].rearrange("p b k -> p (b k)"),
                                             start=False, stop=True, skip_group_check=True).then_inc(z_done, 1)
                    if f and u == 0:
                        pe.wait_ge(xn_done, f.n + 1)
                        if past(f.n):
                            pe.wait_ge(last_v_copied, f.n)
                        if m and past(m.n):
                            pe.wait_ge(x_updated, m.n)
                        nc.tensor.transpose(front[:, 0:P], xn[:, f.parity, :], const["identity"]).then_inc(xn_turned, 1)
                    if m and u == 1:
                        pe.wait_ge(normed, (m.n + 1) * UNITS)
                        if f:
                            pe.wait_ge(xn_copied, f.n + 1)
                        elif past(m.n):
                            pe.wait_ge(x_updated, m.n)
                        nc.tensor.transpose(front[0:BG * NHG, 256:256 + P], probs[m.parity][:, :, LAST],
                                            const["identity"]).then_inc(last_p_turned, 1)
                    if f and u == 1:
                        pe.wait_ge(xn_copied, f.n + 1)
                        nc.tensor.matmul(front[:, P:2 * P], weight("xa_q"), xn_t[:, f.parity, :],
                                         start=True, stop=True).then_inc(q_product, 1)
                    if f and 2 <= u < 5:
                        at, width = KPART[u - 2]
                        if u == 2:
                            pe.wait_ge(ctx_loaded[f.parity], (f.lap + 1) * 16)
                            pe.wait_ge(q_copied, f.n + 1)
                            if m:
                                pe.wait_ge(last_p_spread, m.n + 1)
                        else:
                            pe.wait_ge(k_copied, f.n * 3 + (u - 2))
                        nc.tensor.matmul(front[:, 0:width], weight("xa_k"), ctx[f.parity][:, at:at + width],
                                         start=True, stop=True).then_inc(k_product, 1)
                    if f and 5 <= u < 7:
                        if u == 5:
                            pe.wait_ge(k_copied, (f.n + 1) * 3)
                        else:
                            pe.wait_ge(v_copied, f.n * 2 + 1)
                        for i in range(2):
                            for c in range(CHUNKS):
                                at = (2 * (u - 5) + i) * KEYS + c * P
                                mm = nc.tensor.matmul(front[:, (2 * i + c) * D:(2 * i + c + 1) * D],
                                                      ctx[f.parity][:, at:at + P], weight("xa_v"),
                                                      start=True, stop=True)
                        mm.then_inc(v_product, 1)
                    if f and u == 7:
                        pe.wait_ge(v_copied, (f.n + 1) * 2)
                        pe.wait_ge(last_ctx_copied, f.n + 1)
                        nc.tensor.matmul(front[0:BG * NHG, 0:D],
                                         last_ctx[:, f.parity, :, :].rearrange("p b g -> p (b g)"), weight("xa_v"),
                                         start=True, stop=True).then_inc(last_v_product, 1)
                    if m and u == 7:
                        pe.wait_ge(z_summed, m.n + 1)
                        nc.tensor.matmul(front[:, 384:384 + D], z_t[:, :, :].rearrange("p b q -> p (b q)"),
                                         weight("xa_o"), start=True, stop=True).then_inc(o_product, 1)

        @block.scalar
        def _(act):
            act.wait_ge(shared["loaded"], shared["loaded_count"])
            act.wait_ge(shared["params"], shared["params_count"])
            for step in steps(act, GROUPS, PEEL, DEEPEST):
                f, n, m = step.group(LAG_FRONT), step.group(LAG_STREAM), step.group(LAG_TAIL)
                for u in range(UNITS):
                    if f and u == 1:
                        act.wait_ge(xn_turned, f.n + 1)
                        nc.scalar.activation(xn_t[:, f.parity, :], front[:, 0:P], ACT.Copy).then_inc(xn_copied, 1)
                    if f and 3 <= u < 6:
                        at, width = KPART[u - 3]
                        act.wait_ge(k_product, f.n * 3 + (u - 2))
                        if u == 3 and past(f.n - 1):
                            act.wait_ge(scored, (f.n - 1) * UNITS)
                        nc.scalar.activation(k_t[f.parity][:, at:at + width], front[:, 0:width], ACT.Identity,
                                             bias=column("xa_bk")).then_inc(k_copied, 1)
                    if f and 6 <= u < 8:
                        act.wait_ge(v_product, f.n * 2 + (u - 5))
                        if u == 6 and past(f.n - 1):
                            act.wait_ge(pv_done, (f.n - 1) * BG)
                        nc.scalar.activation(
                            v[f.parity][:, 2 * (u - 6):2 * (u - 5), :, :].rearrange("p b c d -> p (b c d)"),
                            front[:, 0:512], ACT.Copy).then_inc(v_copied, 1)
                    if f and u == 1:
                        act.wait_ge(ctx_loaded[f.parity], (f.lap + 1) * 16)
                        if past(f.n - 1):
                            act.wait_ge(last_v_product, f.n - 1)
                        nc.scalar.activation(
                            last_ctx[:, f.parity, :, :],
                            ctx[f.parity][:, :].rearrange("p (b k) -> p b k", b=BG)[:, :, LAST:KEYS].broadcast_to([P, BG, NHG]),
                            ACT.Copy).then_inc(last_ctx_copied, 1)
                    w, wu = unit_before(m, n, u, 2)
                    if w:
                        act.wait_ge(p_turned, unit_count(w, wu))
                        if past(w.n * BG + (wu // 2 - 1)):
                            act.wait_ge(pv_done, w.n * BG + (wu // 2 - 1))
                        nc.scalar.activation(probs_t[:, wu % 4, :, :, :], turned[u % 2][:, :, :, :],
                                             ACT.Copy).then_inc(p_copied, 1)
                    if n:
                        act.wait_ge(maxed, unit_count(n, u))
                        if u == 0 and past(n.n - 1):
                            act.wait_ge(last_p_turned, n.n - 1)
                        for i in range(2):
                            k = u * 2 + i
                            last = nc.scalar.activation(
                                probs[n.parity][:, k, :], scores[u % 2][:, i, 0:KEYS], ACT.Exp,
                                bias=neg_max[:, n.parity, k:k + 1], scale=-1.0,
                                accum_out=den[:, n.parity, k:k + 1])
                        last.then_inc(exped, 1)

        @block.vector
        def _(dve):
            dve.wait_ge(shared["loaded"], shared["loaded_count"])
            dve.wait_ge(shared["params"], shared["params_count"])
            for t in (last_p[:, :, :], last_v[0][:, :], last_v[1][:, :]):
                last = nc.vector.memset(t, 0.0)
            last.then_inc(zeroed, 1)
            dve.wait_ge(zeroed, 1)
            dve.wait_ge(bias_product, 1)
            nc.vector.tensor_tensor(bias[:, :], front[:, 0:D], row("xa_bo"), ALU.add).then_inc(bias_ready, 1)
            norm.fold_on_vector(dve)
            for step in steps(dve, GROUPS, PEEL, DEEPEST):
                g, s = step.group(LAG_LN), step.group(LAG_STATS)
                f, n, m = step.group(LAG_FRONT), step.group(LAG_STREAM), step.group(LAG_TAIL)
                for u in range(UNITS):
                    if n:
                        b = u // 2
                        units = in_register(dve, unit_count(n, u))
                        masks = in_register(dve, n.n + 1)
                        dve.wait_ge(zeroed, 1)
                        dve.wait_ge(scored, units)
                        if u == 0:
                            dve.wait_ge(mask_ready, masks)
                        for i in range(2):
                            k = u * 2 + i
                            last = nc.vector.tensor_tensor_reduce(
                                scores[u % 2][:, i, 0:KEYS], scores[u % 2][:, i, 0:KEYS],
                                mask_add[n.parity][:, b * KEYS:(b + 1) * KEYS], 1.0, BIG, ALU.add, ALU.min,
                                neg_max[:, n.parity, k:k + 1])
                        last.then_inc(maxed, 1)
                    w, wu = unit_before(m, n, u, 1)
                    if w:
                        dve.wait_ge(exped, unit_count(w, wu))
                        nc.vector.reciprocal(inv_den[:, w.parity, wu * 2:wu * 2 + 2],
                                             den[:, w.parity, wu * 2:wu * 2 + 2]).then_inc(inverted, 1)
                        dve.wait_ge(inverted, unit_count(w, wu))
                        for i in range(2):
                            k = wu * 2 + i
                            last = nc.vector.tensor_scalar(probs[w.parity][:, k, :], probs[w.parity][:, k, :],
                                                           inv_den[:, w.parity, k:k + 1], None, ALU.mult)
                        last.then_inc(normed, 1)
                    if m and u == 1:
                        dve.wait_ge(last_p_turned, m.n + 1)
                        if f:
                            dve.wait_ge(q_product, f.n + 1)
                        if past(m.n):
                            dve.wait_ge(z_done, m.n)
                        nc.vector.tensor_tensor(
                            last_p[0:BG * NHG, :, :],
                            front[0:BG * NHG, 256:256 + P].rearrange("p (o k) -> p o k", o=1).broadcast_to([BG * NHG, BG, P]),
                            const["sequence_of_row"][0:BG * NHG, :].rearrange("p (b o) -> p b o", o=1).broadcast_to([BG * NHG, BG, P]),
                            ALU.mult).then_inc(last_p_spread, 1)
                    if f and u == 1:
                        dve.wait_ge(q_product, f.n + 1)
                        if past(f.n - 1):
                            dve.wait_ge(q_spread, f.n - 1)
                        nc.vector.tensor_scalar(q_t[:, f.parity, :], front[:, P:2 * P], column("xa_bq"), -QK_SCALE,
                                                ALU.add, ALU.mult).then_inc(q_copied, 1)
                    if m and u == 3:
                        dve.wait_ge(z_done, m.n + 1)
                        nc.vector.tensor_tensor(
                            z_heads[:, :, :, :], z[:, :, :].rearrange("p b (h q) -> p b h q", h=HG),
                            const["head_in_group"].rearrange("p (o h i) -> p o h i", o=1, i=1).broadcast_to([P, BG, HG, S]),
                            ALU.mult).then_inc(z_masked, 1)
                        dve.wait_ge(z_masked, m.n + 1)
                        if past(m.n):
                            dve.wait_ge(o_product, m.n)
                        nc.vector.tensor_reduce(z_t[:, :, :], z_heads[:, :, :, :].rearrange("p b h q -> p b q h"),
                                                AXIS_X, ALU.add).then_inc(z_summed, 1)
                    if f and u == 7:
                        dve.wait_ge(last_v_product, f.n + 1)
                        if m:
                            dve.wait_ge(o_product, m.n + 1)
                        if past(f.n - 1):
                            dve.wait_ge(z_done, f.n - 1)
                        nc.vector.tensor_tensor(last_v[f.parity][0:BG * NHG, :], front[0:BG * NHG, 0:D],
                                                const["group_of_d"][0:BG * NHG, :], ALU.mult).then_inc(last_v_copied, 1)
                    if m and u == 7:
                        dve.wait_ge(o_product, m.n + 1)
                        dve.wait_ge(x_biased, m.n + 1)
                        nc.vector.tensor_tensor(x[:, bass.ds(m.n * D, D)], front[:, 384:384 + D],
                                                x_bias[:, m.parity, :], ALU.add).then_inc(x_updated, 1)
                    if s and u == 2:
                        dve.wait_ge(x_updated, s.n + 1)
                        norm.stats_on_vector(x, s.n)
                    if g and u == 7:
                        if past(g.n - 1):
                            dve.wait_ge(xn_turned, g.n - 1)
                        norm.rows_on_vector(dve, xn[:, g.parity, :], x, g.n).then_inc(xn_done, 1)


def self_attention(nc, shared, name, windowed, window_bias=None, inner=None):
    with ExitStack() as stack:
        mem = Memory(nc, stack, name)
        LAG_LN, LAG_QK, LAG_BLOCK, LAG_SCORE, LAG_VALUE, LAG_OUT, LAG_STATS = 0, 1, 2, 3, 4, 5, 6
        PEEL, DEEPEST = 8, 6
        norm = shared["norm"]
        VW = HG * DH + HG
        KEY_BLOCKS_ON_POOL = 3
        x, const, weight, column, row = (shared[k] for k in ("x", "const", "weight", "column", "row"))
        if windowed:
            w_q, w_k, w_v = (weight("wa_qkv", i) for i in range(3))
            b_q, b_k, b_v = (column("wa_bqkv", i, 1) for i in range(3))
            w_o, bias = weight("wa_o"), row("wa_bo")
        else:
            w_q, w_k, w_v = (weight(k) for k in ("sa_q", "sa_k", "sa_v"))
            b_q, b_k, b_v = (column(k) for k in ("sa_bq", "sa_bk", "sa_bv"))
            w_o, bias = weight("sa_o"), row("sa_bo")

        xn = mem.sbuf("xn", [P, 2, D])
        xn_t = [mem.sbuf(f"xn_t{i}", [P, BG, HG, S]) for i in range(2)]
        q_t = mem.sbuf("q_t", [P, 2, BG, S])
        k_t = mem.sbuf("k_t", [P, 2, BG, S])
        k_blocks = [mem.sbuf(f"k_blocks{i}", [P, BG, H, S]) for i in range(2)]
        v_blocks = [mem.sbuf(f"v_blocks{i}", [P, BG, NHG, VW]) for i in range(2)]
        shifted = mem.sbuf("shifted", [P, 2, H, S])
        maxima = mem.sbuf("maxima", [P, 2, H])
        probs = mem.sbuf("probs", [P, 2, H, S])
        probs_t = mem.sbuf("probs_t", [P, 2, NHG, P])
        inv_den = mem.sbuf("inv_den", [P, 2, NHG, HG])
        z_rows = mem.sbuf("z_rows", [P, 2, D])
        z_t = mem.sbuf("z_t", [P, 2, P])
        x_bias = mem.sbuf("x_bias", [P, 2, D])
        scaled = mem.sbuf("scaled", [P, 3])
        if windowed:
            distance_bias = mem.sbuf("distance_bias", [P, H, S])
            gate = mem.sbuf("gate", [P, GROUPS * P])
            z_gated = mem.sbuf("z_gated", [P, 2, P])

        xt_bank = mem.psum("xt_bank", [P, 512])
        qk_bank = mem.psum("qk_bank", [P, 512])
        v_bank = mem.psum("v_bank", [P, BG, NHG, HG * DH])
        score_bank = mem.psum("score_bank", [P, H, S])
        pt_bank = mem.psum("pt_bank", [P, NHG, P])
        z_bank = mem.psum("z_bank", [P, 512])
        zt_bank = mem.psum("zt_bank", [P, 512])
        o_bank = mem.psum("o_bank", [P, 512])

        (prepared, bias_loaded, stats_done, moments_done, var_done, rstd_done, xn_done, xn_turned, xn_copied,
         qk_product, q_copied, k_copied, pool_blocks, dve_blocks, v_product, v_blocked, scored, bounded,
         maxed, shift_done, exped, p_turned, p_copied, pv_done, inverted, z_normed, z_turned, z_copied,
         gate_done, gated, o_product, x_biased, x_updated) = (mem.sem(k) for k in (
             "prepared", "bias_loaded", "stats_done", "moments_done", "var_done", "rstd_done", "xn_done",
             "xn_turned", "xn_copied", "qk_product", "q_copied", "k_copied", "pool_blocks", "dve_blocks",
             "v_product", "v_blocked", "scored", "bounded", "maxed", "shift_done", "exped", "p_turned",
             "p_copied", "pv_done", "inverted", "z_normed", "z_turned", "z_copied", "gate_done", "gated",
             "o_product", "x_biased", "x_updated"))
        PREPARED = 6 if windowed else 3
        y_done = mem.sem("y_done") if windowed else None
        residual = inner if windowed else x

        def key_block(engine, parity, b):
            return engine.tensor_tensor(
                k_blocks[parity][:, b, :, :],
                k_t[:, parity, b, :].rearrange("p (o k) -> p o k", o=1).broadcast_to([P, H, S]),
                const["head"].rearrange("p (h o) -> p h o", o=1).broadcast_to([P, H, S]), ALU.mult)

        block = stack.enter_context(nc.Block())

        if windowed:
            @block.sync
            def _(sp):
                for b in range(BG):
                    sp.dma_start(distance_bias[b * S:(b + 1) * S, :, :].rearrange("p h k -> p (h k)"),
                                 window_bias).then_inc(bias_loaded, 16)

        @block.gpsimd
        def _(pool):
            clear_finished(nc, shared, mem)
            norm.rstd_on_gpsimd(pool, shared["minus_half"], twice=windowed)
            for step in steps(pool, GROUPS, PEEL, DEEPEST):
                f, m = step.group(LAG_BLOCK), step.group(LAG_OUT)
                if m:
                    if windowed:
                        pool.wait_ge(y_done, m.n + 1)
                    if past(m.n - 1):
                        pool.wait_ge(x_updated, m.n - 1)
                    pool.wait_ge(prepared, PREPARED)
                    nc.gpsimd.tensor_tensor(x_bias[:, m.parity, :], residual[:, bass.ds(m.n * D, D)], bias,
                                            ALU.add).then_inc(x_biased, 1)
                if f:
                    pool.wait_ge(k_copied, f.n + 1)
                    if past(f.n - 1):
                        pool.wait_ge(scored, f.n - 1)
                    for b in range(KEY_BLOCKS_ON_POOL):
                        last = key_block(nc.gpsimd, f.parity, b)
                    last.then_inc(pool_blocks, 1)

        @block.tensor
        def _(pe):
            pe.wait_ge(prepared, PREPARED)
            for step in steps(pe, GROUPS, PEEL, DEEPEST):
                f, v, n, w, m = (step.group(k) for k in (LAG_QK, LAG_BLOCK, LAG_SCORE, LAG_VALUE, LAG_OUT))
                if f:
                    pe.wait_ge(xn_done, f.n + 1)
                    if past(f.n):
                        pe.wait_ge(xn_copied, f.n)
                    nc.tensor.transpose(xt_bank[:, 0:P], xn[:, f.parity, :], const["identity"]).then_inc(xn_turned, 1)
                if n:
                    pe.wait_ge(q_copied, n.n + 1)
                    pe.wait_ge(pool_blocks, n.n + 1)
                    pe.wait_ge(dve_blocks, n.n + 1)
                    if past(n.n):
                        pe.wait_ge(bounded, n.n)
                    for b in range(BG):
                        mm = nc.tensor.matmul(score_bank[b * S:(b + 1) * S, :, :].rearrange("p h k -> p (h k)"),
                                              q_t[:, n.parity, b, :],
                                              k_blocks[n.parity][:, b, :, :].rearrange("p h k -> p (h k)"),
                                              start=True, stop=True)
                    mm.then_inc(scored, 1)
                if m:
                    pe.wait_ge(z_normed, m.n + 1)
                    if past(m.n):
                        pe.wait_ge(z_copied, m.n)
                    nc.tensor.transpose(zt_bank[:, 0:P], z_rows[:, m.parity, :], const["identity"]).then_inc(z_turned, 1)
                if w:
                    pe.wait_ge(exped, w.n + 1)
                    if past(w.n):
                        pe.wait_ge(p_copied, w.n)
                    for g in range(NHG):
                        mm = nc.tensor.transpose(
                            pt_bank[:, g, :],
                            probs[:, w.parity, g * HG:(g + 1) * HG, :].rearrange("p h k -> p (h k)"),
                            const["identity"])
                    mm.then_inc(p_turned, 1)
                if v:
                    if past(v.n):
                        pe.wait_ge(v_blocked, v.n)
                    for b in range(BG):
                        mm = nc.tensor.matmul(v_bank[:, b, :, :].rearrange("p g d -> p (g d)"),
                                              xn_t[v.parity][:, b, :, :].rearrange("p r k -> p (r k)"), w_v,
                                              start=True, stop=True)
                    mm.then_inc(v_product, 1)
                if f:
                    pe.wait_ge(xn_copied, f.n + 1)
                    if past(f.n):
                        pe.wait_ge(gate_done if windowed else k_copied, f.n)
                    tokens = xn_t[f.parity][:, :, 0, :]
                    products = [w_q, w_k] + ([weight("wa_gate")] if windowed else [])
                    for i, w_i in enumerate(products):
                        mm = nc.tensor.matmul(qk_bank[:, i * P:(i + 1) * P].rearrange("p (b k) -> p b k", b=BG),
                                              w_i, tokens, start=True, stop=True)
                    mm.then_inc(qk_product, 1)
                if w:
                    pe.wait_ge(p_copied, w.n + 1)
                    pe.wait_ge(v_blocked, w.n + 1)
                    if past(w.n):
                        pe.wait_ge(z_normed, w.n)
                    for g in range(NHG):
                        for b in range(BG):
                            mm = nc.tensor.matmul(z_bank[b * S:(b + 1) * S, g * VW:(g + 1) * VW],
                                                  probs_t[:, w.parity, g, b * S:(b + 1) * S],
                                                  v_blocks[w.parity][:, b, g, :], start=True, stop=True)
                    mm.then_inc(pv_done, 1)
                if m:
                    pe.wait_ge(gated if windowed else z_copied, m.n + 1)
                    if past(m.n):
                        pe.wait_ge(x_updated, m.n)
                    nc.tensor.matmul(o_bank[:, 0:D], (z_gated if windowed else z_t)[:, m.parity, :], w_o,
                                     start=True, stop=True).then_inc(o_product, 1)

        @block.scalar
        def _(act):
            act.wait_ge(prepared, PREPARED)
            for step in steps(act, GROUPS, PEEL, DEEPEST):
                f, n, w, m = (step.group(k) for k in (LAG_QK, LAG_SCORE, LAG_VALUE, LAG_OUT))
                if n:
                    act.wait_ge(v_product, n.n + 1)
                    if past(n.n - 1):
                        act.wait_ge(pv_done, n.n - 1)
                    for h in range(HG):
                        last = nc.scalar.activation(v_blocks[n.parity][:, :, :, h * DH:(h + 1) * DH],
                                                    v_bank[:, :, :, h * DH:(h + 1) * DH], ACT.Copy,
                                                    scale=const["head_of_row"][:, h:h + 1])
                    last.then_inc(v_blocked, 1)
                if f:
                    act.wait_ge(xn_turned, f.n + 1)
                    if past(f.n - 1):
                        act.wait_ge(v_product, f.n - 1)
                    turned = xt_bank[:, 0:P].rearrange("p (b o k) -> p b o k", b=BG, o=1).broadcast_to([P, BG, HG, S])
                    if windowed:
                        last = nc.scalar.activation(xn_t[f.parity][:, :, :, :], turned, ACT.Identity,
                                                    bias=column("wa_b1"), scale=column("wa_g1"))
                    else:
                        last = nc.scalar.activation(xn_t[f.parity][:, :, :, :], turned, ACT.Copy)
                    last.then_inc(xn_copied, 1)
                if m:
                    act.wait_ge(z_turned, m.n + 1)
                    if past(m.n - 1):
                        act.wait_ge(gated if windowed else o_product, m.n - 1)
                    if windowed:
                        last = nc.scalar.activation(z_t[:, m.parity, :], zt_bank[:, 0:P], ACT.Identity,
                                                    bias=scaled[:, 2:3], scale=0.5)
                    else:
                        last = nc.scalar.activation(z_t[:, m.parity, :], zt_bank[:, 0:P], ACT.Identity, bias=b_v)
                    last.then_inc(z_copied, 1)
                if w:
                    act.wait_ge(p_turned, w.n + 1)
                    if past(w.n - 1):
                        act.wait_ge(pv_done, w.n - 1)
                    nc.scalar.activation(probs_t[:, w.parity, :, :], pt_bank[:, :, :], ACT.Copy).then_inc(p_copied, 1)
                if f:
                    act.wait_ge(qk_product, f.n + 1)
                    if past(f.n - 1):
                        act.wait_ge(dve_blocks, f.n - 1)
                        act.wait_ge(pool_blocks, f.n - 1)
                    nc.scalar.activation(k_t[:, f.parity, :, :], qk_bank[:, P:2 * P], ACT.Identity,
                                         bias=b_k).then_inc(k_copied, 1)
                    if past(f.n - 1):
                        act.wait_ge(scored, f.n - 1)
                    nc.scalar.activation(q_t[:, f.parity, :, :], qk_bank[:, 0:P], ACT.Identity,
                                         bias=scaled[:, 0:1], scale=QK_SCALE).then_inc(q_copied, 1)
                    if windowed:
                        act.wait_ge(prepared, PREPARED)
                        nc.scalar.activation(gate[:, bass.ds(f.n * P, P)], qk_bank[:, 2 * P:3 * P], ACT.Tanh,
                                             bias=scaled[:, 1:2], scale=0.5).then_inc(gate_done, 1)
                if n:
                    act.wait_ge(shift_done, n.n + 1)
                    if past(n.n - 1):
                        act.wait_ge(p_turned, n.n - 1)
                    nc.scalar.activation(probs[:, n.parity, :, :], shifted[:, n.parity, :, :],
                                         ACT.Exp).then_inc(exped, 1)

        @block.vector
        def _(dve):
            dve.wait_ge(shared["loaded"], shared["loaded_count"])
            dve.wait_ge(shared["params"], shared["params_count"])
            for i in range(2):
                nc.vector.tensor_copy(
                    v_blocks[i][:, :, :, HG * DH:VW],
                    const["head_of_row"].rearrange("p (a c h) -> p a c h", a=1, c=1).broadcast_to([P, BG, NHG, HG])
                ).then_inc(prepared, 1)
            nc.vector.tensor_scalar(scaled[:, 0:1], b_q, QK_SCALE, None, ALU.mult).then_inc(prepared, 1)
            if windowed:
                nc.vector.tensor_scalar(scaled[:, 1:2], column("wa_bgate"), 0.5, None, ALU.mult).then_inc(prepared, 1)
                nc.vector.tensor_scalar(scaled[:, 2:3], b_v, 0.5, None, ALU.mult).then_inc(prepared, 1)
                dve.wait_ge(bias_loaded, 16 * BG)
                nc.vector.tensor_tensor(
                    distance_bias[:, :, :], distance_bias[:, :, :],
                    const["causal_sum"].rearrange("p (o k) -> p o k", o=1).broadcast_to([P, H, S]),
                    ALU.add).then_inc(prepared, 1)
                dve.wait_ge(prepared, PREPARED)
            norm.fold_on_vector(dve)
            for step in steps(dve, GROUPS, PEEL, DEEPEST):
                g, v, n, w, m, s = (step.group(k) for k in (
                    LAG_LN, LAG_BLOCK, LAG_SCORE, LAG_VALUE, LAG_OUT, LAG_STATS))
                if v:
                    dve.wait_ge(k_copied, v.n + 1)
                    if past(v.n - 1):
                        dve.wait_ge(scored, v.n - 1)
                    for b in range(KEY_BLOCKS_ON_POOL, BG):
                        last = key_block(nc.vector, v.parity, b)
                    last.then_inc(dve_blocks, 1)
                if n:
                    dve.wait_ge(scored, n.n + 1)
                    if past(n.n - 1):
                        dve.wait_ge(exped, n.n - 1)
                    if windowed:
                        last = nc.vector.tensor_tensor(shifted[:, n.parity, :, :], score_bank[:, :, :],
                                                       distance_bias[:, :, :], ALU.add)
                    else:
                        last = nc.vector.tensor_tensor(
                            shifted[:, n.parity, :, :], score_bank[:, :, :],
                            const["causal_bound"].rearrange("p (o k) -> p o k", o=1).broadcast_to([P, H, S]),
                            ALU.min)
                    last.then_inc(bounded, 1)
                if g:
                    if past(g.n - 1):
                        dve.wait_ge(xn_turned, g.n - 1)
                    norm.rows_on_vector(dve, xn[:, g.parity, :], x, g.n, twice=windowed).then_inc(xn_done, 1)
                if n:
                    dve.wait_ge(bounded, n.n + 1)
                    nc.vector.tensor_reduce(maxima[:, n.parity, :], shifted[:, n.parity, :, :], AXIS_X,
                                            ALU.max).then_inc(maxed, 1)
                if windowed and m:
                    dve.wait_ge(z_copied, m.n + 1)
                    if past(m.n - 1):
                        dve.wait_ge(o_product, m.n - 1)
                    nc.vector.scalar_tensor_tensor(out=z_gated[:, m.parity, :], in0=gate[:, bass.ds(m.n * P, P)],
                                                   scalar=1.0, in1=z_t[:, m.parity, :], op0=ALU.add,
                                                   op1=ALU.mult).then_inc(gated, 1)
                if n:
                    dve.wait_ge(maxed, n.n + 1)
                    nc.vector.tensor_tensor(
                        shifted[:, n.parity, :, :], shifted[:, n.parity, :, :],
                        maxima[:, n.parity, :].rearrange("p (h o) -> p h o", o=1).broadcast_to([P, H, S]),
                        ALU.subtract).then_inc(shift_done, 1)
                if w:
                    z_of = z_bank[:, 0:NHG * VW].rearrange("p (g c) -> p g c", g=NHG)
                    dve.wait_ge(pv_done, w.n + 1)
                    nc.vector.reciprocal(inv_den[:, w.parity, :, :], z_of[:, :, HG * DH:VW]).then_inc(inverted, 1)
                if s:
                    dve.wait_ge(x_updated, s.n + 1)
                    norm.stats_on_vector(residual, s.n)
                if w:
                    dve.wait_ge(inverted, w.n + 1)
                    if past(w.n - 1):
                        dve.wait_ge(z_turned, w.n - 1)
                    nc.vector.tensor_tensor(
                        z_rows[:, w.parity, :].rearrange("p (g h d) -> p g h d", g=NHG, h=HG),
                        z_of[:, :, 0:HG * DH].rearrange("p g (h d) -> p g h d", h=HG),
                        inv_den[:, w.parity, :, :].rearrange("p g (h o) -> p g h o", o=1).broadcast_to([P, NHG, HG, DH]),
                        ALU.mult).then_inc(z_normed, 1)
                if m:
                    dve.wait_ge(o_product, m.n + 1)
                    dve.wait_ge(x_biased, m.n + 1)
                    nc.vector.tensor_tensor(residual[:, bass.ds(m.n * D, D)], o_bank[:, 0:D], x_bias[:, m.parity, :],
                                            ALU.add).then_inc(x_updated, 1)
                if g and windowed:
                    norm.rows_on_vector(dve, inner[:, bass.ds(g.n * D, D)], x, g.n).then_inc(y_done, 1)


def channel_mix(nc, shared, context):
    with ExitStack() as stack:
        mem = Memory(nc, stack, "cm")
        LAG_LN, LAG_TURN, LAG_MIX, LAG_OUT, LAG_STATS = 0, 1, 2, 3, 4
        PEEL, DEEPEST = 6, 4
        x, const, weight, column = (shared[k] for k in ("x", "const", "weight", "column"))
        norm = shared["norm"]
        xn = mem.sbuf("xn", [P, 2, D])
        xn_done = mem.sem("xn_done")
        now_t = mem.sbuf("now_t", [P, 2, BG, S])
        before_t = mem.sbuf("before_t", [P, 2, BG, S])
        weights = mem.sbuf("weights", [P, 4, D])
        half_v = mem.sbuf("half_v", [P, D])
        gate = mem.sbuf("gate", [P, 2, D])
        relu_t = mem.sbuf("relu_t", [P, 2, P])
        key_t = mem.sbuf("key_t", [P, 2, P])
        mixed = mem.sbuf("mixed", [P, 2, D])
        xt_bank, r_bank, k_bank, v_bank = (mem.psum(k, [P, 512]) for k in ("xt_bank", "r_bank", "k_bank", "v_bank"))
        (made, turned, now_copied, before_copied, r_product, k_product, gate_done, relu_done, key_done, v_product,
         mixed_done, x_updated) = (mem.sem(k) for k in (
             "made", "turned", "now_copied", "before_copied", "r_product", "k_product", "gate_done",
             "relu_done", "key_done", "v_product", "mixed_done", "x_updated"))
        MADE = 8
        block = stack.enter_context(nc.Block())

        @block.sync
        def _(sp):
            context.load_first(sp)

        @block.gpsimd
        def _(pool):
            clear_finished(nc, shared, mem)
            pool.wait_ge(made, MADE)
            norm.rstd_on_gpsimd(pool, shared["minus_half"])
            for step in steps(pool, GROUPS, PEEL, DEEPEST):
                g, f = step.group(LAG_LN), step.group(LAG_TURN)
                if f:
                    copies, products = in_register(pool, f.n + 1), in_register(pool, f.n - 1)
                    pool.wait_ge(made, MADE)
                    pool.wait_ge(now_copied, copies)
                    if past(products):
                        pool.wait_ge(k_product, products)
                    nc.gpsimd.tensor_copy(before_t[:, f.parity, :, 1:S],
                                          now_t[:, f.parity, :, 0:S - 1]).then_inc(before_copied, 1)

        @block.tensor
        def _(pe):
            pe.wait_ge(made, MADE)
            for step in steps(pe, GROUPS, PEEL, DEEPEST):
                f, n, m = (step.group(k) for k in (LAG_TURN, LAG_MIX, LAG_OUT))
                if f:
                    pe.wait_ge(xn_done, f.n + 1)
                    if past(f.n):
                        pe.wait_ge(now_copied, f.n)
                    nc.tensor.transpose(xt_bank[:, 0:P], xn[:, f.parity, :], const["identity"]).then_inc(turned, 1)
                if n:
                    now = now_t[:, n.parity, :, :].rearrange("p b s -> p (b s)")
                    before = before_t[:, n.parity, :, :].rearrange("p b s -> p (b s)")
                    pe.wait_ge(before_copied, n.n + 1)
                    if past(n.n):
                        pe.wait_ge(gate_done, n.n)
                    nc.tensor.matmul(r_bank[:, 0:D], now, weights[:, 0, :], start=True, stop=False)
                    nc.tensor.matmul(r_bank[:, 0:D], before, weights[:, 1, :], start=False, stop=True).then_inc(r_product, 1)
                    if past(n.n):
                        pe.wait_ge(relu_done, n.n)
                    nc.tensor.matmul(k_bank[:, 0:P], weights[:, 2, :], now, start=True, stop=False)
                    nc.tensor.matmul(k_bank[:, 0:P], weights[:, 3, :], before, start=False, stop=True).then_inc(k_product, 1)
                if m:
                    pe.wait_ge(key_done, m.n + 1)
                    if past(m.n):
                        pe.wait_ge(mixed_done, m.n)
                    nc.tensor.matmul(v_bank[:, 0:D], key_t[:, m.parity, :], half_v[:, :], start=True,
                                     stop=True).then_inc(v_product, 1)

        @block.scalar
        def _(act):
            act.wait_ge(made, MADE)
            for step in steps(act, GROUPS, PEEL, DEEPEST):
                f, n = step.group(LAG_TURN), step.group(LAG_MIX)
                if f:
                    act.wait_ge(turned, f.n + 1)
                    if past(f.n - 1):
                        act.wait_ge(k_product, f.n - 1)
                    nc.scalar.activation(now_t[:, f.parity, :, :], xt_bank[:, 0:P], ACT.Copy).then_inc(now_copied, 1)
                if n:
                    act.wait_ge(r_product, n.n + 1)
                    if past(n.n - 1):
                        act.wait_ge(mixed_done, n.n - 1)
                    nc.scalar.activation(gate[:, n.parity, :], r_bank[:, 0:D], ACT.Tanh, scale=0.5).then_inc(gate_done, 1)
                    act.wait_ge(k_product, n.n + 1)
                    if past(n.n - 1):
                        act.wait_ge(key_done, n.n - 1)
                    nc.scalar.activation(relu_t[:, n.parity, :], k_bank[:, 0:P], ACT.Relu).then_inc(relu_done, 1)

        @block.vector
        def _(dve):
            dve.wait_ge(shared["loaded"], shared["loaded_count"])
            dve.wait_ge(shared["params"], shared["params_count"])
            for i, (w, mu) in enumerate((("cm_r", "cm_mu_r"), ("cm_k", "cm_mu_k"))):
                nc.vector.tensor_scalar(weights[:, 2 * i, :], weight(w), column(mu), None, ALU.mult).then_inc(made, 1)
                dve.wait_ge(made, 3 * i + 1)
                nc.vector.tensor_scalar(weights[:, 2 * i + 1, :], weight(w), column(mu), None, ALU.mult).then_inc(made, 1)
                dve.wait_ge(made, 3 * i + 2)
                nc.vector.tensor_tensor(weights[:, 2 * i + 1, :], weight(w), weights[:, 2 * i + 1, :],
                                        ALU.subtract).then_inc(made, 1)
            nc.vector.tensor_scalar(half_v[:, :], weight("cm_v"), 0.5, None, ALU.mult).then_inc(made, 1)
            nc.vector.memset(before_t[:, :, :, 0:1], 0.0).then_inc(made, 1)
            norm.fold_on_vector(dve)
            for step in steps(dve, GROUPS, PEEL, DEEPEST):
                g, n, m = (step.group(k) for k in (LAG_LN, LAG_MIX, LAG_OUT))
                s = step.group(LAG_STATS)
                if g:
                    if past(g.n - 1):
                        dve.wait_ge(turned, g.n - 1)
                    norm.rows_on_vector(dve, xn[:, g.parity, :], x, g.n).then_inc(xn_done, 1)
                if s:
                    dve.wait_ge(x_updated, s.n + 1)
                    norm.stats_on_vector(x, s.n)
                if n:
                    dve.wait_ge(relu_done, n.n + 1)
                    if past(n.n - 1):
                        dve.wait_ge(v_product, n.n - 1)
                    nc.vector.tensor_tensor(key_t[:, n.parity, :], relu_t[:, n.parity, :], relu_t[:, n.parity, :],
                                            ALU.mult).then_inc(key_done, 1)
                if m:
                    dve.wait_ge(v_product, m.n + 1)
                    dve.wait_ge(gate_done, m.n + 1)
                    nc.vector.scalar_tensor_tensor(out=mixed[:, m.parity, :], in0=gate[:, m.parity, :], scalar=1.0,
                                                   in1=v_bank[:, 0:D], op0=ALU.add, op1=ALU.mult).then_inc(mixed_done, 1)
                    dve.wait_ge(mixed_done, m.n + 1)
                    nc.vector.tensor_tensor(x[:, bass.ds(m.n * D, D)], x[:, bass.ds(m.n * D, D)],
                                            mixed[:, m.parity, :], ALU.add).then_inc(x_updated, 1)


class Context:
    RING = 3

    def __init__(self, mem, ctx_t, ctx_rows, ctx_last):
        self.ctx_t, self.ctx_rows, self.ctx_last = ctx_t, ctx_rows, ctx_last
        self.keys_t = [mem.sbuf(f"keys_t{i}", [P, BG * KEYS]) for i in range(self.RING)]
        self.keys = [mem.sbuf(f"keys{i}", [P, BG, CHUNKS, D]) for i in range(self.RING)]
        self.last_key = mem.sbuf("last_key", [P, GROUPS, D])
        self.keys_t_loaded = [mem.sem(f"keys_t_loaded{i}") for i in range(self.RING)]
        self.keys_loaded = [mem.sem(f"keys_loaded{i}") for i in range(self.RING)]
        self.last_loaded = mem.sem("last_loaded")

    def load_keys_t(self, sp, n, i):
        sp.dma_start(self.keys_t[i][:, :], self.ctx_t[:, bass.ds(n * BG * KEYS, BG * KEYS)]).then_inc(
            self.keys_t_loaded[i], 16)

    def load_keys(self, sp, n, i):
        sp.dma_start(self.keys[i][:, :, :, :].rearrange("p b c d -> p (b c d)"),
                     self.ctx_rows[:, bass.ds(n * BG * CHUNKS * D, BG * CHUNKS * D)]).then_inc(
            self.keys_loaded[i], 16)

    def load_first(self, sp):
        for n in range(self.RING):
            self.load_keys_t(sp, n, n)
            self.load_keys(sp, n, n)
        rows_of = self.ctx_last.rearrange("(n b) d -> b n d", b=BG)
        for b in range(BG):
            sp.dma_start(self.last_key[b * S:(b + 1) * S, :, :],
                         rows_of[b:b + 1, :, :].broadcast_to([S, GROUPS, D])).then_inc(self.last_loaded, 16)


def similarity_attention(nc, shared, context):
    with ExitStack() as stack:
        mem = Memory(nc, stack, "bi")
        LAG_LN, LAG_TURN, LAG_SIM, LAG_NORM, LAG_MIX, LAG_FEATURE, LAG_OUT, LAG_STATS = range(8)
        PEEL, DEEPEST, BODY = 8, 7, 6
        RING = 3
        KCOLS = BG * KEYS
        x, const, weight, column, row = (shared[k] for k in ("x", "const", "weight", "column", "row"))
        norm = shared["norm"]
        xn = mem.sbuf("xn", [P, BODY, D])
        xn_done = mem.sem("xn_done")
        keys_t, keys, last_key = context.keys_t, context.keys, context.last_key
        keys_t_loaded, keys_loaded, last_loaded = context.keys_t_loaded, context.keys_loaded, context.last_loaded
        x_t = mem.sbuf("x_t", [P, BODY, P])
        sim_rows = mem.sbuf("sim_rows", [P, 2, P])
        negated = mem.sbuf("negated", [P, 2])
        x_w1 = mem.sbuf("x_w1", [P, 2, D])
        x_part = mem.sbuf("x_part", [P, BODY])
        neg_max = mem.sbuf("neg_max", [P, 2])
        row_max = mem.sbuf("row_max", [P, BODY])
        probs = mem.sbuf("probs", [P, RING, KEYS])
        den = mem.sbuf("den", [P, RING])
        inv_den = mem.sbuf("inv_den", [P, RING])
        probs_t = mem.sbuf("probs_t", [P, 2, CHUNKS, P])
        maxima = mem.sbuf("maxima", [P, 2, P])
        neg_top = mem.sbuf("neg_top", [P, 2, 2])
        token_exp = mem.sbuf("token_exp", [P, 2, P])
        token_sum = mem.sbuf("token_sum", [P, 2, 2])
        own_exp = mem.sbuf("own_exp", [P, 2, 2])
        token_weights = mem.sbuf("token_weights", [P, 2, P])
        mix_rows = mem.sbuf("mix_rows", [P, 2, D])
        last_part = mem.sbuf("last_part", [P, 2, D])
        mix_t = mem.sbuf("mix_t", [P, 2, P])
        x_mix_t = mem.sbuf("x_mix_t", [P, 2, P])
        x_mean_t = mem.sbuf("x_mean_t", [P, 2, P])
        x_bias = mem.sbuf("x_bias", [P, 2, D])
        (xt_bank, sim_bank, pt_bank, max_bank, mix_bank, mixt_bank, mean_bank, o_bank) = (
            mem.psum(k, [P, 512]) for k in ("xt_bank", "sim_bank", "pt_bank", "max_bank", "mix_bank",
                                            "mixt_bank", "mean_bank", "o_bank"))
        (made, turned, x_copied, sim_rows_done, x_part_done, sim_done, min_done, exped,
         inverted, normed, row_max_done, p_turned, p_copied, max_spread, top_done, top_negated, token_exped,
         own_exped, sum_inverted, weight_scaled, weights_done, last_part_done, mix_product, mix_done,
         mix_turned, mix_copied, mean_product, x_mixed, x_meaned, o_product, x_biased, x_updated) = (
             mem.sem(k) for k in (
                 "made", "turned", "x_copied", "sim_rows_done", "x_part_done", "sim_done",
                 "min_done", "exped", "inverted", "normed", "row_max_done", "p_turned", "p_copied",
                 "max_spread", "top_done", "top_negated", "token_exped", "own_exped", "sum_inverted",
                 "weight_scaled", "weights_done", "last_part_done", "mix_product", "mix_done", "mix_turned",
                 "mix_copied", "mean_product", "x_mixed", "x_meaned", "o_product", "x_biased", "x_updated"))
        MADE = 2

        def past_loads(g):
            return (g.lap * (BODY // RING) + (g.slot // RING + 1)) * 16

        block = stack.enter_context(nc.Block())

        @block.sync
        def _(sp):
            def load(n, i):
                sp.wait_ge(sim_done, n - (RING - 1))
                context.load_keys_t(sp, n, i)
                sp.wait_ge(mix_product, n - (RING - 1))
                context.load_keys(sp, n, i)

            first = RING + (GROUPS - RING) % RING
            for n in range(RING, first):
                load(n, n % RING)
            with sp.Fori(0, (GROUPS - first) // RING) as j:
                for i in range(RING):
                    load(j * RING + (first + i), (first + i) % RING)

        @block.gpsimd
        def _(pool):
            clear_finished(nc, shared, mem)
            pool.wait_ge(made, MADE)
            pool.wait_ge(last_loaded, 16 * BG)
            norm.rstd_on_gpsimd(pool, shared["minus_half"])
            for step in steps(pool, GROUPS, PEEL, DEEPEST, BODY):
                g, m = step.group(LAG_LN), step.group(LAG_OUT)
                if m:
                    if past(m.n - 1):
                        pool.wait_ge(x_updated, m.n - 1)
                    pool.wait_ge(made, MADE)
                    nc.gpsimd.tensor_tensor(x_bias[:, m.parity, :], x[:, bass.ds(m.n * D, D)], row("bi_bqv"),
                                            ALU.add).then_inc(x_biased, 1)

        @block.tensor
        def _(pe):
            pe.wait_ge(made, MADE)
            for step in steps(pe, GROUPS, PEEL, DEEPEST, BODY):
                f, n, e, w, v, m = (step.group(k) for k in (LAG_TURN, LAG_SIM, LAG_NORM, LAG_MIX, LAG_FEATURE, LAG_OUT))
                if m:
                    pe.wait_ge(x_mixed, m.n + 1)
                    pe.wait_ge(x_meaned, m.n + 1)
                    if past(m.n):
                        pe.wait_ge(x_updated, m.n)
                    features = (x_t[:, m.slot, :], mix_t[:, m.parity, :], x_mix_t[:, m.parity, :],
                                x_mean_t[:, m.parity, :])
                    for i, feature in enumerate(features):
                        mm = nc.tensor.matmul(o_bank[:, 0:D], feature, weight("bi_qv", i), start=(i == 0),
                                              stop=(i == 3))
                    mm.then_inc(o_product, 1)
                if f:
                    pe.wait_ge(xn_done, f.n + 1)
                    if past(f.n):
                        pe.wait_ge(sim_rows_done, f.n)
                    nc.tensor.transpose(xt_bank[:, 0:P], xn[:, f.slot, :], const["identity"]).then_inc(turned, 1)
                if n:
                    pe.wait_ge(sim_rows_done, n.n + 1)
                    pe.wait_ge(keys_t_loaded[n.slot % RING], past_loads(n))
                    if past(n.n):
                        pe.wait_ge(exped, n.n)
                    for b in range(BG):
                        mm = nc.tensor.matmul(sim_bank[b * S:(b + 1) * S, 0:KEYS],
                                              sim_rows[:, n.parity, b * S:(b + 1) * S],
                                              keys_t[n.slot % RING][:, b * KEYS:(b + 1) * KEYS], start=True, stop=True)
                    mm.then_inc(sim_done, 1)
                if e:
                    pe.wait_ge(row_max_done, e.n + 1)
                    if past(e.n):
                        pe.wait_ge(top_done, e.n)
                    nc.tensor.matmul(max_bank[:, 0:P], row_max[:, e.slot:e.slot + 1].broadcast_to([P, P]),
                                     const["identity"], start=True, stop=True).then_inc(max_spread, 1)
                if w:
                    pe.wait_ge(normed, w.n + 1)
                    if past(w.n):
                        pe.wait_ge(p_copied, w.n)
                    for c in range(CHUNKS):
                        mm = nc.tensor.transpose(pt_bank[:, c * P:(c + 1) * P],
                                                 probs[:, w.slot % RING, c * P:(c + 1) * P], const["identity"])
                    mm.then_inc(p_turned, 1)
                if v:
                    pe.wait_ge(mix_done, v.n + 1)
                    if past(v.n):
                        pe.wait_ge(mix_copied, v.n)
                    nc.tensor.transpose(mixt_bank[:, 0:P], mix_rows[:, v.parity, :], const["identity"]).then_inc(mix_turned, 1)
                    pe.wait_ge(weights_done, v.n + 1)
                    if past(v.n):
                        pe.wait_ge(x_meaned, v.n)
                    nc.tensor.matmul(mean_bank[:, 0:P], xn[:, v.slot, :], token_weights[:, v.parity, :],
                                     start=True, stop=True).then_inc(mean_product, 1)
                if w:
                    pe.wait_ge(p_copied, w.n + 1)
                    pe.wait_ge(keys_loaded[w.slot % RING], past_loads(w))
                    if past(w.n):
                        pe.wait_ge(mix_done, w.n)
                    for c in range(CHUNKS):
                        for b in range(BG):
                            mm = nc.tensor.matmul(mix_bank[b * S:(b + 1) * S, 0:D],
                                                  probs_t[:, w.parity, c, b * S:(b + 1) * S],
                                                  keys[w.slot % RING][:, b, c, :], start=(c == 0),
                                                  stop=(c == CHUNKS - 1), skip_group_check=True)
                    mm.then_inc(mix_product, 1)

        @block.scalar
        def _(act):
            act.wait_ge(made, MADE)
            for step in steps(act, GROUPS, PEEL, DEEPEST, BODY):
                f, n, e, w, v = (step.group(k) for k in (LAG_TURN, LAG_SIM, LAG_NORM, LAG_MIX, LAG_FEATURE))
                if f:
                    act.wait_ge(turned, f.n + 1)
                    if past(f.n - 5):
                        act.wait_ge(o_product, f.n - 5)
                        act.wait_ge(x_meaned, f.n - 5)
                    nc.scalar.activation(x_t[:, f.slot, :], xt_bank[:, 0:P], ACT.Copy).then_inc(x_copied, 1)
                    if past(f.n - 1):
                        act.wait_ge(sim_done, f.n - 1)
                    nc.scalar.activation(sim_rows[:, f.parity, :], xt_bank[:, 0:P], ACT.Identity,
                                         bias=negated[:, 0:1], scale=negated[:, 1:2]).then_inc(sim_rows_done, 1)
                if w:
                    act.wait_ge(p_turned, w.n + 1)
                    if past(w.n - 1):
                        act.wait_ge(mix_product, w.n - 1)
                    nc.scalar.activation(probs_t[:, w.parity, :, :].rearrange("p c k -> p (c k)"),
                                         pt_bank[:, 0:CHUNKS * P], ACT.Copy).then_inc(p_copied, 1)
                if n:
                    act.wait_ge(min_done, n.n + 1)
                    if past(n.n - 2):
                        act.wait_ge(p_turned, n.n - 2)
                        act.wait_ge(last_part_done, n.n - 2)
                    k = n.slot % RING
                    nc.scalar.activation(probs[:, k, :], sim_bank[:, 0:KEYS], ACT.Exp,
                                         bias=neg_max[:, n.parity:n.parity + 1], scale=-1.0,
                                         accum_out=den[:, k:k + 1]).then_inc(exped, 1)
                if v:
                    act.wait_ge(mix_turned, v.n + 1)
                    if past(v.n - 1):
                        act.wait_ge(o_product, v.n - 1)
                    nc.scalar.activation(mix_t[:, v.parity, :], mixt_bank[:, 0:P], ACT.Copy).then_inc(mix_copied, 1)
                if e:
                    act.wait_ge(top_negated, e.n + 1)
                    if past(e.n - 1):
                        act.wait_ge(weight_scaled, e.n - 1)
                    nc.scalar.activation(token_exp[:, e.parity, :], maxima[:, e.parity, :], ACT.Exp,
                                         bias=neg_top[:, e.parity, 1:2],
                                         accum_out=token_sum[:, e.parity, 0:1]).then_inc(token_exped, 1)
                    nc.scalar.activation(own_exp[:, e.parity, 0:1], row_max[:, e.slot:e.slot + 1], ACT.Exp,
                                         bias=neg_top[:, e.parity, 1:2]).then_inc(own_exped, 1)

        @block.vector
        def _(dve):
            dve.wait_ge(shared["loaded"], shared["loaded_count"])
            dve.wait_ge(shared["params"], shared["params_count"])
            nc.vector.tensor_scalar(negated[:, 0:1], column("bi_w2"), -1.0, None, ALU.mult).then_inc(made, 1)
            nc.vector.tensor_scalar(negated[:, 1:2], column("bi_w3"), -1.0, None, ALU.mult).then_inc(made, 1)
            dve.wait_ge(last_loaded, 16 * BG)
            norm.fold_on_vector(dve)
            for step in steps(dve, GROUPS, PEEL, DEEPEST, BODY):
                g, f, n, e, w, v, m, s = (step.group(k) for k in (
                    LAG_LN, LAG_TURN, LAG_SIM, LAG_NORM, LAG_MIX, LAG_FEATURE, LAG_OUT, LAG_STATS))
                if g:
                    if past(g.n - 5):
                        dve.wait_ge(mean_product, g.n - 5)
                    norm.rows_on_vector(dve, xn[:, g.slot, :], x, g.n).then_inc(xn_done, 1)
                if s:
                    dve.wait_ge(x_updated, s.n + 1)
                    norm.stats_on_vector(x, s.n)
                if e:
                    k = e.slot % RING
                    dve.wait_ge(exped, e.n + 1)
                    nc.vector.reciprocal(inv_den[:, k:k + 1], den[:, k:k + 1]).then_inc(inverted, 1)
                if w:
                    k = w.parity
                    dve.wait_ge(token_exped, w.n + 1)
                    nc.vector.reciprocal(token_sum[:, k, 1:2], token_sum[:, k, 0:1]).then_inc(sum_inverted, 1)
                if e:
                    k = e.slot % RING
                    dve.wait_ge(inverted, e.n + 1)
                    nc.vector.tensor_scalar(probs[:, k, :], probs[:, k, :], inv_den[:, k:k + 1], None,
                                            ALU.mult).then_inc(normed, 1)
                if w:
                    k = w.parity
                    dve.wait_ge(own_exped, w.n + 1)
                    dve.wait_ge(sum_inverted, w.n + 1)
                    nc.vector.tensor_tensor(own_exp[:, k, 1:2], own_exp[:, k, 0:1], token_sum[:, k, 1:2],
                                            ALU.mult).then_inc(weight_scaled, 1)
                if e:
                    k = e.parity
                    spreads, exps = in_register(dve, e.n + 1), in_register(dve, e.n - 1)
                    dve.wait_ge(made, MADE)
                    dve.wait_ge(max_spread, spreads)
                    if past(exps):
                        dve.wait_ge(token_exped, exps)
                    nc.vector.tensor_tensor_reduce(maxima[:, k, :], max_bank[:, 0:P], const["other_sequence"],
                                                   1.0, -BIG, ALU.add, ALU.max, neg_top[:, k, 0:1]).then_inc(top_done, 1)
                if w:
                    k = w.parity
                    dve.wait_ge(weight_scaled, w.n + 1)
                    if past(w.n - 1):
                        dve.wait_ge(mean_product, w.n - 1)
                    nc.vector.tensor_scalar(token_weights[:, k, :], const["same_sequence"], own_exp[:, k, 1:2], None,
                                            ALU.mult).then_inc(weights_done, 1)
                if e:
                    k = e.parity
                    dve.wait_ge(top_done, e.n + 1)
                    if past(e.n - 1):
                        dve.wait_ge(own_exped, e.n - 1)
                    nc.vector.tensor_scalar(neg_top[:, k, 1:2], neg_top[:, k, 0:1], -1.0, None,
                                            ALU.mult).then_inc(top_negated, 1)
                if n:
                    k = n.parity
                    dve.wait_ge(sim_done, n.n + 1)
                    if past(n.n - 1):
                        dve.wait_ge(exped, n.n - 1)
                    nc.vector.tensor_reduce(neg_max[:, k:k + 1], sim_bank[:, 0:KEYS], AXIS_X, ALU.min).then_inc(min_done, 1)
                if e:
                    dve.wait_ge(normed, e.n + 1)
                    if past(e.n - 1):
                        dve.wait_ge(mix_done, e.n - 1)
                    nc.vector.tensor_scalar(last_part[:, e.parity, :],
                                            last_key[:, bass.ds(e.n, 1), :].rearrange("p n d -> p (n d)"),
                                            probs[:, e.slot % RING, LAST:KEYS], None, ALU.mult).then_inc(last_part_done, 1)
                if f:
                    k = f.slot
                    dve.wait_ge(xn_done, f.n + 1)
                    if past(f.n - 5):
                        dve.wait_ge(row_max_done, f.n - 5)
                    nc.vector.tensor_tensor_reduce(x_w1[:, f.parity, :], xn[:, k, :], row("bi_w1"), 1.0,
                                                   row("bi_b"), ALU.mult, ALU.add,
                                                   x_part[:, k:k + 1]).then_inc(x_part_done, 1)
                if n:
                    dve.wait_ge(min_done, n.n + 1)
                    dve.wait_ge(x_part_done, n.n + 1)
                    if past(n.n - 5):
                        dve.wait_ge(max_spread, n.n - 5)
                        dve.wait_ge(own_exped, n.n - 5)
                    nc.vector.tensor_tensor(row_max[:, n.slot:n.slot + 1], x_part[:, n.slot:n.slot + 1],
                                            neg_max[:, n.parity:n.parity + 1], ALU.subtract).then_inc(row_max_done, 1)
                if m:
                    dve.wait_ge(o_product, m.n + 1)
                    dve.wait_ge(x_biased, m.n + 1)
                    nc.vector.tensor_tensor(x[:, bass.ds(m.n * D, D)], o_bank[:, 0:D], x_bias[:, m.parity, :],
                                            ALU.add).then_inc(x_updated, 1)
                if v:
                    k = v.parity
                    dve.wait_ge(mean_product, v.n + 1)
                    if past(v.n - 1):
                        dve.wait_ge(o_product, v.n - 1)
                    nc.vector.tensor_tensor(x_mean_t[:, k, :], mean_bank[:, 0:P], x_t[:, v.slot, :],
                                            ALU.mult).then_inc(x_meaned, 1)
                    dve.wait_ge(mix_copied, v.n + 1)
                    nc.vector.tensor_tensor(x_mix_t[:, k, :], x_t[:, v.slot, :], mix_t[:, k, :],
                                            ALU.mult).then_inc(x_mixed, 1)
                if w:
                    k = w.parity
                    dve.wait_ge(mix_product, w.n + 1)
                    dve.wait_ge(last_part_done, w.n + 1)
                    if past(w.n - 1):
                        dve.wait_ge(mix_turned, w.n - 1)
                    nc.vector.tensor_tensor(mix_rows[:, k, :], mix_bank[:, 0:D], last_part[:, k, :],
                                            ALU.add).then_inc(mix_done, 1)


def gelu_block(nc, shared, inner):
    with ExitStack() as stack:
        mem = Memory(nc, stack, "gelu")
        LAG_LN, LAG_TURN, LAG_UP, LAG_DOWN, LAG_STATS = 0, 1, 2, 3, 4
        PEEL, DEEPEST = 6, 4
        PARTS = FF // P
        x, const, weight, column, row = (shared[k] for k in ("x", "const", "weight", "column", "row"))
        norm = shared["norm"]
        xn = mem.sbuf("xn", [P, 2, D])
        xn_done = mem.sem("xn_done")
        x_t = mem.sbuf("x_t", [P, 2, P])
        hidden = mem.sbuf("hidden", [P, 2, PARTS, P])
        x_inner = mem.sbuf("x_inner", [P, 2, D])
        x_summed = mem.sem("x_summed")
        x_bias = mem.sbuf("x_bias", [P, 2, D])
        xt_bank, o_bank = (mem.psum(k, [P, 512]) for k in ("xt_bank", "o_bank"))
        up_bank = [mem.psum(f"up_bank{i}", [P, PARTS, P]) for i in range(2)]
        (made, turned, x_copied, up_product, hidden_done, o_product, x_biased, x_updated) = (
            mem.sem(k) for k in ("made", "turned", "x_copied", "up_product", "hidden_done", "o_product",
                                 "x_biased", "x_updated"))
        block = stack.enter_context(nc.Block())

        @block.gpsimd
        def _(pool):
            clear_finished(nc, shared, mem)
            pool.wait_ge(made, 1)
            norm.rstd_on_gpsimd(pool, shared["minus_half"])
            for step in steps(pool, GROUPS, PEEL, DEEPEST):
                g, m = step.group(LAG_LN), step.group(LAG_DOWN)
                if m:
                    if past(m.n - 1):
                        pool.wait_ge(x_updated, m.n - 1)
                    pool.wait_ge(made, 1)
                    nc.gpsimd.tensor_tensor(x_inner[:, m.parity, :], x[:, bass.ds(m.n * D, D)],
                                            inner[:, bass.ds(m.n * D, D)], ALU.add).then_inc(x_summed, 1)
                    pool.wait_ge(x_summed, m.n + 1)
                    pool.wait_ge(made, 1)
                    nc.gpsimd.tensor_tensor(x_bias[:, m.parity, :], x_inner[:, m.parity, :], row("wa_bfc2"),
                                            ALU.add).then_inc(x_biased, 1)

        @block.tensor
        def _(pe):
            pe.wait_ge(made, 1)
            for step in steps(pe, GROUPS, PEEL, DEEPEST):
                f, n, m = (step.group(k) for k in (LAG_TURN, LAG_UP, LAG_DOWN))
                if f:
                    pe.wait_ge(xn_done, f.n + 1)
                    if past(f.n):
                        pe.wait_ge(x_copied, f.n)
                    nc.tensor.transpose(xt_bank[:, 0:P], xn[:, f.parity, :], const["identity"]).then_inc(turned, 1)
                if n:
                    pe.wait_ge(x_copied, n.n + 1)
                    if past(n.n - 1):
                        pe.wait_ge(hidden_done, n.n - 1)
                    for c in range(PARTS):
                        mm = nc.tensor.matmul(up_bank[n.parity][:, c, :], weight("wa_fc1", c), x_t[:, n.parity, :],
                                              start=True, stop=True)
                    mm.then_inc(up_product, 1)
                if m:
                    pe.wait_ge(hidden_done, m.n + 1)
                    if past(m.n):
                        pe.wait_ge(x_updated, m.n)
                    for c in range(PARTS):
                        mm = nc.tensor.matmul(o_bank[:, 0:D], hidden[:, m.parity, c, :], weight("wa_fc2", c),
                                              start=(c == 0), stop=(c == PARTS - 1))
                    mm.then_inc(o_product, 1)

        @block.scalar
        def _(act):
            act.wait_ge(made, 1)
            for step in steps(act, GROUPS, PEEL, DEEPEST):
                f, n = step.group(LAG_TURN), step.group(LAG_UP)
                if f:
                    act.wait_ge(turned, f.n + 1)
                    if past(f.n - 1):
                        act.wait_ge(up_product, f.n - 1)
                    nc.scalar.activation(x_t[:, f.parity, :], xt_bank[:, 0:P], ACT.Identity,
                                         bias=column("wa_b2"), scale=column("wa_g2")).then_inc(x_copied, 1)
                if n:
                    act.wait_ge(up_product, n.n + 1)
                    if past(n.n - 1):
                        act.wait_ge(o_product, n.n - 1)
                    for c in range(PARTS):
                        last = nc.scalar.activation(hidden[:, n.parity, c, :], up_bank[n.parity][:, c, :], ACT.Gelu,
                                                    bias=column("wa_bfc1", c, 1))
                    last.then_inc(hidden_done, 1)

        @block.vector
        def _(dve):
            dve.wait_ge(shared["loaded"], shared["loaded_count"])
            dve.wait_ge(shared["params"], shared["params_count"])
            dve.sem_inc(made, 1)
            norm.fold_on_vector(dve)
            for step in steps(dve, GROUPS, PEEL, DEEPEST):
                g, m = step.group(LAG_LN), step.group(LAG_DOWN)
                s = step.group(LAG_STATS)
                if g:
                    if past(g.n - 1):
                        dve.wait_ge(turned, g.n - 1)
                    norm.rows_on_vector(dve, xn[:, g.parity, :], inner, g.n).then_inc(xn_done, 1)
                if s:
                    dve.wait_ge(x_updated, s.n + 1)
                    norm.stats_on_vector(x, s.n)
                if m:
                    dve.wait_ge(o_product, m.n + 1)
                    dve.wait_ge(x_biased, m.n + 1)
                    nc.vector.tensor_tensor(x[:, bass.ds(m.n * D, D)], o_bank[:, 0:D], x_bias[:, m.parity, :],
                                            ALU.add).then_inc(x_updated, 1)


def mixture(nc, shared, out_rows, stored):
    with ExitStack() as stack:
        mem = Memory(nc, stack, "moe")
        x, const, weight = (shared[k] for k in ("x", "const", "weight"))
        OUTS = EXPERTS + 1
        x_t = mem.sbuf("x_t", [P, GROUPS * P])
        share = mem.sbuf("share", [P, GROUPS, OUTS])

        with ExitStack() as router:
            route_tokens(nc, shared, Memory(nc, router, "route"), x_t, share)

        TILES = 4
        CHUNK = TILES * P
        N_CHUNKS = GROUPS // TILES
        HIDDEN = EXPERTS + 2
        RING = 3
        hidden = mem.sbuf("hidden", [P, RING, CHUNK])
        gate = mem.sbuf("gate", [P, 2, CHUNK])
        up = mem.sbuf("up", [P, CHUNK])
        hidden_bank = [mem.psum(f"hidden_bank{i}", [P, CHUNK]) for i in range(2)]
        out_bank = [mem.psum(f"out_bank{i}", [P, TILES, D]) for i in range(RING)]
        (hidden_product, silu_done, up_copied, gate_done, shared_done, out_product, added) = (
            mem.sem(k) for k in ("hidden_product", "silu_done", "up_copied", "gate_done", "shared_done",
                                 "out_product", "added"))
        block = stack.enter_context(nc.Block())

        def chunks_of(engine):
            yield 0
            with engine.Fori(1, N_CHUNKS) as c:
                yield c

        def expert_of(k):
            return EXPERTS if k == 0 else k - 1

        @block.sync
        def _(sp):
            for c in chunks_of(sp):
                sp.wait_ge(added, (c + 1) * OUTS)
                sp.dma_start(out_rows[:, bass.ds(c * TILES, TILES), :],
                             x[:, bass.ds(c * CHUNK, CHUNK)].rearrange("p (n d) -> p n d", d=D)).then_inc(stored, 16)
            sp.wait_ge(stored, 16 * N_CHUNKS)

        @block.tensor
        def _(pe):
            for c in chunks_of(pe):
                for i in range(HIDDEN + 1):
                    if i < HIDDEN:
                        w = weight("moe_gate_up", 1 - i) if i < 2 else weight("moe_w1", i - 2)
                        if past(c * HIDDEN + (i - 1)):
                            pe.wait_ge(silu_done, c * HIDDEN + (i - 1))
                        nc.tensor.matmul(hidden_bank[i % 2][:, :], w, x_t[:, bass.ds(c * CHUNK, CHUNK)],
                                         start=True, stop=True).then_inc(hidden_product, 1)
                    if i >= 2:
                        k = i - 2
                        if k == 0:
                            pe.wait_ge(shared_done, c + 1)
                        else:
                            pe.wait_ge(silu_done, c * HIDDEN + (k + 2))
                        if past(c * OUTS + (k - 2)):
                            pe.wait_ge(added, c * OUTS + (k - 2))
                        w = weight("moe_down") if k == 0 else weight("moe_w2", k - 1)
                        for j in range(TILES):
                            mm = nc.tensor.matmul(out_bank[k % RING][:, j, :], hidden[:, k % RING, j * P:(j + 1) * P],
                                                  w, start=True, stop=True)
                        mm.then_inc(out_product, 1)

        @block.scalar
        def _(act):
            for c in chunks_of(act):
                for i in range(HIDDEN):
                    act.wait_ge(hidden_product, c * HIDDEN + (i + 1))
                    if i == 0:
                        if past(c):
                            act.wait_ge(shared_done, c)
                        last = nc.scalar.activation(up[:, :], hidden_bank[i % 2][:, :], ACT.Copy)
                    elif i == 1:
                        last = nc.scalar.activation(gate[:, 0, :], hidden_bank[i % 2][:, :], ACT.Silu)
                    else:
                        k = i - 1
                        if past(c * OUTS + (k - 2)):
                            act.wait_ge(out_product, c * OUTS + (k - 2))
                        last = nc.scalar.activation(hidden[:, k % RING, :], hidden_bank[i % 2][:, :], ACT.Silu)
                    last.then_inc(silu_done, 1)

        @block.vector
        def _(dve):
            for c in chunks_of(dve):
                dve.wait_ge(silu_done, c * HIDDEN + 2)
                if past(c * OUTS - 2):
                    dve.wait_ge(out_product, c * OUTS - 2)
                nc.vector.tensor_tensor(hidden[:, 0, :], gate[:, 0, :], up[:, :], ALU.mult).then_inc(shared_done, 1)
                for k in range(OUTS):
                    dve.wait_ge(out_product, c * OUTS + (k + 1))
                    if past(c * OUTS + k):
                        dve.wait_ge(added, c * OUTS + k)
                    for j in range(TILES):
                        rows = x[:, bass.ds((c * TILES + j) * D, D)]
                        last = nc.vector.scalar_tensor_tensor(
                            out=rows, in0=out_bank[k % RING][:, j, :],
                            scalar=share[:, bass.ds(c * TILES + j, 1), expert_of(k):expert_of(k) + 1].rearrange("p n e -> p (n e)"),
                            in1=rows, op0=ALU.mult, op1=ALU.add)
                    last.then_inc(added, 1)


def route_tokens(nc, shared, mem, x_t, share):
    x, const, weight = (shared[k] for k in ("x", "const", "weight"))
    LAG_LN, LAG_TURN, LAG_LOGIT = 0, 1, 2
    PEEL, DEEPEST = 4, 2
    norm = shared["norm"]
    xn = mem.sbuf("xn", [P, 2, D])
    xn_done = mem.sem("xn_done")
    own_t = mem.sbuf("own_t", [P, 2, P])
    logits = mem.sbuf("logits", [P, GROUPS, EXPERTS + 1])
    probs = mem.sbuf("probs", [P, GROUPS, EXPERTS])
    rest = mem.sbuf("rest", [P, GROUPS, EXPERTS])
    ranks = mem.sbuf("ranks", [P, GROUPS, EXPERTS])
    chosen = mem.sbuf("chosen", [P, GROUPS, EXPERTS])
    one = mem.sbuf("one", [P, GROUPS])
    half_tanh = mem.sbuf("half_tanh", [P, GROUPS])
    xt_bank, logit_bank = (mem.psum(k, [P, 512]) for k in ("xt_bank", "logit_bank"))
    (made, turned, own_copied, kept, logit_product, logit_copied, chain, exped, tanh_done) = (
        mem.sem(k) for k in ("made", "turned", "own_copied", "kept", "logit_product", "logit_copied",
                             "chain", "exped", "tanh_done"))
    with nc.Block() as block:

        @block.gpsimd
        def _(pool):
            clear_finished(nc, shared, mem)
            pool.wait_ge(made, 1)
            norm.rstd_on_gpsimd(pool, shared["minus_half"])
            for step in steps(pool, GROUPS, PEEL, DEEPEST):
                g, f = step.group(LAG_LN), step.group(LAG_TURN)
                if f:
                    pool.wait_ge(own_copied, f.n + 1)
                    pool.wait_ge(made, 1)
                    nc.gpsimd.tensor_copy(x_t[:, bass.ds(f.n * P, P)], own_t[:, f.parity, :]).then_inc(kept, 1)

        @block.tensor
        def _(pe):
            pe.wait_ge(made, 1)
            for step in steps(pe, GROUPS, PEEL, DEEPEST):
                f, n = step.group(LAG_TURN), step.group(LAG_LOGIT)
                if f:
                    pe.wait_ge(xn_done, f.n + 1)
                    if past(f.n):
                        pe.wait_ge(own_copied, f.n)
                    nc.tensor.transpose(xt_bank[:, 0:P], xn[:, f.parity, :], const["identity"]).then_inc(turned, 1)
                if n:
                    pe.wait_ge(own_copied, n.n + 1)
                    if past(n.n):
                        pe.wait_ge(logit_copied, n.n)
                    nc.tensor.matmul(logit_bank[:, 0:EXPERTS + 1], own_t[:, n.parity, :], shared["router"],
                                     start=True, stop=True).then_inc(logit_product, 1)

        @block.scalar
        def _(act):
            act.wait_ge(made, 1)
            for step in steps(act, GROUPS, PEEL, DEEPEST):
                f, n = step.group(LAG_TURN), step.group(LAG_LOGIT)
                if f:
                    act.wait_ge(turned, f.n + 1)
                    if past(f.n - 1):
                        act.wait_ge(logit_product, f.n - 1)
                        act.wait_ge(kept, f.n - 1)
                    nc.scalar.activation(own_t[:, f.parity, :], xt_bank[:, 0:P], ACT.Copy).then_inc(own_copied, 1)
                if n:
                    act.wait_ge(logit_product, n.n + 1)
                    act.wait_ge(made, 1)
                    nc.scalar.activation(logits[:, bass.ds(n.n, 1), :].rearrange("p n e -> p (n e)"),
                                         logit_bank[:, 0:EXPERTS + 1], ACT.Copy).then_inc(logit_copied, 1)
            act.wait_ge(logit_copied, GROUPS)
            nc.scalar.activation(half_tanh[:, :], logits[:, :, EXPERTS], ACT.Tanh, scale=0.5).then_inc(tanh_done, 1)
            act.wait_ge(chain, 2)
            nc.scalar.activation(probs[:, :, :], rest[:, :, :], ACT.Exp).then_inc(exped, 1)

        @block.vector
        def _(dve):
            dve.wait_ge(shared["loaded"], shared["loaded_count"])
            dve.wait_ge(shared["params"], shared["params_count"])
            dve.sem_inc(made, 1)
            norm.fold_on_vector(dve)
            for step in steps(dve, GROUPS, PEEL, DEEPEST):
                g = step.group(LAG_LN)
                if g:
                    if past(g.n - 1):
                        dve.wait_ge(turned, g.n - 1)
                    norm.rows_on_vector(dve, xn[:, g.parity, :], x, g.n).then_inc(xn_done, 1)
            whole = [P, GROUPS, EXPERTS]
            count = [0]

            def then(instruction):
                count[0] += 1
                instruction.then_inc(chain, 1)
                dve.wait_ge(chain, count[0])

            def wide(column_per_group):
                return column_per_group.rearrange("p (n o) -> p n o", o=1).broadcast_to(whole)

            rank = const["expert_rank"].rearrange("p (o e) -> p o e", o=1).broadcast_to(whole)
            dve.wait_ge(logit_copied, GROUPS)
            then(nc.vector.tensor_reduce(one[:, :], logits[:, :, 0:EXPERTS], AXIS_X, ALU.max))
            then(nc.vector.tensor_tensor(rest[:, :, :], logits[:, :, 0:EXPERTS], wide(one[:, :]), ALU.subtract))
            dve.wait_ge(exped, 1)
            then(nc.vector.tensor_reduce(one[:, :], probs[:, :, :], AXIS_X, ALU.add))
            then(nc.vector.reciprocal(one[:, :], one[:, :]))
            then(nc.vector.tensor_tensor(probs[:, :, :], probs[:, :, :], wide(one[:, :]), ALU.mult))
            then(nc.vector.tensor_copy(rest[:, :, :], probs[:, :, :]))
            for turn in range(2):
                then(nc.vector.tensor_reduce(one[:, :], rest[:, :, :], AXIS_X, ALU.max))
                then(nc.vector.tensor_tensor(ranks[:, :, :], rest[:, :, :], wide(one[:, :]), ALU.is_equal))
                then(nc.vector.tensor_tensor(ranks[:, :, :], ranks[:, :, :], rank, ALU.mult))
                then(nc.vector.tensor_reduce(one[:, :], ranks[:, :, :], AXIS_X, ALU.max))
                then(nc.vector.tensor_tensor(chosen[:, :, :], ranks[:, :, :], wide(one[:, :]), ALU.is_equal))
                if turn == 0:
                    then(nc.vector.tensor_tensor(share[:, :, 0:EXPERTS], chosen[:, :, :], probs[:, :, :], ALU.mult))
                    then(nc.vector.scalar_tensor_tensor(out=rest[:, :, :], in0=chosen[:, :, :], scalar=-2.0,
                                                        in1=rest[:, :, :], op0=ALU.mult, op1=ALU.add))
                else:
                    then(nc.vector.tensor_tensor(chosen[:, :, :], chosen[:, :, :], probs[:, :, :], ALU.mult))
                    then(nc.vector.tensor_tensor(share[:, :, 0:EXPERTS], share[:, :, 0:EXPERTS], chosen[:, :, :],
                                                 ALU.add))
            dve.wait_ge(tanh_done, 1)
            then(nc.vector.tensor_scalar(share[:, :, EXPERTS], half_tanh[:, :], 0.5, 0.5, ALU.mult, ALU.add))


PHASES = range(6)


def program(nc, x_in, ctx_t, ctx_rows, ctx_last, mask, constants, matrices, columns, rows, window_bias, out):
    with ExitStack() as stack:
        mem = Memory(nc, stack, "all")
        matrix_at, matrix_width = offsets(MATRICES)
        column_at, column_width = offsets(COLUMNS)
        row_at, row_width = offsets(ROWS)
        const_at, const_width = offsets({k: CONST_WIDTH[k] for k in CONSTANTS})
        x = mem.sbuf("x", [P, GROUPS * D])
        const_sb = mem.sbuf("constants", [P, const_width])
        matrix_sb = mem.sbuf("matrices", [P, matrix_width])
        column_sb = mem.sbuf("columns", [P, column_width])
        row_sb = mem.sbuf("rows", [P, row_width])
        minus_half = mem.sbuf("minus_half", [P, 1])
        PIECE = 8
        x_loaded = [mem.sem(f"x_loaded{i}") for i in range(GROUPS // PIECE)]
        params, rest_loaded, stored = mem.sem("params"), mem.sem("rest_loaded"), mem.sem("stored")

        def piece(tile, where):
            def get(name, part=None, width=D):
                at, whole = where[name]
                return tile[:, at:at + whole] if part is None else tile[:, at + part * width:at + (part + 1) * width]
            return get

        norm = Norm(nc, mem)
        shared = {"norm": norm, "finished": [], "x": x, "weight": piece(matrix_sb, matrix_at), "column": piece(column_sb, column_at),
                  "row": piece(row_sb, row_at), "minus_half": minus_half,
                  "const": {k: const_sb[:, at:at + w] for k, (at, w) in const_at.items()},
                  "router": matrix_sb[:, matrix_at["moe_router"][0]:matrix_at["moe_gate_w"][0] + 1],
                  "loaded": x_loaded[-1], "loaded_count": 16, "params": params, "params_count": 16 * 4 + 1}
        first_width = matrix_at["sa_q"][0]
        x_pieces = [slice(i * PIECE, (i + 1) * PIECE) for i in range(GROUPS // PIECE)]
        x_rows = x_in.rearrange("(n b) q d -> (b q) n d", b=BG)
        out_rows = out.rearrange("(n b) q d -> (b q) n d", b=BG)

        block = nc.Block()
        with block:
            @block.sync
            def _(sp):
                for piece, done in zip(x_pieces, x_loaded):
                    sp.dma_start(x[:, piece.start * D:piece.stop * D].rearrange("p (n d) -> p n d", d=D),
                                 x_rows[:, piece, :]).then_inc(done, 16)
                sp.dma_start(matrix_sb[:, first_width:], matrices[:, first_width:]).then_inc(rest_loaded, 16)

            @block.scalar
            def _(act):
                act.dma_start(const_sb[:, :], constants).then_inc(params, 16)
                act.dma_start(matrix_sb[:, 0:first_width], matrices[:, 0:first_width]).then_inc(params, 16)
                act.dma_start(row_sb[:, :], rows.broadcast_to([P, row_width])).then_inc(params, 16)
                act.dma_start(column_sb[:, :], columns).then_inc(params, 16)

            @block.vector
            def _(dve):
                nc.vector.memset(minus_half[:, :], -0.5).then_inc(params, 1)
                for piece, done in zip(x_pieces, x_loaded):
                    dve.wait_ge(done, 16)
                    for n in range(piece.start, piece.stop):
                        norm.stats_on_vector(x, n)

        if 0 in PHASES:
            cross_attention(nc, shared, ctx_t, mask, rest_loaded)
            norm.next_layer()
        if 1 in PHASES:
            self_attention(nc, shared, "sa", windowed=False)
            norm.next_layer()
        context = Context(mem, ctx_t, ctx_rows, ctx_last)
        if 2 in PHASES:
            channel_mix(nc, shared, context)
            norm.next_layer()
        if 3 in PHASES:
            similarity_attention(nc, shared, context)
            norm.next_layer()
        if 4 in PHASES:
            inner = mem.sbuf("inner", [P, GROUPS * D])
            self_attention(nc, shared, "wa", windowed=True, window_bias=window_bias, inner=inner)
            norm.next_layer()
            gelu_block(nc, shared, inner)
            norm.next_layer()
        if 5 in PHASES:
            mixture(nc, shared, out_rows, stored)


def kernel(**inputs):
    import numpy as _np
    import concourse.bacc as _bacc
    from concourse import mybir as _mybir
    from concourse.bass_utils import run_bass_kernel_spmd as _run

    a = {k: _np.asarray(v) for k, v in inputs.items()}

    def chunks(w):
        return w.reshape(-1, P, w.shape[-1]).transpose(1, 0, 2).reshape(P, -1)

    matrices = {
        "xa_q": a["L0_xattn_wq"].T, "xa_k": a["L0_xattn_wk"].T, "xa_v": a["L0_xattn_wv"].T,
        "xa_o": a["L0_xattn_wo"].T,
        "sa_q": a["L0_attn_Wq"], "sa_k": a["L0_attn_Wk"], "sa_v": a["L0_attn_Wv"], "sa_o": a["L0_attn_Wo"],
        "cm_r": a["L0_ffn_W_r"].T, "cm_k": a["L0_ffn_W_k"].T, "cm_v": a["L0_ffn_W_v"].T,
        "bi_qv": chunks(a["L1_xattn_W_qv"]),
        "wa_qkv": a["L1_attn_qkv_w"], "wa_gate": a["L1_attn_gate_w"], "wa_o": a["L1_attn_out_w"],
        "wa_fc1": a["L1_attn_fc1_w"], "wa_fc2": chunks(a["L1_attn_fc2_w"]),
        "moe_router": a["L1_ffn_router_w"], "moe_gate_w": a["L1_ffn_shared_gate_w"],
        "moe_w1": a["L1_ffn_w1"].transpose(1, 0, 2).reshape(P, -1),
        "moe_w2": a["L1_ffn_w2"].transpose(1, 0, 2).reshape(P, -1),
        "moe_gate_up": a["L1_ffn_shared_gate_up"], "moe_down": a["L1_ffn_shared_down"],
    }
    w_sim = a["L1_xattn_w_sim"].reshape(3, D)
    columns = {
        "xa_bq": a["L0_xattn_bq"], "xa_bk": a["L0_xattn_bk"], "xa_bv": a["L0_xattn_bv"],
        "sa_bq": a["L0_attn_bq"], "sa_bk": a["L0_attn_bk"], "sa_bv": a["L0_attn_bv"],
        "cm_mu_r": a["L0_ffn_mu_r"], "cm_mu_k": a["L0_ffn_mu_k"], "bi_w2": w_sim[1], "bi_w3": w_sim[2],
        "wa_g1": a["L1_attn_ln1_g"], "wa_b1": a["L1_attn_ln1_b"], "wa_bqkv": a["L1_attn_qkv_b"],
        "wa_bgate": a["L1_attn_gate_b"], "wa_g2": a["L1_attn_ln2_g"], "wa_b2": a["L1_attn_ln2_b"],
        "wa_bfc1": a["L1_attn_fc1_b"],
    }
    rows = {"xa_bo": a["L0_xattn_bo"], "sa_bo": a["L0_attn_bo"], "bi_w1": w_sim[0],
            "bi_bqv": a["L1_xattn_b_qv"], "wa_bo": a["L1_attn_out_b"], "wa_bfc2": a["L1_attn_fc2_b"],
            "bi_b": a["L1_xattn_b_sim"]}
    ctx = a["ctx_1024"]
    distance = _np.maximum(_np.arange(S)[:, None] - _np.arange(S)[None, :], 0)
    toeplitz = a["L1_attn_pos_bias"][distance].transpose(0, 2, 1).reshape(S, H * S)
    constants = shape_constants()
    arrays = {
        "x": a["x"],
        "ctx_t": ctx.transpose(2, 0, 1).reshape(D, B * KEYS),
        "ctx_rows": ctx[:, :LAST].reshape(B, CHUNKS, P, D).transpose(2, 0, 1, 3).reshape(P, B * CHUNKS * D),
        "ctx_last": ctx[:, LAST],
        "mask": a["mask_BxS2_ff1"].reshape(1, B * KEYS),
        "constants": _np.concatenate([constants[k] for k in CONSTANTS], axis=1),
        "matrices": _np.concatenate([matrices[k] for k in MATRICES], axis=1),
        "columns": _np.concatenate([columns[k].reshape(-1, P) for k in COLUMNS], axis=0).T,
        "rows": _np.concatenate([rows[k] for k in ROWS]).reshape(1, -1),
        "window_bias": toeplitz,
    }
    arrays = {f"in_{k}_dram": _np.ascontiguousarray(v) for k, v in arrays.items()}
    nc = _bacc.Bacc("TRN2", target_bir_lowering=False, num_devices=1)
    args = [nc.dram_tensor(k, v.shape, _mybir.dt.from_np(v.dtype), kind="ExternalInput").ap()
            for k, v in arrays.items()]
    out = nc.dram_tensor("out_dram", a["x"].shape, F32, kind="ExternalOutput").ap()
    program(nc, *args, out)
    r = _run(nc, [arrays], core_ids=[0])
    return r.results[0]["out_dram"]
```

```python
from contextlib import ExitStack

import concourse.bass as bass
import numpy as np
from concourse import mybir

F32 = mybir.dt.float32
ACT = mybir.ActivationFunctionType
ALU = mybir.AluOpType
AXIS_X = mybir.AxisListType.X

P = 128
B, S, D = 128, 32, 128
KEYS = 257
H, DH = 16, 8
BG = P // S
GROUPS = B // BG
CHUNKS = KEYS // P
LAST = CHUNKS * P
HG = P // S
NHG = H // HG
FF = 512
EXPERTS = 8
BIG = 3.0e38
LN_EPS = 1e-5
QK_SCALE = DH ** -0.5


def shape_constants():
    row = np.arange(P)[:, None]
    col = np.arange(P)[None, :]
    tables = {
        "identity": row == col,
        "head": row // DH == np.arange(H)[None, :],
        "head_in_group": (row // DH) % HG == np.arange(HG)[None, :],
        "head_of_row": row // S == np.arange(HG)[None, :],
        "same_sequence": row // S == col // S,
        "other_sequence": np.where(row // S == col // S, 0.0, -BIG),
        "causal_bound": np.where(np.arange(S)[None, :] <= row % S, BIG, -10000.0),
        "causal_sum": np.where(np.arange(S)[None, :] <= row % S, 0.0, -1.0e30),
        "expert_rank": EXPERTS - np.arange(EXPERTS)[None, :],
    }
    return {k: np.broadcast_to(v, (P, v.shape[1])).astype(np.float32) for k, v in tables.items()}


CONST_WIDTH = {"identity": P, "head": H, "head_in_group": HG, "head_of_row": HG, "same_sequence": P, "other_sequence": P,
               "causal_bound": S, "causal_sum": S, "expert_rank": EXPERTS}
CONSTANTS = list(CONST_WIDTH)
MATRICES = {"xa_q": D, "xa_k": D, "xa_v": D, "xa_o": D,
            "sa_q": D, "sa_k": D, "sa_v": D, "sa_o": D,
            "cm_r": D, "cm_k": D, "cm_v": D,
            "bi_qv": 4 * D,
            "wa_qkv": 3 * D, "wa_gate": D, "wa_o": D, "wa_fc1": FF, "wa_fc2": (FF // P) * D,
            "moe_router": EXPERTS, "moe_gate_w": 1, "moe_w1": EXPERTS * D, "moe_w2": EXPERTS * D,
            "moe_gate_up": 2 * D, "moe_down": D}
COLUMNS = {"xa_bq": 1, "xa_bk": 1, "xa_bv": 1, "sa_bq": 1, "sa_bk": 1, "sa_bv": 1,
           "cm_mu_r": 1, "cm_mu_k": 1, "bi_w2": 1, "bi_w3": 1,
           "wa_g1": 1, "wa_b1": 1, "wa_bqkv": 3, "wa_bgate": 1, "wa_g2": 1, "wa_b2": 1,
           "wa_bfc1": FF // P}
ROWS = {"xa_bo": D, "sa_bo": D, "bi_w1": D, "bi_bqv": D, "wa_bo": D, "wa_bfc2": D, "bi_b": 1}


def offsets(widths):
    out, at = {}, 0
    for name, width in widths.items():
        out[name] = (at, width)
        at += width
    return out, at


class Group:

    def __init__(self, n, slot, lap):
        self.n, self.slot, self.parity, self.lap = n, slot, slot % 2, lap


class Step:

    def __init__(self, j, base, count, body):
        self.j, self.base, self.count, self.body = j, base, count, body

    def group(self, lag):
        at = self.base - lag
        if isinstance(self.j, int):
            if not 0 <= at < self.count:
                return None
            return Group(at, at % self.body, at // self.body)
        return Group(self.j * self.body + at, at % self.body, self.j + at // self.body)


def steps(engine, count, peel, deepest, body=2):
    assert body % 2 == 0 and peel > deepest and (count - peel) % body == 0
    for t in range(peel):
        yield Step(0, t, count, body)
    with engine.Fori(0, (count - peel) // body) as j:
        for u in range(body):
            yield Step(j, peel + u, count, body)
    for t in range(count, count + deepest):
        yield Step(0, t, count, body)


def past(value):
    return not isinstance(value, int) or value > 0


def in_register(engine, value):
    return value if isinstance(value, int) else engine.to_reg(value)


class Memory:

    def __init__(self, nc, stack, prefix):
        self.nc, self.stack, self.prefix, self.semaphores = nc, stack, prefix, []

    def sbuf(self, name, shape):
        return self.stack.enter_context(self.nc.sbuf_tensor(f"{self.prefix}_{name}", shape, F32))

    def psum(self, name, shape):
        return self.stack.enter_context(self.nc.psum_tensor(f"{self.prefix}_{name}", shape, F32))

    def sem(self, name):
        self.semaphores.append(self.nc.alloc_semaphore(f"{self.prefix}_{name}"))
        return self.semaphores[-1]


def clear_finished(nc, shared, mem):
    if shared["finished"]:
        nc.clear_and_free_semaphores(shared["finished"])
    shared["finished"] = mem.semaphores


class Norm:
    FOLDS = 9
    PIECES = [slice(0, 2)] + [slice(at, at + 6) for at in range(2, GROUPS, 6)]

    def __init__(self, nc, mem):
        self.nc = nc
        self.stats = mem.sbuf("stats", [P, GROUPS, 2, 3])
        self.mean = mem.sbuf("mean", [P, GROUPS])
        self.part = mem.sbuf("part", [P, 3, GROUPS])
        self.variance = mem.sbuf("variance", [P, 2, GROUPS])
        self.rstd = mem.sbuf("rstd", [P, 2, GROUPS])
        self.stats_done, self.folded, self.rstd_done = (mem.sem(k) for k in ("stats_done", "folded", "rstd_done"))
        self.layer = 0

    def next_layer(self):
        self.layer += 1

    def stats_on_vector(self, rows, n):
        self.nc.vector.bn_stats(self.stats[:, bass.ds(n, 1), :, :].rearrange("p n h s -> p (n h s)"),
                                rows[:, bass.ds(n * D, D)]).then_inc(self.stats_done, 1)

    def fold_on_vector(self, dve):
        v, part, base = self.nc.vector, self.part, self.layer * self.FOLDS

        def after(k):
            dve.wait_ge(self.folded, base + k)

        dve.wait_ge(self.stats_done, GROUPS * (self.layer + 1))
        means, squares = self.stats[:, :, :, 1], self.stats[:, :, :, 2]
        v.tensor_tensor(part[:, 0, :], means[:, :, 0], means[:, :, 1], ALU.subtract).then_inc(self.folded, 1)
        v.tensor_tensor(part[:, 1, :], squares[:, :, 0], squares[:, :, 1], ALU.add).then_inc(self.folded, 1)
        after(1)
        v.tensor_tensor(part[:, 2, :], part[:, 0, :], part[:, 0, :], ALU.mult).then_inc(self.folded, 1)
        after(2)
        v.tensor_scalar(part[:, 1, :], part[:, 1, :], 1.0 / D, None, ALU.mult).then_inc(self.folded, 1)
        v.tensor_tensor(self.mean[:, :], means[:, :, 0], means[:, :, 1], ALU.add).then_inc(self.folded, 1)
        after(4)
        v.scalar_tensor_tensor(out=part[:, 0, :], in0=part[:, 2, :], scalar=0.25, in1=part[:, 1, :],
                               op0=ALU.mult, op1=ALU.add).then_inc(self.folded, 1)
        after(5)
        v.tensor_scalar(self.mean[:, :], self.mean[:, :], 0.5, None, ALU.mult).then_inc(self.folded, 1)
        after(6)
        v.tensor_scalar(self.variance[:, 0, :], part[:, 0, :], LN_EPS, None, ALU.add).then_inc(self.folded, 1)
        v.tensor_scalar(self.variance[:, 1, :], part[:, 0, :], 1.0 + LN_EPS, LN_EPS * LN_EPS, ALU.mult,
                        ALU.add).then_inc(self.folded, 1)

    def rstd_on_gpsimd(self, pool, piece, minus_half, twice=False):
        if piece == 0:
            pool.wait_ge(self.folded, self.layer * self.FOLDS + (9 if twice else 8))
        kinds, groups = 2 if twice else 1, self.PIECES[piece]
        shape = [P, kinds, groups.stop - groups.start]
        self.nc.gpsimd.tensor_tensor(self.rstd[:, 0:kinds, groups], self.variance[:, 0:kinds, groups],
                                     minus_half[:, 0:1].rearrange("p (k g) -> p k g", k=1).broadcast_to(shape),
                                     ALU.pow).then_inc(self.rstd_done, 1)

    def next_rstd_on_gpsimd(self, pool, step, minus_half, twice=False):
        if isinstance(step.j, int) and step.base + 1 < len(self.PIECES):
            self.rstd_on_gpsimd(pool, step.base + 1, minus_half, twice)

    def rows_on_vector(self, dve, out, rows, n, last_before_loop, twice=False):
        before = self.layer * len(self.PIECES)
        starts = [piece.start for piece in self.PIECES]
        if isinstance(n, int) and n in (0, last_before_loop):
            dve.wait_ge(self.folded, (self.layer + 1) * self.FOLDS)
        if isinstance(n, int) and n == last_before_loop:
            dve.wait_ge(self.rstd_done, before + len(starts))
        elif isinstance(n, int) and n in starts:
            dve.wait_ge(self.rstd_done, before + starts.index(n) + 1)
        k = 1 if twice else 0
        return self.nc.vector.tensor_scalar(
            out, rows[:, bass.ds(n * D, D)], self.mean[:, bass.ds(n, 1)],
            self.rstd[:, k, bass.ds(n, 1)], ALU.subtract, ALU.mult)


def cross_attention(nc, shared, ctx_t, mask, start, rest_loaded):
    with ExitStack() as stack:
        mem = Memory(nc, stack, "xa")
        UNITS = BG * NHG // 2
        KCOLS = BG * KEYS
        KPART = [(0, 343), (343, 343), (686, 342)]
        LAG_LN, LAG_FRONT, LAG_STREAM, LAG_TAIL, LAG_STATS = 0, 1, 2, 3, 4
        PEEL, DEEPEST = 6, 4
        norm = shared["norm"]
        x, const, weight, column, row = (shared[k] for k in ("x", "const", "weight", "column", "row"))

        ctx = [mem.sbuf(f"ctx{i}", [P, KCOLS]) for i in range(2)]
        mask_raw = [mem.sbuf(f"mask_raw{i}", [P, KCOLS]) for i in range(2)]
        mask_add = [mem.sbuf(f"mask_add{i}", [P, KCOLS]) for i in range(2)]
        xn = mem.sbuf("xn", [P, 2, D])
        xn_t = mem.sbuf("xn_t", [P, 2, P])
        q_t = mem.sbuf("q_t", [P, 2, P])
        q_blocks = [mem.sbuf(f"q_blocks{i}", [P, BG, H, S]) for i in range(2)]
        k_t = [mem.sbuf(f"k_t{i}", [P, KCOLS]) for i in range(2)]
        v = [mem.sbuf(f"v{i}", [P, BG, CHUNKS, D]) for i in range(2)]
        ctx_diff = [mem.sbuf(f"ctx_diff{i}", [P, BG, LAST]) for i in range(2)]
        last_v_t = mem.sbuf("last_v_t", [P, 2, BG])
        probs = [mem.sbuf(f"probs{i}", [P, BG * NHG, KEYS]) for i in range(2)]
        neg_max = mem.sbuf("neg_max", [P, 2, BG * NHG])
        den = mem.sbuf("den", [P, 2, BG * NHG])
        inv_den = mem.sbuf("inv_den", [P, 2, BG * NHG])
        probs_t = mem.sbuf("probs_t", [P, 4, 2, CHUNKS, P])
        z_heads = mem.sbuf("z_heads", [P, BG, HG, S])
        z_sum = mem.sbuf("z_sum", [P, BG, S])
        z_t = mem.sbuf("z_t", [P, BG, S])
        x_bias = mem.sbuf("x_bias", [P, 2, D])
        bias = mem.sbuf("bias", [P, D])

        scores = [mem.psum(f"scores{i}", [P, 2, 512]) for i in range(2)]
        turned = [mem.psum(f"turned{i}", [P, 2, CHUNKS, P]) for i in range(2)]
        z = mem.psum("z", [P, BG, P])
        front = mem.psum("front", [P, 512])

        ctx_loaded = [mem.sem(f"ctx_loaded{i}") for i in range(2)]
        mask_loaded = [mem.sem(f"mask_loaded{i}") for i in range(2)]
        xn_done = mem.sem("xn_done")
        bias_product, bias_ready = mem.sem("bias_product"), mem.sem("bias_ready")
        xn_turned, xn_copied = mem.sem("xn_turned"), mem.sem("xn_copied")
        q_product, q_copied, q_spread = mem.sem("q_product"), mem.sem("q_copied"), mem.sem("q_spread")
        k_product, k_copied = mem.sem("k_product"), mem.sem("k_copied")
        v_product, v_copied = mem.sem("v_product"), mem.sem("v_copied")
        ctx_diffed = mem.sem("ctx_diffed")
        last_v_product, last_v_copied = mem.sem("last_v_product"), mem.sem("last_v_copied")
        mask_ready = mem.sem("mask_ready")
        scored, maxed, exped, inverted, normed = (
            mem.sem(k) for k in ("scored", "maxed", "exped", "inverted", "normed"))
        p_turned, p_copied, pv_done = (mem.sem(k) for k in ("p_turned", "p_copied", "pv_done"))
        z_masked, z_reduced, z_summed, o_product = (
            mem.sem(k) for k in ("z_masked", "z_reduced", "z_summed", "o_product"))
        x_biased, x_updated = mem.sem("x_biased"), mem.sem("x_updated")

        def unit_count(g, u):
            return g.n * UNITS + (u + 1)

        def unit_before(tail, stream, u, back):
            return (stream, u - back) if u >= back else (tail, u - back + UNITS)

        block = stack.enter_context(nc.Block())

        @block.sync
        def _(sp):
            def load(n, parity, wait):
                if wait:
                    sp.wait_ge(last_v_product, n - 1)
                    sp.wait_ge(ctx_diffed, n - 1)
                sp.dma_start(ctx[parity][:, :], ctx_t[:, bass.ds(n * KCOLS, KCOLS)]).then_inc(
                    ctx_loaded[parity], 16)
                if wait:
                    sp.wait_ge(mask_ready, n - 1)
                sp.dma_start(mask_raw[parity][:, :],
                             mask[:, bass.ds(n * KCOLS, KCOLS)].broadcast_to([P, KCOLS])).then_inc(
                    mask_loaded[parity], 16)

            start["load_x"](sp)
            for n in range(2):
                load(n, n, False)
            start["load_rest"](sp)
            with sp.Fori(0, (GROUPS - 2) // 2) as j:
                for parity in range(2):
                    load(j * 2 + (2 + parity), parity, True)
            sp.wait_ge(rest_loaded, 16 * (1 + BG))

        @block.gpsimd
        def _(pool):
            clear_finished(nc, shared, mem)
            pool.wait_ge(shared["loaded"], shared["loaded_count"])
            pool.wait_ge(shared["params"], shared["params_count"])
            norm.rstd_on_gpsimd(pool, 0, shared["minus_half"])
            for step in steps(pool, GROUPS, PEEL, DEEPEST):
                f = step.group(LAG_FRONT)
                if f:
                    pool.wait_ge(ctx_loaded[f.parity], (f.lap + 1) * 16)
                    if past(f.n - 1):
                        pool.wait_ge(v_product, (f.n - 1) * 2)
                    keys = ctx[f.parity][:, :].rearrange("p (b k) -> p b k", b=BG)
                    nc.gpsimd.tensor_tensor(ctx_diff[f.parity][:, :, :], keys[:, :, 0:LAST],
                                            keys[:, :, LAST:KEYS].broadcast_to([P, BG, LAST]),
                                            ALU.subtract).then_inc(ctx_diffed, 1)
                    loads = in_register(pool, (f.lap + 1) * 16)
                    units = in_register(pool, (f.n - 1) * UNITS)
                    pool.wait_ge(bias_ready, 1)
                    pool.wait_ge(mask_loaded[f.parity], loads)
                    if past(units):
                        pool.wait_ge(maxed, units)
                    nc.gpsimd.tensor_scalar(mask_add[f.parity][:, :], mask_raw[f.parity][:, :],
                                            -10000.0, 10000.0, ALU.mult, ALU.add).then_inc(mask_ready, 1)
                    pool.wait_ge(q_copied, f.n + 1)
                    if past(f.n - 1):
                        pool.wait_ge(scored, (f.n - 1) * UNITS)
                    for b in range(BG):
                        last = nc.gpsimd.tensor_tensor(
                            q_blocks[f.parity][:, b, :, :],
                            q_t[:, f.parity, b * S:(b + 1) * S].rearrange("p (o q) -> p o q", o=1).broadcast_to([P, H, S]),
                            const["head"].rearrange("p (h o) -> p h o", o=1).broadcast_to([P, H, S]),
                            ALU.mult)
                    last.then_inc(q_spread, 1)
                m = step.group(LAG_TAIL)
                if m:
                    if past(m.n - 1):
                        pool.wait_ge(x_updated, m.n - 1)
                    pool.wait_ge(bias_ready, 1)
                    nc.gpsimd.tensor_tensor(x_bias[:, m.parity, :], x[:, bass.ds(m.n * D, D)], bias[:, :],
                                            ALU.add).then_inc(x_biased, 1)
                norm.next_rstd_on_gpsimd(pool, step, shared["minus_half"])

        @block.tensor
        def _(pe):
            pe.wait_ge(shared["loaded"], shared["loaded_count"])
            pe.wait_ge(shared["params"], shared["params_count"])
            nc.tensor.matmul(front[:, 0:D], column("xa_bv").broadcast_to([P, P]), weight("xa_o"),
                             start=True, stop=True).then_inc(bias_product, 1)
            pe.wait_ge(bias_ready, 1)
            for step in steps(pe, GROUPS, PEEL, DEEPEST):
                f, n, m = step.group(LAG_FRONT), step.group(LAG_STREAM), step.group(LAG_TAIL)
                for u in range(UNITS):
                    if n:
                        b, gp = u // 2, u % 2
                        if u == 0:
                            pe.wait_ge(q_spread, n.n + 1)
                            pe.wait_ge(k_copied, (n.n + 1) * 3)
                        if past(unit_count(n, u) - 2):
                            pe.wait_ge(exped, unit_count(n, u) - 2)
                        for i in range(2):
                            g = gp * 2 + i
                            mm = nc.tensor.matmul(
                                scores[u % 2][:, i, 0:KEYS],
                                q_blocks[n.parity][:, b, g * HG:(g + 1) * HG, :].rearrange("p h q -> p (h q)"),
                                k_t[n.parity][:, b * KEYS:(b + 1) * KEYS], start=True, stop=True)
                        mm.then_inc(scored, 1)
                    w, wu = unit_before(m, n, u, 2)
                    if w:
                        pe.wait_ge(normed, unit_count(w, wu))
                        if past(unit_count(w, wu) - 2):
                            pe.wait_ge(p_copied, unit_count(w, wu) - 2)
                        for i in range(2):
                            for c in range(CHUNKS):
                                mm = nc.tensor.transpose(
                                    turned[u % 2][:, i, c, :],
                                    probs[w.parity][:, wu * 2 + i, c * P:(c + 1) * P], const["identity"])
                        mm.then_inc(p_turned, 1)
                    w, wu = unit_before(m, n, u, 4)
                    if u % 2 == 0 and w:
                        b = wu // 2
                        pe.wait_ge(p_copied, unit_count(w, wu + 1))
                        if b == 0:
                            pe.wait_ge(v_copied, (w.n + 1) * 2)
                            if past(w.n):
                                pe.wait_ge(z_masked, w.n)
                        for c in range(CHUNKS):
                            for g in range(NHG):
                                rows = slice(g * HG * DH, (g + 1) * HG * DH)
                                mm = nc.tensor.matmul(
                                    z[rows, b, :], v[w.parity][:, b, c, rows],
                                    probs_t[:, (wu + g // 2) % 4, g % 2, c, :],
                                    start=(c == 0), stop=(c == CHUNKS - 1),
                                    skip_group_check=True)
                        mm.then_inc(pv_done, 1)
                    if f and u == 0:
                        pe.wait_ge(xn_done, f.n + 1)
                        if past(f.n):
                            pe.wait_ge(last_v_copied, f.n)
                        if m and past(m.n):
                            pe.wait_ge(x_updated, m.n)
                        nc.tensor.transpose(front[:, 0:P], xn[:, f.parity, :], const["identity"]).then_inc(xn_turned, 1)
                    if f and u == 1:
                        pe.wait_ge(xn_copied, f.n + 1)
                        nc.tensor.matmul(front[:, P:2 * P], weight("xa_q"), xn_t[:, f.parity, :],
                                         start=True, stop=True).then_inc(q_product, 1)
                    if f and 2 <= u < 5:
                        at, width = KPART[u - 2]
                        if u == 2:
                            pe.wait_ge(ctx_loaded[f.parity], (f.lap + 1) * 16)
                            pe.wait_ge(q_copied, f.n + 1)
                        else:
                            pe.wait_ge(k_copied, f.n * 3 + (u - 2))
                        nc.tensor.matmul(front[:, 0:width], weight("xa_k"), ctx[f.parity][:, at:at + width],
                                         start=True, stop=True).then_inc(k_product, 1)
                    if f and 5 <= u < 7:
                        if u == 5:
                            pe.wait_ge(ctx_diffed, f.n + 1)
                            pe.wait_ge(k_copied, (f.n + 1) * 3)
                        else:
                            pe.wait_ge(v_copied, f.n * 2 + 1)
                        for i in range(2):
                            for c in range(CHUNKS):
                                mm = nc.tensor.matmul(front[:, (2 * i + c) * D:(2 * i + c + 1) * D],
                                                      ctx_diff[f.parity][:, 2 * (u - 5) + i, c * P:(c + 1) * P],
                                                      weight("xa_v"), start=True, stop=True)
                        mm.then_inc(v_product, 1)
                    if f and u == 7:
                        pe.wait_ge(v_copied, (f.n + 1) * 2)
                        keys = ctx[f.parity][:, :].rearrange("p (b k) -> p b k", b=BG)
                        nc.tensor.matmul(front[:, 0:BG], weight("xa_v"), keys[:, :, LAST],
                                         start=True, stop=True).then_inc(last_v_product, 1)
                    if m and u == 7:
                        pe.wait_ge(z_summed, m.n + 1)
                        nc.tensor.matmul(front[:, 384:384 + D], z_t[:, :, :].rearrange("p b q -> p (b q)"),
                                         weight("xa_o"), start=True, stop=True).then_inc(o_product, 1)

        @block.scalar
        def _(act):
            start["load_params"](act)
            act.wait_ge(shared["loaded"], shared["loaded_count"])
            act.wait_ge(shared["params"], shared["params_count"])
            for step in steps(act, GROUPS, PEEL, DEEPEST):
                f, n, m = step.group(LAG_FRONT), step.group(LAG_STREAM), step.group(LAG_TAIL)
                for u in range(UNITS):
                    if f and u == 1:
                        act.wait_ge(xn_turned, f.n + 1)
                        nc.scalar.activation(xn_t[:, f.parity, :], front[:, 0:P], ACT.Copy).then_inc(xn_copied, 1)
                    if f and 3 <= u < 6:
                        at, width = KPART[u - 3]
                        act.wait_ge(k_product, f.n * 3 + (u - 2))
                        if u == 3 and past(f.n - 1):
                            act.wait_ge(scored, (f.n - 1) * UNITS)
                        nc.scalar.activation(k_t[f.parity][:, at:at + width], front[:, 0:width], ACT.Identity,
                                             bias=column("xa_bk")).then_inc(k_copied, 1)
                    if f and 6 <= u < 8:
                        act.wait_ge(v_product, f.n * 2 + (u - 5))
                        if u == 6 and past(f.n - 1):
                            act.wait_ge(pv_done, (f.n - 1) * BG)
                        nc.scalar.activation(
                            v[f.parity][:, 2 * (u - 6):2 * (u - 5), :, :].rearrange("p b c d -> p (b c d)"),
                            front[:, 0:512], ACT.Copy).then_inc(v_copied, 1)
                    w, wu = unit_before(m, n, u, 2)
                    if w:
                        act.wait_ge(p_turned, unit_count(w, wu))
                        if past(w.n * BG + (wu // 2 - 1)):
                            act.wait_ge(pv_done, w.n * BG + (wu // 2 - 1))
                        nc.scalar.activation(probs_t[:, wu % 4, :, :, :], turned[u % 2][:, :, :, :],
                                             ACT.Copy).then_inc(p_copied, 1)
                    if n:
                        act.wait_ge(maxed, unit_count(n, u))
                        if u == 0 and past(n.n - 1):
                            act.wait_ge(p_turned, (n.n - 1) * UNITS)
                        for i in range(2):
                            k = u * 2 + i
                            last = nc.scalar.activation(
                                probs[n.parity][:, k, :], scores[u % 2][:, i, 0:KEYS], ACT.Exp,
                                bias=neg_max[:, n.parity, k:k + 1], scale=-1.0,
                                accum_out=den[:, n.parity, k:k + 1])
                        last.then_inc(exped, 1)

        @block.vector
        def _(dve):
            start["first_stats"](dve)
            dve.wait_ge(shared["loaded"], shared["loaded_count"])
            dve.wait_ge(shared["params"], shared["params_count"])
            dve.wait_ge(bias_product, 1)
            nc.vector.tensor_tensor(bias[:, :], front[:, 0:D], row("xa_bo"), ALU.add).then_inc(bias_ready, 1)
            norm.fold_on_vector(dve)
            for step in steps(dve, GROUPS, PEEL, DEEPEST):
                g, s = step.group(LAG_LN), step.group(LAG_STATS)
                f, n, m = step.group(LAG_FRONT), step.group(LAG_STREAM), step.group(LAG_TAIL)
                for u in range(UNITS):
                    w, wu = unit_before(m, n, u, 1)
                    if w:
                        dve.wait_ge(exped, unit_count(w, wu))
                        nc.vector.reciprocal(inv_den[:, w.parity, wu * 2:wu * 2 + 2],
                                             den[:, w.parity, wu * 2:wu * 2 + 2]).then_inc(inverted, 1)
                    if n:
                        b = u // 2
                        units = in_register(dve, unit_count(n, u))
                        masks = in_register(dve, n.n + 1)
                        dve.wait_ge(bias_ready, 1)
                        dve.wait_ge(scored, units)
                        if u == 0:
                            dve.wait_ge(mask_ready, masks)
                        for i in range(2):
                            k = u * 2 + i
                            last = nc.vector.tensor_tensor_reduce(
                                scores[u % 2][:, i, 0:KEYS], scores[u % 2][:, i, 0:KEYS],
                                mask_add[n.parity][:, b * KEYS:(b + 1) * KEYS], 1.0, BIG, ALU.add, ALU.min,
                                neg_max[:, n.parity, k:k + 1])
                        last.then_inc(maxed, 1)
                    if w:
                        dve.wait_ge(inverted, unit_count(w, wu))
                        for i in range(2):
                            k = wu * 2 + i
                            last = nc.vector.tensor_scalar(probs[w.parity][:, k, 0:LAST], probs[w.parity][:, k, 0:LAST],
                                                           inv_den[:, w.parity, k:k + 1], None, ALU.mult)
                        last.then_inc(normed, 1)
                    if f and u == 1:
                        dve.wait_ge(q_product, f.n + 1)
                        if past(f.n - 1):
                            dve.wait_ge(q_spread, f.n - 1)
                        nc.vector.tensor_scalar(q_t[:, f.parity, :], front[:, P:2 * P], column("xa_bq"), -QK_SCALE,
                                                ALU.add, ALU.mult).then_inc(q_copied, 1)
                    if m and u == 3:
                        dve.wait_ge(pv_done, (m.n + 1) * BG)
                        nc.vector.tensor_tensor(
                            z_heads[:, :, :, :], z[:, :, :].rearrange("p b (h q) -> p b h q", h=HG),
                            const["head_in_group"].rearrange("p (o h i) -> p o h i", o=1, i=1).broadcast_to([P, BG, HG, S]),
                            ALU.mult).then_inc(z_masked, 1)
                    if m and u == 4:
                        dve.wait_ge(z_masked, m.n + 1)
                        nc.vector.tensor_reduce(z_sum[:, :, :], z_heads[:, :, :, :].rearrange("p b h q -> p b q h"),
                                                AXIS_X, ALU.add).then_inc(z_reduced, 1)
                    if m and u == 5:
                        dve.wait_ge(z_reduced, m.n + 1)
                        if past(m.n):
                            dve.wait_ge(o_product, m.n)
                        dve.wait_ge(last_v_copied, m.n + 1)
                        nc.vector.tensor_tensor(
                            z_t[:, :, :], z_sum[:, :, :],
                            last_v_t[:, m.parity, :].rearrange("p (b o) -> p b o", o=1).broadcast_to([P, BG, S]),
                            ALU.add).then_inc(z_summed, 1)
                    if f and u == 7:
                        dve.wait_ge(last_v_product, f.n + 1)
                        if m:
                            dve.wait_ge(o_product, m.n + 1)
                        nc.vector.tensor_copy(last_v_t[:, f.parity, :], front[:, 0:BG]).then_inc(last_v_copied, 1)
                    if m and u == 7:
                        dve.wait_ge(o_product, m.n + 1)
                        dve.wait_ge(x_biased, m.n + 1)
                        nc.vector.tensor_tensor(x[:, bass.ds(m.n * D, D)], front[:, 384:384 + D],
                                                x_bias[:, m.parity, :], ALU.add).then_inc(x_updated, 1)
                    if s and u == 2:
                        dve.wait_ge(x_updated, s.n + 1)
                        norm.stats_on_vector(x, s.n)
                    if g and u == 7:
                        if past(g.n - 1):
                            dve.wait_ge(xn_turned, g.n - 1)
                        norm.rows_on_vector(dve, xn[:, g.parity, :], x, g.n, PEEL - 1).then_inc(xn_done, 1)


def self_attention(nc, shared, name, windowed, distance_bias=None, inner=None):
    with ExitStack() as stack:
        mem = Memory(nc, stack, name)
        LAG_LN, LAG_QK, LAG_BLOCK, LAG_SCORE, LAG_VALUE, LAG_OUT, LAG_STATS = 0, 1, 2, 3, 4, 5, 6
        PEEL, DEEPEST, BODY = 8, 6, 4
        norm = shared["norm"]
        VW = HG * DH + HG
        KEY_BLOCKS_ON_POOL = 3
        x, const, weight, column, row = (shared[k] for k in ("x", "const", "weight", "column", "row"))
        if windowed:
            w_q, w_k, w_v = (weight("wa_qkv", i) for i in range(3))
            b_q, b_k, b_v = (column("wa_bqkv", i, 1) for i in range(3))
            w_o, bias = weight("wa_o"), row("wa_bo")
        else:
            w_q, w_k, w_v = (weight(k) for k in ("sa_q", "sa_k", "sa_v"))
            b_q, b_k, b_v = (column(k) for k in ("sa_bq", "sa_bk", "sa_bv"))
            w_o, bias = weight("sa_o"), row("sa_bo")

        xn = mem.sbuf("xn", [P, 2, D])
        xn_t = [mem.sbuf(f"xn_t{i}", [P, BG, HG, S]) for i in range(2)]
        q_t = mem.sbuf("q_t", [P, 2, BG, S])
        k_t = mem.sbuf("k_t", [P, 2, BG, S])
        k_blocks = [mem.sbuf(f"k_blocks{i}", [P, BG, H, S]) for i in range(2)]
        v_blocks = [mem.sbuf(f"v_blocks{i}", [P, BG, NHG, VW]) for i in range(2)]
        shifted = mem.sbuf("shifted", [P, 2, H, S])
        maxima = mem.sbuf("maxima", [P, 2, H])
        probs = mem.sbuf("probs", [P, 2, H, S])
        probs_t = mem.sbuf("probs_t", [P, 2, NHG, P])
        inv_den = mem.sbuf("inv_den", [P, 2, NHG, HG])
        z_rows = mem.sbuf("z_rows", [P, 2, D])
        z_t = mem.sbuf("z_t", [P, 2, P])
        x_bias = mem.sbuf("x_bias", [P, 2, D])
        scaled = mem.sbuf("scaled", [P, 3])
        if windowed:
            gate = mem.sbuf("gate", [P, GROUPS * P])
            z_gated = mem.sbuf("z_gated", [P, 2, P])

        xt_bank = mem.psum("xt_bank", [P, 512])
        qk_bank = mem.psum("qk_bank", [P, 512])
        v_bank = mem.psum("v_bank", [P, BG, NHG, HG * DH])
        score_bank = mem.psum("score_bank", [P, H, S])
        pt_bank = mem.psum("pt_bank", [P, NHG, P])
        z_bank = mem.psum("z_bank", [P, 512])
        zt_bank = mem.psum("zt_bank", [P, 512])
        o_bank = mem.psum("o_bank", [P, 512])

        (prepared, xn_done, xn_turned, xn_copied,
         qk_product, q_copied, k_copied, pool_blocks, dve_blocks, v_product, v_blocked, scored, bounded,
         maxed, shift_done, exped, p_turned, p_copied, pv_done, inverted, z_normed, z_turned, z_copied,
         gate_done, gated, o_product, x_biased, x_updated) = (mem.sem(k) for k in (
             "prepared", "xn_done",
             "xn_turned", "xn_copied", "qk_product", "q_copied", "k_copied", "pool_blocks", "dve_blocks",
             "v_product", "v_blocked", "scored", "bounded", "maxed", "shift_done", "exped", "p_turned",
             "p_copied", "pv_done", "inverted", "z_normed", "z_turned", "z_copied", "gate_done", "gated",
             "o_product", "x_biased", "x_updated"))
        PREPARED = 6 if windowed else 3
        y_done = mem.sem("y_done") if windowed else None
        residual = inner if windowed else x

        def key_block(engine, parity, b):
            return engine.tensor_tensor(
                k_blocks[parity][:, b, :, :],
                k_t[:, parity, b, :].rearrange("p (o k) -> p o k", o=1).broadcast_to([P, H, S]),
                const["head"].rearrange("p (h o) -> p h o", o=1).broadcast_to([P, H, S]), ALU.mult)

        block = stack.enter_context(nc.Block())

        @block.gpsimd
        def _(pool):
            clear_finished(nc, shared, mem)
            norm.rstd_on_gpsimd(pool, 0, shared["minus_half"], twice=windowed)
            for step in steps(pool, GROUPS, PEEL, DEEPEST, BODY):
                f, m = step.group(LAG_BLOCK), step.group(LAG_OUT)
                if m:
                    if windowed:
                        pool.wait_ge(y_done, m.n + 1)
                    if past(m.n - 1):
                        pool.wait_ge(x_updated, m.n - 1)
                    pool.wait_ge(prepared, PREPARED)
                    nc.gpsimd.tensor_tensor(x_bias[:, m.parity, :], residual[:, bass.ds(m.n * D, D)], bias,
                                            ALU.add).then_inc(x_biased, 1)
                if f:
                    pool.wait_ge(k_copied, f.n + 1)
                    if past(f.n - 1):
                        pool.wait_ge(scored, f.n - 1)
                    for b in range(KEY_BLOCKS_ON_POOL):
                        last = key_block(nc.gpsimd, f.parity, b)
                    last.then_inc(pool_blocks, 1)
                norm.next_rstd_on_gpsimd(pool, step, shared["minus_half"], twice=windowed)

        @block.tensor
        def _(pe):
            pe.wait_ge(prepared, PREPARED)
            for step in steps(pe, GROUPS, PEEL, DEEPEST, BODY):
                f, v, n, w, m = (step.group(k) for k in (LAG_QK, LAG_BLOCK, LAG_SCORE, LAG_VALUE, LAG_OUT))
                if f:
                    pe.wait_ge(xn_done, f.n + 1)
                    if past(f.n):
                        pe.wait_ge(xn_copied, f.n)
                    nc.tensor.transpose(xt_bank[:, 0:P], xn[:, f.parity, :], const["identity"]).then_inc(xn_turned, 1)
                if n:
                    pe.wait_ge(q_copied, n.n + 1)
                    pe.wait_ge(pool_blocks, n.n + 1)
                    pe.wait_ge(dve_blocks, n.n + 1)
                    if past(n.n):
                        pe.wait_ge(bounded, n.n)
                    for b in range(BG):
                        mm = nc.tensor.matmul(score_bank[b * S:(b + 1) * S, :, :].rearrange("p h k -> p (h k)"),
                                              q_t[:, n.parity, b, :],
                                              k_blocks[n.parity][:, b, :, :].rearrange("p h k -> p (h k)"),
                                              start=True, stop=True)
                    mm.then_inc(scored, 1)
                if m:
                    pe.wait_ge(z_normed, m.n + 1)
                    if past(m.n):
                        pe.wait_ge(z_copied, m.n)
                    nc.tensor.transpose(zt_bank[:, 0:P], z_rows[:, m.parity, :], const["identity"]).then_inc(z_turned, 1)
                if w:
                    pe.wait_ge(exped, w.n + 1)
                    if past(w.n):
                        pe.wait_ge(p_copied, w.n)
                    for g in range(NHG):
                        mm = nc.tensor.transpose(
                            pt_bank[:, g, :],
                            probs[:, w.parity, g * HG:(g + 1) * HG, :].rearrange("p h k -> p (h k)"),
                            const["identity"])
                    mm.then_inc(p_turned, 1)
                if v:
                    if past(v.n):
                        pe.wait_ge(v_blocked, v.n)
                    for b in range(BG):
                        mm = nc.tensor.matmul(v_bank[:, b, :, :].rearrange("p g d -> p (g d)"),
                                              xn_t[v.parity][:, b, :, :].rearrange("p r k -> p (r k)"), w_v,
                                              start=True, stop=True)
                    mm.then_inc(v_product, 1)
                if f:
                    pe.wait_ge(xn_copied, f.n + 1)
                    if past(f.n):
                        pe.wait_ge(gate_done if windowed else k_copied, f.n)
                    tokens = xn_t[f.parity][:, :, 0, :]
                    products = [w_q, w_k] + ([weight("wa_gate")] if windowed else [])
                    for i, w_i in enumerate(products):
                        mm = nc.tensor.matmul(qk_bank[:, i * P:(i + 1) * P].rearrange("p (b k) -> p b k", b=BG),
                                              w_i, tokens, start=True, stop=True)
                    mm.then_inc(qk_product, 1)
                if w:
                    pe.wait_ge(p_copied, w.n + 1)
                    pe.wait_ge(v_blocked, w.n + 1)
                    if past(w.n):
                        pe.wait_ge(z_normed, w.n)
                    for g in range(NHG):
                        for b in range(BG):
                            mm = nc.tensor.matmul(z_bank[b * S:(b + 1) * S, g * VW:(g + 1) * VW],
                                                  probs_t[:, w.parity, g, b * S:(b + 1) * S],
                                                  v_blocks[w.parity][:, b, g, :], start=True, stop=True)
                    mm.then_inc(pv_done, 1)
                if m:
                    pe.wait_ge(gated if windowed else z_copied, m.n + 1)
                    if past(m.n):
                        pe.wait_ge(x_updated, m.n)
                    nc.tensor.matmul(o_bank[:, 0:D], (z_gated if windowed else z_t)[:, m.parity, :], w_o,
                                     start=True, stop=True).then_inc(o_product, 1)

        @block.scalar
        def _(act):
            act.wait_ge(prepared, PREPARED)
            for step in steps(act, GROUPS, PEEL, DEEPEST, BODY):
                f, n, w, m = (step.group(k) for k in (LAG_QK, LAG_SCORE, LAG_VALUE, LAG_OUT))
                if n:
                    act.wait_ge(v_product, n.n + 1)
                    if past(n.n - 1):
                        act.wait_ge(pv_done, n.n - 1)
                    for h in range(HG):
                        last = nc.scalar.activation(v_blocks[n.parity][:, :, :, h * DH:(h + 1) * DH],
                                                    v_bank[:, :, :, h * DH:(h + 1) * DH], ACT.Copy,
                                                    scale=const["head_of_row"][:, h:h + 1])
                    last.then_inc(v_blocked, 1)
                if f:
                    act.wait_ge(xn_turned, f.n + 1)
                    if past(f.n - 1):
                        act.wait_ge(v_product, f.n - 1)
                    turned = xt_bank[:, 0:P].rearrange("p (b o k) -> p b o k", b=BG, o=1).broadcast_to([P, BG, HG, S])
                    if windowed:
                        last = nc.scalar.activation(xn_t[f.parity][:, :, :, :], turned, ACT.Identity,
                                                    bias=column("wa_b1"), scale=column("wa_g1"))
                    else:
                        last = nc.scalar.activation(xn_t[f.parity][:, :, :, :], turned, ACT.Copy)
                    last.then_inc(xn_copied, 1)
                if m:
                    act.wait_ge(z_turned, m.n + 1)
                    if past(m.n - 1):
                        act.wait_ge(gated if windowed else o_product, m.n - 1)
                    if windowed:
                        last = nc.scalar.activation(z_t[:, m.parity, :], zt_bank[:, 0:P], ACT.Identity,
                                                    bias=scaled[:, 2:3], scale=0.5)
                    else:
                        last = nc.scalar.activation(z_t[:, m.parity, :], zt_bank[:, 0:P], ACT.Identity, bias=b_v)
                    last.then_inc(z_copied, 1)
                if w:
                    act.wait_ge(p_turned, w.n + 1)
                    if past(w.n - 1):
                        act.wait_ge(pv_done, w.n - 1)
                    nc.scalar.activation(probs_t[:, w.parity, :, :], pt_bank[:, :, :], ACT.Copy).then_inc(p_copied, 1)
                if f:
                    act.wait_ge(qk_product, f.n + 1)
                    if past(f.n - 1):
                        act.wait_ge(dve_blocks, f.n - 1)
                        act.wait_ge(pool_blocks, f.n - 1)
                    nc.scalar.activation(k_t[:, f.parity, :, :], qk_bank[:, P:2 * P], ACT.Identity,
                                         bias=b_k).then_inc(k_copied, 1)
                    if past(f.n - 1):
                        act.wait_ge(scored, f.n - 1)
                    nc.scalar.activation(q_t[:, f.parity, :, :], qk_bank[:, 0:P], ACT.Identity,
                                         bias=scaled[:, 0:1], scale=QK_SCALE).then_inc(q_copied, 1)
                    if windowed:
                        act.wait_ge(prepared, PREPARED)
                        nc.scalar.activation(gate[:, bass.ds(f.n * P, P)], qk_bank[:, 2 * P:3 * P], ACT.Tanh,
                                             bias=scaled[:, 1:2], scale=0.5).then_inc(gate_done, 1)
                if n:
                    act.wait_ge(shift_done, n.n + 1)
                    if past(n.n - 1):
                        act.wait_ge(p_turned, n.n - 1)
                    nc.scalar.activation(probs[:, n.parity, :, :], shifted[:, n.parity, :, :],
                                         ACT.Exp).then_inc(exped, 1)

        @block.vector
        def _(dve):
            dve.wait_ge(shared["loaded"], shared["loaded_count"])
            dve.wait_ge(shared["params"], shared["params_count"])
            norm.fold_on_vector(dve)
            for i in range(2):
                nc.vector.tensor_copy(
                    v_blocks[i][:, :, :, HG * DH:VW],
                    const["head_of_row"].rearrange("p (a c h) -> p a c h", a=1, c=1).broadcast_to([P, BG, NHG, HG])
                ).then_inc(prepared, 1)
            nc.vector.tensor_scalar(scaled[:, 0:1], b_q, QK_SCALE, None, ALU.mult).then_inc(prepared, 1)
            if windowed:
                nc.vector.tensor_scalar(scaled[:, 1:2], column("wa_bgate"), 0.5, None, ALU.mult).then_inc(prepared, 1)
                nc.vector.tensor_scalar(scaled[:, 2:3], b_v, 0.5, None, ALU.mult).then_inc(prepared, 1)
                nc.vector.tensor_tensor(
                    distance_bias[:, :, :], distance_bias[:, :, :],
                    const["causal_sum"].rearrange("p (o k) -> p o k", o=1).broadcast_to([P, H, S]),
                    ALU.add).then_inc(prepared, 1)
                dve.wait_ge(prepared, PREPARED)
            for step in steps(dve, GROUPS, PEEL, DEEPEST, BODY):
                g, v, n, w, m, s = (step.group(k) for k in (
                    LAG_LN, LAG_BLOCK, LAG_SCORE, LAG_VALUE, LAG_OUT, LAG_STATS))
                if v:
                    dve.wait_ge(k_copied, v.n + 1)
                    if past(v.n - 1):
                        dve.wait_ge(scored, v.n - 1)
                    for b in range(KEY_BLOCKS_ON_POOL, BG):
                        last = key_block(nc.vector, v.parity, b)
                    last.then_inc(dve_blocks, 1)
                if n:
                    dve.wait_ge(scored, n.n + 1)
                    if past(n.n - 1):
                        dve.wait_ge(exped, n.n - 1)
                    if windowed:
                        last = nc.vector.tensor_tensor(shifted[:, n.parity, :, :], score_bank[:, :, :],
                                                       distance_bias[:, :, :], ALU.add)
                    else:
                        last = nc.vector.tensor_tensor(
                            shifted[:, n.parity, :, :], score_bank[:, :, :],
                            const["causal_bound"].rearrange("p (o k) -> p o k", o=1).broadcast_to([P, H, S]),
                            ALU.min)
                    last.then_inc(bounded, 1)
                if g:
                    if past(g.n - 1):
                        dve.wait_ge(xn_turned, g.n - 1)
                    norm.rows_on_vector(dve, xn[:, g.parity, :], x, g.n, PEEL - 1, twice=windowed).then_inc(xn_done, 1)
                if n:
                    dve.wait_ge(bounded, n.n + 1)
                    nc.vector.tensor_reduce(maxima[:, n.parity, :], shifted[:, n.parity, :, :], AXIS_X,
                                            ALU.max).then_inc(maxed, 1)
                if windowed and m:
                    dve.wait_ge(z_copied, m.n + 1)
                    if past(m.n - 1):
                        dve.wait_ge(o_product, m.n - 1)
                    nc.vector.scalar_tensor_tensor(out=z_gated[:, m.parity, :], in0=gate[:, bass.ds(m.n * P, P)],
                                                   scalar=1.0, in1=z_t[:, m.parity, :], op0=ALU.add,
                                                   op1=ALU.mult).then_inc(gated, 1)
                if n:
                    dve.wait_ge(maxed, n.n + 1)
                    nc.vector.tensor_tensor(
                        shifted[:, n.parity, :, :], shifted[:, n.parity, :, :],
                        maxima[:, n.parity, :].rearrange("p (h o) -> p h o", o=1).broadcast_to([P, H, S]),
                        ALU.subtract).then_inc(shift_done, 1)
                if w:
                    z_of = z_bank[:, 0:NHG * VW].rearrange("p (g c) -> p g c", g=NHG)
                    dve.wait_ge(pv_done, w.n + 1)
                    nc.vector.reciprocal(inv_den[:, w.parity, :, :], z_of[:, :, HG * DH:VW]).then_inc(inverted, 1)
                if s:
                    dve.wait_ge(x_updated, s.n + 1)
                    norm.stats_on_vector(residual, s.n)
                if w:
                    dve.wait_ge(inverted, w.n + 1)
                    if past(w.n - 1):
                        dve.wait_ge(z_turned, w.n - 1)
                    nc.vector.tensor_tensor(
                        z_rows[:, w.parity, :].rearrange("p (g h d) -> p g h d", g=NHG, h=HG),
                        z_of[:, :, 0:HG * DH].rearrange("p g (h d) -> p g h d", h=HG),
                        inv_den[:, w.parity, :, :].rearrange("p g (h o) -> p g h o", o=1).broadcast_to([P, NHG, HG, DH]),
                        ALU.mult).then_inc(z_normed, 1)
                if m:
                    dve.wait_ge(o_product, m.n + 1)
                    dve.wait_ge(x_biased, m.n + 1)
                    nc.vector.tensor_tensor(residual[:, bass.ds(m.n * D, D)], o_bank[:, 0:D], x_bias[:, m.parity, :],
                                            ALU.add).then_inc(x_updated, 1)
                if g and windowed:
                    norm.rows_on_vector(dve, inner[:, bass.ds(g.n * D, D)], x, g.n, PEEL - 1).then_inc(y_done, 1)


def channel_mix(nc, shared, context):
    with ExitStack() as stack:
        mem = Memory(nc, stack, "cm")
        LAG_LN, LAG_TURN, LAG_MIX, LAG_OUT, LAG_STATS = 0, 1, 2, 3, 4
        PEEL, DEEPEST, BODY = 8, 4, 4
        x, const, weight, column = (shared[k] for k in ("x", "const", "weight", "column"))
        norm = shared["norm"]
        xn = mem.sbuf("xn", [P, 2, D])
        xn_done = mem.sem("xn_done")
        now_t = mem.sbuf("now_t", [P, 2, BG, S])
        before_t = mem.sbuf("before_t", [P, 2, BG, S])
        weights = mem.sbuf("weights", [P, 4, D])
        half_v = mem.sbuf("half_v", [P, D])
        gate = mem.sbuf("gate", [P, 2, D])
        relu_t = mem.sbuf("relu_t", [P, 2, P])
        key_t = mem.sbuf("key_t", [P, 2, P])
        mixed = mem.sbuf("mixed", [P, 2, D])
        xt_bank, r_bank, k_bank, v_bank = (mem.psum(k, [P, 512]) for k in ("xt_bank", "r_bank", "k_bank", "v_bank"))
        (made, turned, now_copied, before_copied, r_product, k_product, gate_done, relu_done, key_done, v_product,
         mixed_done, x_updated) = (mem.sem(k) for k in (
             "made", "turned", "now_copied", "before_copied", "r_product", "k_product", "gate_done",
             "relu_done", "key_done", "v_product", "mixed_done", "x_updated"))
        MADE = 8
        block = stack.enter_context(nc.Block())

        @block.sync
        def _(sp):
            context.load_first(sp)

        @block.gpsimd
        def _(pool):
            clear_finished(nc, shared, mem)
            pool.wait_ge(made, MADE)
            norm.rstd_on_gpsimd(pool, 0, shared["minus_half"])
            for step in steps(pool, GROUPS, PEEL, DEEPEST, BODY):
                g, f = step.group(LAG_LN), step.group(LAG_TURN)
                if f:
                    copies, products = in_register(pool, f.n + 1), in_register(pool, f.n - 1)
                    pool.wait_ge(made, MADE)
                    pool.wait_ge(now_copied, copies)
                    if past(products):
                        pool.wait_ge(k_product, products)
                    nc.gpsimd.tensor_copy(before_t[:, f.parity, :, 1:S],
                                          now_t[:, f.parity, :, 0:S - 1]).then_inc(before_copied, 1)
                norm.next_rstd_on_gpsimd(pool, step, shared["minus_half"])

        @block.tensor
        def _(pe):
            pe.wait_ge(made, MADE)
            for step in steps(pe, GROUPS, PEEL, DEEPEST, BODY):
                f, n, m = (step.group(k) for k in (LAG_TURN, LAG_MIX, LAG_OUT))
                if f:
                    pe.wait_ge(xn_done, f.n + 1)
                    if past(f.n):
                        pe.wait_ge(now_copied, f.n)
                    nc.tensor.transpose(xt_bank[:, 0:P], xn[:, f.parity, :], const["identity"]).then_inc(turned, 1)
                if n:
                    now = now_t[:, n.parity, :, :].rearrange("p b s -> p (b s)")
                    before = before_t[:, n.parity, :, :].rearrange("p b s -> p (b s)")
                    pe.wait_ge(before_copied, n.n + 1)
                    if past(n.n):
                        pe.wait_ge(gate_done, n.n)
                    nc.tensor.matmul(r_bank[:, 0:D], now, weights[:, 0, :], start=True, stop=False)
                    nc.tensor.matmul(r_bank[:, 0:D], before, weights[:, 1, :], start=False, stop=True).then_inc(r_product, 1)
                    if past(n.n):
                        pe.wait_ge(relu_done, n.n)
                    nc.tensor.matmul(k_bank[:, 0:P], weights[:, 2, :], now, start=True, stop=False)
                    nc.tensor.matmul(k_bank[:, 0:P], weights[:, 3, :], before, start=False, stop=True).then_inc(k_product, 1)
                if m:
                    pe.wait_ge(key_done, m.n + 1)
                    if past(m.n):
                        pe.wait_ge(mixed_done, m.n)
                    nc.tensor.matmul(v_bank[:, 0:D], key_t[:, m.parity, :], half_v[:, :], start=True,
                                     stop=True).then_inc(v_product, 1)

        @block.scalar
        def _(act):
            act.wait_ge(made, MADE)
            for step in steps(act, GROUPS, PEEL, DEEPEST, BODY):
                f, n = step.group(LAG_TURN), step.group(LAG_MIX)
                if f:
                    act.wait_ge(turned, f.n + 1)
                    if past(f.n - 1):
                        act.wait_ge(k_product, f.n - 1)
                    nc.scalar.activation(now_t[:, f.parity, :, :], xt_bank[:, 0:P], ACT.Copy).then_inc(now_copied, 1)
                if n:
                    act.wait_ge(r_product, n.n + 1)
                    if past(n.n - 1):
                        act.wait_ge(mixed_done, n.n - 1)
                    nc.scalar.activation(gate[:, n.parity, :], r_bank[:, 0:D], ACT.Tanh, scale=0.5).then_inc(gate_done, 1)
                    act.wait_ge(k_product, n.n + 1)
                    if past(n.n - 1):
                        act.wait_ge(key_done, n.n - 1)
                    nc.scalar.activation(relu_t[:, n.parity, :], k_bank[:, 0:P], ACT.Relu).then_inc(relu_done, 1)

        @block.vector
        def _(dve):
            dve.wait_ge(shared["loaded"], shared["loaded_count"])
            dve.wait_ge(shared["params"], shared["params_count"])
            norm.fold_on_vector(dve)
            for i, (w, mu) in enumerate((("cm_r", "cm_mu_r"), ("cm_k", "cm_mu_k"))):
                nc.vector.tensor_scalar(weights[:, 2 * i, :], weight(w), column(mu), None, ALU.mult).then_inc(made, 1)
                dve.wait_ge(made, 3 * i + 1)
                nc.vector.tensor_scalar(weights[:, 2 * i + 1, :], weight(w), column(mu), None, ALU.mult).then_inc(made, 1)
                dve.wait_ge(made, 3 * i + 2)
                nc.vector.tensor_tensor(weights[:, 2 * i + 1, :], weight(w), weights[:, 2 * i + 1, :],
                                        ALU.subtract).then_inc(made, 1)
            nc.vector.tensor_scalar(half_v[:, :], weight("cm_v"), 0.5, None, ALU.mult).then_inc(made, 1)
            nc.vector.memset(before_t[:, :, :, 0:1], 0.0).then_inc(made, 1)
            for step in steps(dve, GROUPS, PEEL, DEEPEST, BODY):
                g, n, m = (step.group(k) for k in (LAG_LN, LAG_MIX, LAG_OUT))
                s = step.group(LAG_STATS)
                if g:
                    if past(g.n - 1):
                        dve.wait_ge(turned, g.n - 1)
                    norm.rows_on_vector(dve, xn[:, g.parity, :], x, g.n, PEEL - 1).then_inc(xn_done, 1)
                if s:
                    dve.wait_ge(x_updated, s.n + 1)
                    norm.stats_on_vector(x, s.n)
                if n:
                    dve.wait_ge(relu_done, n.n + 1)
                    if past(n.n - 1):
                        dve.wait_ge(v_product, n.n - 1)
                    nc.vector.tensor_tensor(key_t[:, n.parity, :], relu_t[:, n.parity, :], relu_t[:, n.parity, :],
                                            ALU.mult).then_inc(key_done, 1)
                if m:
                    dve.wait_ge(v_product, m.n + 1)
                    dve.wait_ge(gate_done, m.n + 1)
                    nc.vector.scalar_tensor_tensor(out=mixed[:, m.parity, :], in0=gate[:, m.parity, :], scalar=1.0,
                                                   in1=v_bank[:, 0:D], op0=ALU.add, op1=ALU.mult).then_inc(mixed_done, 1)
                    dve.wait_ge(mixed_done, m.n + 1)
                    nc.vector.tensor_tensor(x[:, bass.ds(m.n * D, D)], x[:, bass.ds(m.n * D, D)],
                                            mixed[:, m.parity, :], ALU.add).then_inc(x_updated, 1)


class Context:
    RING = 6

    def __init__(self, mem, ctx_t, ctx_rows, ctx_last):
        self.ctx_t, self.ctx_rows, self.ctx_last = ctx_t, ctx_rows, ctx_last
        self.keys_t = [mem.sbuf(f"keys_t{i}", [P, BG * KEYS]) for i in range(self.RING)]
        self.keys = [mem.sbuf(f"keys{i}", [P, BG, CHUNKS, D]) for i in range(self.RING)]
        self.last_key = mem.sbuf("last_key", [P, GROUPS, D])
        self.keys_t_loaded = [mem.sem(f"keys_t_loaded{i}") for i in range(self.RING)]
        self.keys_loaded = [mem.sem(f"keys_loaded{i}") for i in range(self.RING)]
        self.last_loaded = mem.sem("last_loaded")

    def load_keys_t(self, sp, n, i):
        sp.dma_start(self.keys_t[i][:, :], self.ctx_t[:, bass.ds(n * BG * KEYS, BG * KEYS)]).then_inc(
            self.keys_t_loaded[i], 16)

    def load_keys(self, sp, n, i):
        sp.dma_start(self.keys[i][:, :, :, :].rearrange("p b c d -> p (b c d)"),
                     self.ctx_rows[:, bass.ds(n * BG * CHUNKS * D, BG * CHUNKS * D)]).then_inc(
            self.keys_loaded[i], 16)

    def load_first(self, sp):
        for n in range(self.RING):
            self.load_keys_t(sp, n, n)
            self.load_keys(sp, n, n)
        rows_of = self.ctx_last.rearrange("(n b) d -> b n d", b=BG)
        for b in range(BG):
            sp.dma_start(self.last_key[b * S:(b + 1) * S, :, :],
                         rows_of[b:b + 1, :, :].broadcast_to([S, GROUPS, D])).then_inc(self.last_loaded, 16)


def similarity_attention(nc, shared, context):
    with ExitStack() as stack:
        mem = Memory(nc, stack, "bi")
        LAG_LN, LAG_TURN, LAG_SIM, LAG_NORM, LAG_MIX, LAG_FEATURE, LAG_OUT, LAG_STATS = range(8)
        PEEL, DEEPEST, BODY = 8, 7, 6
        RING, KEY_RING = 3, context.RING
        KCOLS = BG * KEYS
        x, const, weight, column, row = (shared[k] for k in ("x", "const", "weight", "column", "row"))
        norm = shared["norm"]
        xn = mem.sbuf("xn", [P, BODY, D])
        xn_done = mem.sem("xn_done")
        keys_t, keys, last_key = context.keys_t, context.keys, context.last_key
        keys_t_loaded, keys_loaded, last_loaded = context.keys_t_loaded, context.keys_loaded, context.last_loaded
        x_t = mem.sbuf("x_t", [P, BODY, P])
        sim_rows = mem.sbuf("sim_rows", [P, 2, P])
        negated = mem.sbuf("negated", [P, 2])
        x_w1 = mem.sbuf("x_w1", [P, 2, D])
        x_part = mem.sbuf("x_part", [P, BODY])
        neg_max = mem.sbuf("neg_max", [P, 2])
        row_max = mem.sbuf("row_max", [P, BODY])
        probs = mem.sbuf("probs", [P, RING, KEYS])
        den = mem.sbuf("den", [P, RING])
        inv_den = mem.sbuf("inv_den", [P, RING])
        probs_t = mem.sbuf("probs_t", [P, 2, CHUNKS, P])
        maxima = mem.sbuf("maxima", [P, 2, P])
        neg_top = mem.sbuf("neg_top", [P, 2, 2])
        token_exp = mem.sbuf("token_exp", [P, 2, P])
        token_sum = mem.sbuf("token_sum", [P, 2, 2])
        own_exp = mem.sbuf("own_exp", [P, 2, 2])
        token_weights = mem.sbuf("token_weights", [P, 2, P])
        mix_rows = mem.sbuf("mix_rows", [P, 2, D])
        last_part = mem.sbuf("last_part", [P, 2, D])
        mix_t = mem.sbuf("mix_t", [P, 2, P])
        x_mix_t = mem.sbuf("x_mix_t", [P, 2, P])
        x_mean_t = mem.sbuf("x_mean_t", [P, 2, P])
        x_bias = mem.sbuf("x_bias", [P, 2, D])
        (xt_bank, sim_bank, pt_bank, max_bank, mix_bank, mixt_bank, mean_bank, o_bank) = (
            mem.psum(k, [P, 512]) for k in ("xt_bank", "sim_bank", "pt_bank", "max_bank", "mix_bank",
                                            "mixt_bank", "mean_bank", "o_bank"))
        (made, turned, x_copied, sim_rows_done, x_part_done, sim_done, min_done, exped,
         inverted, normed, row_max_done, p_turned, p_copied, max_spread, top_done, top_negated, token_exped,
         own_exped, sum_inverted, weight_scaled, weights_done, last_part_done, mix_product, mix_done,
         mix_turned, mix_copied, mean_product, x_mixed, x_meaned, o_product, x_biased, x_updated) = (
             mem.sem(k) for k in (
                 "made", "turned", "x_copied", "sim_rows_done", "x_part_done", "sim_done",
                 "min_done", "exped", "inverted", "normed", "row_max_done", "p_turned", "p_copied",
                 "max_spread", "top_done", "top_negated", "token_exped", "own_exped", "sum_inverted",
                 "weight_scaled", "weights_done", "last_part_done", "mix_product", "mix_done", "mix_turned",
                 "mix_copied", "mean_product", "x_mixed", "x_meaned", "o_product", "x_biased", "x_updated"))
        MADE = 2

        def past_loads(g):
            return (g.lap * (BODY // KEY_RING) + (g.slot // KEY_RING + 1)) * 16

        block = stack.enter_context(nc.Block())

        @block.sync
        def _(sp):
            def load(n, i):
                sp.wait_ge(sim_done, n - (KEY_RING - 1))
                context.load_keys_t(sp, n, i)
                sp.wait_ge(mix_product, n - (KEY_RING - 1))
                context.load_keys(sp, n, i)

            first = KEY_RING + (GROUPS - KEY_RING) % KEY_RING
            for n in range(KEY_RING, first):
                load(n, n % KEY_RING)
            with sp.Fori(0, (GROUPS - first) // KEY_RING) as j:
                for i in range(KEY_RING):
                    load(j * KEY_RING + (first + i), (first + i) % KEY_RING)

        @block.gpsimd
        def _(pool):
            clear_finished(nc, shared, mem)
            pool.wait_ge(made, MADE)
            pool.wait_ge(last_loaded, 16 * BG)
            norm.rstd_on_gpsimd(pool, 0, shared["minus_half"])
            for step in steps(pool, GROUPS, PEEL, DEEPEST, BODY):
                g, m = step.group(LAG_LN), step.group(LAG_OUT)
                if m:
                    if past(m.n - 1):
                        pool.wait_ge(x_updated, m.n - 1)
                    pool.wait_ge(made, MADE)
                    nc.gpsimd.tensor_tensor(x_bias[:, m.parity, :], x[:, bass.ds(m.n * D, D)], row("bi_bqv"),
                                            ALU.add).then_inc(x_biased, 1)
                norm.next_rstd_on_gpsimd(pool, step, shared["minus_half"])

        @block.tensor
        def _(pe):
            pe.wait_ge(made, MADE)
            for step in steps(pe, GROUPS, PEEL, DEEPEST, BODY):
                f, n, e, w, v, m = (step.group(k) for k in (LAG_TURN, LAG_SIM, LAG_NORM, LAG_MIX, LAG_FEATURE, LAG_OUT))
                if f:
                    pe.wait_ge(xn_done, f.n + 1)
                    if past(f.n):
                        pe.wait_ge(sim_rows_done, f.n)
                    nc.tensor.transpose(xt_bank[:, 0:P], xn[:, f.slot, :], const["identity"]).then_inc(turned, 1)
                if n:
                    pe.wait_ge(sim_rows_done, n.n + 1)
                    pe.wait_ge(keys_t_loaded[n.slot % KEY_RING], past_loads(n))
                    if past(n.n):
                        pe.wait_ge(exped, n.n)
                    for b in range(BG):
                        mm = nc.tensor.matmul(sim_bank[b * S:(b + 1) * S, 0:KEYS],
                                              sim_rows[:, n.parity, b * S:(b + 1) * S],
                                              keys_t[n.slot % KEY_RING][:, b * KEYS:(b + 1) * KEYS], start=True, stop=True)
                    mm.then_inc(sim_done, 1)
                if e:
                    pe.wait_ge(row_max_done, e.n + 1)
                    if past(e.n):
                        pe.wait_ge(top_done, e.n)
                    nc.tensor.matmul(max_bank[:, 0:P], row_max[:, e.slot:e.slot + 1].broadcast_to([P, P]),
                                     const["identity"], start=True, stop=True).then_inc(max_spread, 1)
                if w:
                    pe.wait_ge(normed, w.n + 1)
                    if past(w.n):
                        pe.wait_ge(p_copied, w.n)
                    for c in range(CHUNKS):
                        mm = nc.tensor.transpose(pt_bank[:, c * P:(c + 1) * P],
                                                 probs[:, w.slot % RING, c * P:(c + 1) * P], const["identity"])
                    mm.then_inc(p_turned, 1)
                if v:
                    pe.wait_ge(mix_done, v.n + 1)
                    if past(v.n):
                        pe.wait_ge(mix_copied, v.n)
                    nc.tensor.transpose(mixt_bank[:, 0:P], mix_rows[:, v.parity, :], const["identity"]).then_inc(mix_turned, 1)
                    pe.wait_ge(weights_done, v.n + 1)
                    if past(v.n):
                        pe.wait_ge(x_meaned, v.n)
                    nc.tensor.matmul(mean_bank[:, 0:P], xn[:, v.slot, :], token_weights[:, v.parity, :],
                                     start=True, stop=True).then_inc(mean_product, 1)
                if m:
                    pe.wait_ge(x_mixed, m.n + 1)
                    pe.wait_ge(x_meaned, m.n + 1)
                    if past(m.n):
                        pe.wait_ge(x_updated, m.n)
                    features = (x_t[:, m.slot, :], mix_t[:, m.parity, :], x_mix_t[:, m.parity, :],
                                x_mean_t[:, m.parity, :])
                    for i, feature in enumerate(features):
                        mm = nc.tensor.matmul(o_bank[:, 0:D], feature, weight("bi_qv", i), start=(i == 0),
                                              stop=(i == 3))
                    mm.then_inc(o_product, 1)
                if w:
                    pe.wait_ge(p_copied, w.n + 1)
                    pe.wait_ge(keys_loaded[w.slot % KEY_RING], past_loads(w))
                    if past(w.n):
                        pe.wait_ge(mix_done, w.n)
                    for c in range(CHUNKS):
                        for b in range(BG):
                            mm = nc.tensor.matmul(mix_bank[b * S:(b + 1) * S, 0:D],
                                                  probs_t[:, w.parity, c, b * S:(b + 1) * S],
                                                  keys[w.slot % KEY_RING][:, b, c, :], start=(c == 0),
                                                  stop=(c == CHUNKS - 1), skip_group_check=True)
                    mm.then_inc(mix_product, 1)

        @block.scalar
        def _(act):
            act.wait_ge(made, MADE)
            for step in steps(act, GROUPS, PEEL, DEEPEST, BODY):
                f, n, e, w, v = (step.group(k) for k in (LAG_TURN, LAG_SIM, LAG_NORM, LAG_MIX, LAG_FEATURE))
                if f:
                    act.wait_ge(turned, f.n + 1)
                    if past(f.n - 5):
                        act.wait_ge(o_product, f.n - 5)
                        act.wait_ge(x_meaned, f.n - 5)
                    nc.scalar.activation(x_t[:, f.slot, :], xt_bank[:, 0:P], ACT.Copy).then_inc(x_copied, 1)
                    if past(f.n - 1):
                        act.wait_ge(sim_done, f.n - 1)
                    nc.scalar.activation(sim_rows[:, f.parity, :], xt_bank[:, 0:P], ACT.Identity,
                                         bias=negated[:, 0:1], scale=negated[:, 1:2]).then_inc(sim_rows_done, 1)
                if w:
                    act.wait_ge(p_turned, w.n + 1)
                    if past(w.n - 1):
                        act.wait_ge(mix_product, w.n - 1)
                    nc.scalar.activation(probs_t[:, w.parity, :, :].rearrange("p c k -> p (c k)"),
                                         pt_bank[:, 0:CHUNKS * P], ACT.Copy).then_inc(p_copied, 1)
                if n:
                    act.wait_ge(min_done, n.n + 1)
                    if past(n.n - 2):
                        act.wait_ge(p_turned, n.n - 2)
                        act.wait_ge(last_part_done, n.n - 2)
                    k = n.slot % RING
                    nc.scalar.activation(probs[:, k, :], sim_bank[:, 0:KEYS], ACT.Exp,
                                         bias=neg_max[:, n.parity:n.parity + 1], scale=-1.0,
                                         accum_out=den[:, k:k + 1]).then_inc(exped, 1)
                if v:
                    act.wait_ge(mix_turned, v.n + 1)
                    if past(v.n - 1):
                        act.wait_ge(o_product, v.n - 1)
                    nc.scalar.activation(mix_t[:, v.parity, :], mixt_bank[:, 0:P], ACT.Copy).then_inc(mix_copied, 1)
                if e:
                    act.wait_ge(top_negated, e.n + 1)
                    if past(e.n - 1):
                        act.wait_ge(weight_scaled, e.n - 1)
                    nc.scalar.activation(token_exp[:, e.parity, :], maxima[:, e.parity, :], ACT.Exp,
                                         bias=neg_top[:, e.parity, 1:2],
                                         accum_out=token_sum[:, e.parity, 0:1]).then_inc(token_exped, 1)
                    nc.scalar.activation(own_exp[:, e.parity, 0:1], row_max[:, e.slot:e.slot + 1], ACT.Exp,
                                         bias=neg_top[:, e.parity, 1:2]).then_inc(own_exped, 1)

        @block.vector
        def _(dve):
            dve.wait_ge(shared["loaded"], shared["loaded_count"])
            dve.wait_ge(shared["params"], shared["params_count"])
            norm.fold_on_vector(dve)
            nc.vector.tensor_scalar(negated[:, 0:1], column("bi_w2"), -1.0, None, ALU.mult).then_inc(made, 1)
            nc.vector.tensor_scalar(negated[:, 1:2], column("bi_w3"), -1.0, None, ALU.mult).then_inc(made, 1)
            dve.wait_ge(last_loaded, 16 * BG)
            for step in steps(dve, GROUPS, PEEL, DEEPEST, BODY):
                g, f, n, e, w, v, m, s = (step.group(k) for k in (
                    LAG_LN, LAG_TURN, LAG_SIM, LAG_NORM, LAG_MIX, LAG_FEATURE, LAG_OUT, LAG_STATS))
                if g:
                    if past(g.n - 5):
                        dve.wait_ge(mean_product, g.n - 5)
                    norm.rows_on_vector(dve, xn[:, g.slot, :], x, g.n, PEEL - 1).then_inc(xn_done, 1)
                if s:
                    dve.wait_ge(x_updated, s.n + 1)
                    norm.stats_on_vector(x, s.n)
                if e:
                    k = e.slot % RING
                    dve.wait_ge(exped, e.n + 1)
                    nc.vector.reciprocal(inv_den[:, k:k + 1], den[:, k:k + 1]).then_inc(inverted, 1)
                if w:
                    k = w.parity
                    dve.wait_ge(token_exped, w.n + 1)
                    nc.vector.reciprocal(token_sum[:, k, 1:2], token_sum[:, k, 0:1]).then_inc(sum_inverted, 1)
                if e:
                    k = e.slot % RING
                    dve.wait_ge(inverted, e.n + 1)
                    nc.vector.tensor_scalar(probs[:, k, :], probs[:, k, :], inv_den[:, k:k + 1], None,
                                            ALU.mult).then_inc(normed, 1)
                if w:
                    k = w.parity
                    dve.wait_ge(own_exped, w.n + 1)
                    dve.wait_ge(sum_inverted, w.n + 1)
                    nc.vector.tensor_tensor(own_exp[:, k, 1:2], own_exp[:, k, 0:1], token_sum[:, k, 1:2],
                                            ALU.mult).then_inc(weight_scaled, 1)
                if e:
                    k = e.parity
                    spreads, exps = in_register(dve, e.n + 1), in_register(dve, e.n - 1)
                    dve.wait_ge(made, MADE)
                    dve.wait_ge(max_spread, spreads)
                    if past(exps):
                        dve.wait_ge(token_exped, exps)
                    nc.vector.tensor_tensor_reduce(maxima[:, k, :], max_bank[:, 0:P], const["other_sequence"],
                                                   1.0, -BIG, ALU.add, ALU.max, neg_top[:, k, 0:1]).then_inc(top_done, 1)
                if w:
                    k = w.parity
                    dve.wait_ge(weight_scaled, w.n + 1)
                    if past(w.n - 1):
                        dve.wait_ge(mean_product, w.n - 1)
                    nc.vector.tensor_scalar(token_weights[:, k, :], const["same_sequence"], own_exp[:, k, 1:2], None,
                                            ALU.mult).then_inc(weights_done, 1)
                if e:
                    k = e.parity
                    dve.wait_ge(top_done, e.n + 1)
                    if past(e.n - 1):
                        dve.wait_ge(own_exped, e.n - 1)
                    nc.vector.tensor_scalar(neg_top[:, k, 1:2], neg_top[:, k, 0:1], -1.0, None,
                                            ALU.mult).then_inc(top_negated, 1)
                if n:
                    k = n.parity
                    dve.wait_ge(sim_done, n.n + 1)
                    if past(n.n - 1):
                        dve.wait_ge(exped, n.n - 1)
                    nc.vector.tensor_reduce(neg_max[:, k:k + 1], sim_bank[:, 0:KEYS], AXIS_X, ALU.min).then_inc(min_done, 1)
                if e:
                    dve.wait_ge(normed, e.n + 1)
                    if past(e.n - 1):
                        dve.wait_ge(mix_done, e.n - 1)
                    nc.vector.tensor_scalar(last_part[:, e.parity, :],
                                            last_key[:, bass.ds(e.n, 1), :].rearrange("p n d -> p (n d)"),
                                            probs[:, e.slot % RING, LAST:KEYS], None, ALU.mult).then_inc(last_part_done, 1)
                if f:
                    k = f.slot
                    dve.wait_ge(xn_done, f.n + 1)
                    if past(f.n - 5):
                        dve.wait_ge(row_max_done, f.n - 5)
                    nc.vector.tensor_tensor_reduce(x_w1[:, f.parity, :], xn[:, k, :], row("bi_w1"), 1.0,
                                                   row("bi_b"), ALU.mult, ALU.add,
                                                   x_part[:, k:k + 1]).then_inc(x_part_done, 1)
                if n:
                    dve.wait_ge(min_done, n.n + 1)
                    dve.wait_ge(x_part_done, n.n + 1)
                    if past(n.n - 5):
                        dve.wait_ge(max_spread, n.n - 5)
                        dve.wait_ge(own_exped, n.n - 5)
                    nc.vector.tensor_tensor(row_max[:, n.slot:n.slot + 1], x_part[:, n.slot:n.slot + 1],
                                            neg_max[:, n.parity:n.parity + 1], ALU.subtract).then_inc(row_max_done, 1)
                if m:
                    dve.wait_ge(o_product, m.n + 1)
                    dve.wait_ge(x_biased, m.n + 1)
                    nc.vector.tensor_tensor(x[:, bass.ds(m.n * D, D)], o_bank[:, 0:D], x_bias[:, m.parity, :],
                                            ALU.add).then_inc(x_updated, 1)
                if v:
                    k = v.parity
                    dve.wait_ge(mean_product, v.n + 1)
                    if past(v.n - 1):
                        dve.wait_ge(o_product, v.n - 1)
                    nc.vector.tensor_tensor(x_mean_t[:, k, :], mean_bank[:, 0:P], x_t[:, v.slot, :],
                                            ALU.mult).then_inc(x_meaned, 1)
                    dve.wait_ge(mix_copied, v.n + 1)
                    nc.vector.tensor_tensor(x_mix_t[:, k, :], x_t[:, v.slot, :], mix_t[:, k, :],
                                            ALU.mult).then_inc(x_mixed, 1)
                if w:
                    k = w.parity
                    dve.wait_ge(mix_product, w.n + 1)
                    dve.wait_ge(last_part_done, w.n + 1)
                    if past(w.n - 1):
                        dve.wait_ge(mix_turned, w.n - 1)
                    nc.vector.tensor_tensor(mix_rows[:, k, :], mix_bank[:, 0:D], last_part[:, k, :],
                                            ALU.add).then_inc(mix_done, 1)


def gelu_block(nc, shared, inner):
    with ExitStack() as stack:
        mem = Memory(nc, stack, "gelu")
        LAG_LN, LAG_TURN, LAG_UP, LAG_DOWN, LAG_STATS = 0, 1, 2, 3, 4
        PEEL, DEEPEST, BODY = 8, 4, 4
        PARTS = FF // P
        x, const, weight, column, row = (shared[k] for k in ("x", "const", "weight", "column", "row"))
        norm = shared["norm"]
        xn = mem.sbuf("xn", [P, 2, D])
        xn_done = mem.sem("xn_done")
        x_t = mem.sbuf("x_t", [P, 2, P])
        hidden = mem.sbuf("hidden", [P, 2, PARTS, P])
        x_inner = mem.sbuf("x_inner", [P, 2, D])
        x_summed = mem.sem("x_summed")
        x_bias = mem.sbuf("x_bias", [P, 2, D])
        xt_bank, o_bank = (mem.psum(k, [P, 512]) for k in ("xt_bank", "o_bank"))
        up_bank = [mem.psum(f"up_bank{i}", [P, PARTS, P]) for i in range(2)]
        (made, turned, x_copied, up_product, hidden_done, o_product, x_biased, x_updated) = (
            mem.sem(k) for k in ("made", "turned", "x_copied", "up_product", "hidden_done", "o_product",
                                 "x_biased", "x_updated"))
        block = stack.enter_context(nc.Block())

        @block.gpsimd
        def _(pool):
            clear_finished(nc, shared, mem)
            pool.wait_ge(made, 1)
            norm.rstd_on_gpsimd(pool, 0, shared["minus_half"])
            for step in steps(pool, GROUPS, PEEL, DEEPEST, BODY):
                g, m = step.group(LAG_LN), step.group(LAG_DOWN)
                if m:
                    if past(m.n - 1):
                        pool.wait_ge(x_updated, m.n - 1)
                    pool.wait_ge(made, 1)
                    nc.gpsimd.tensor_tensor(x_inner[:, m.parity, :], x[:, bass.ds(m.n * D, D)],
                                            inner[:, bass.ds(m.n * D, D)], ALU.add).then_inc(x_summed, 1)
                    pool.wait_ge(x_summed, m.n + 1)
                    pool.wait_ge(made, 1)
                    nc.gpsimd.tensor_tensor(x_bias[:, m.parity, :], x_inner[:, m.parity, :], row("wa_bfc2"),
                                            ALU.add).then_inc(x_biased, 1)
                norm.next_rstd_on_gpsimd(pool, step, shared["minus_half"])

        @block.tensor
        def _(pe):
            pe.wait_ge(made, 1)
            for step in steps(pe, GROUPS, PEEL, DEEPEST, BODY):
                f, n, m = (step.group(k) for k in (LAG_TURN, LAG_UP, LAG_DOWN))
                if f:
                    pe.wait_ge(xn_done, f.n + 1)
                    if past(f.n):
                        pe.wait_ge(x_copied, f.n)
                    nc.tensor.transpose(xt_bank[:, 0:P], xn[:, f.parity, :], const["identity"]).then_inc(turned, 1)
                if n:
                    pe.wait_ge(x_copied, n.n + 1)
                    if past(n.n - 1):
                        pe.wait_ge(hidden_done, n.n - 1)
                    for c in range(PARTS):
                        mm = nc.tensor.matmul(up_bank[n.parity][:, c, :], weight("wa_fc1", c), x_t[:, n.parity, :],
                                              start=True, stop=True)
                    mm.then_inc(up_product, 1)
                if m:
                    pe.wait_ge(hidden_done, m.n + 1)
                    if past(m.n):
                        pe.wait_ge(x_updated, m.n)
                    for c in range(PARTS):
                        mm = nc.tensor.matmul(o_bank[:, 0:D], hidden[:, m.parity, c, :], weight("wa_fc2", c),
                                              start=(c == 0), stop=(c == PARTS - 1))
                    mm.then_inc(o_product, 1)

        @block.scalar
        def _(act):
            act.wait_ge(made, 1)
            for step in steps(act, GROUPS, PEEL, DEEPEST, BODY):
                f, n = step.group(LAG_TURN), step.group(LAG_UP)
                if f:
                    act.wait_ge(turned, f.n + 1)
                    if past(f.n - 1):
                        act.wait_ge(up_product, f.n - 1)
                    nc.scalar.activation(x_t[:, f.parity, :], xt_bank[:, 0:P], ACT.Identity,
                                         bias=column("wa_b2"), scale=column("wa_g2")).then_inc(x_copied, 1)
                if n:
                    act.wait_ge(up_product, n.n + 1)
                    if past(n.n - 1):
                        act.wait_ge(o_product, n.n - 1)
                    for c in range(PARTS):
                        last = nc.scalar.activation(hidden[:, n.parity, c, :], up_bank[n.parity][:, c, :], ACT.Gelu,
                                                    bias=column("wa_bfc1", c, 1))
                    last.then_inc(hidden_done, 1)

        @block.vector
        def _(dve):
            dve.wait_ge(shared["loaded"], shared["loaded_count"])
            dve.wait_ge(shared["params"], shared["params_count"])
            norm.fold_on_vector(dve)
            dve.sem_inc(made, 1)
            for step in steps(dve, GROUPS, PEEL, DEEPEST, BODY):
                g, m = step.group(LAG_LN), step.group(LAG_DOWN)
                s = step.group(LAG_STATS)
                if g:
                    if past(g.n - 1):
                        dve.wait_ge(turned, g.n - 1)
                    norm.rows_on_vector(dve, xn[:, g.parity, :], inner, g.n, PEEL - 1).then_inc(xn_done, 1)
                if s:
                    dve.wait_ge(x_updated, s.n + 1)
                    norm.stats_on_vector(x, s.n)
                if m:
                    dve.wait_ge(o_product, m.n + 1)
                    dve.wait_ge(x_biased, m.n + 1)
                    nc.vector.tensor_tensor(x[:, bass.ds(m.n * D, D)], o_bank[:, 0:D], x_bias[:, m.parity, :],
                                            ALU.add).then_inc(x_updated, 1)


def mixture(nc, shared, out_rows, stored):
    with ExitStack() as stack:
        mem = Memory(nc, stack, "moe")
        x, const, weight = (shared[k] for k in ("x", "const", "weight"))
        OUTS = EXPERTS + 1
        x_t = mem.sbuf("x_t", [P, GROUPS * P])
        share = mem.sbuf("share", [P, GROUPS, OUTS])

        choose_experts = route_tokens(nc, shared, mem, x_t, share)

        TILES = 4
        CHUNK = TILES * P
        N_CHUNKS = GROUPS // TILES
        HIDDEN = EXPERTS + 2
        RING = 3
        hidden = mem.sbuf("hidden", [P, RING, CHUNK])
        gate = mem.sbuf("gate", [P, CHUNK])
        up = mem.sbuf("up", [P, CHUNK])
        hidden_bank = [mem.psum(f"hidden_bank{i}", [P, CHUNK]) for i in range(2)]
        out_bank = [mem.psum(f"out_bank{i}", [P, TILES, D]) for i in range(RING)]
        (hidden_product, silu_done, shared_done, out_product, added) = (
            mem.sem(k) for k in ("hidden_product", "silu_done", "shared_done",
                                 "out_product", "added"))
        block = stack.enter_context(nc.Block())

        def chunks_of(engine):
            yield 0
            with engine.Fori(1, N_CHUNKS) as c:
                yield c

        def expert_of(k):
            return (0, EXPERTS)[k] if k < 2 else k - 1

        @block.sync
        def _(sp):
            for c in chunks_of(sp):
                sp.wait_ge(added, (c + 1) * OUTS)
                sp.dma_start(out_rows[:, bass.ds(c * TILES, TILES), :],
                             x[:, bass.ds(c * CHUNK, CHUNK)].rearrange("p (n d) -> p n d", d=D)).then_inc(stored, 16)
            sp.wait_ge(stored, 16 * N_CHUNKS)

        @block.tensor
        def _(pe):
            for c in chunks_of(pe):
                for i in range(HIDDEN + 2):
                    if i < HIDDEN:
                        w = weight("moe_gate_up", 1 - i) if i < 2 else weight("moe_w1", i - 2)
                        if past(c * HIDDEN + (i - 1)):
                            pe.wait_ge(silu_done, c * HIDDEN + (i - 1))
                        nc.tensor.matmul(hidden_bank[i % 2][:, :], w, x_t[:, bass.ds(c * CHUNK, CHUNK)],
                                         start=True, stop=True).then_inc(hidden_product, 1)
                    if i >= 3:
                        k = i - 3
                        if k == 1:
                            pe.wait_ge(shared_done, c + 1)
                        else:
                            pe.wait_ge(silu_done, c * HIDDEN + max(k + 2, 3))
                        if past(c * OUTS + (k - 2)):
                            pe.wait_ge(added, c * OUTS + (k - 2))
                        w = weight("moe_down") if k == 1 else weight("moe_w2", expert_of(k))
                        for j in range(TILES):
                            mm = nc.tensor.matmul(out_bank[k % RING][:, j, :], hidden[:, k % RING, j * P:(j + 1) * P],
                                                  w, start=True, stop=True)
                        mm.then_inc(out_product, 1)

        @block.scalar
        def _(act):
            for c in chunks_of(act):
                for i in range(HIDDEN):
                    act.wait_ge(hidden_product, c * HIDDEN + (i + 1))
                    if i == 0:
                        if past(c):
                            act.wait_ge(shared_done, c)
                        last = nc.scalar.activation(up[:, :], hidden_bank[i % 2][:, :], ACT.Copy)
                    elif i == 1:
                        last = nc.scalar.activation(gate[:, :], hidden_bank[i % 2][:, :], ACT.Silu)
                    else:
                        k = 0 if i == 2 else i - 1
                        if past(c * OUTS + (k - 2)):
                            act.wait_ge(out_product, c * OUTS + (k - 2))
                        last = nc.scalar.activation(hidden[:, k % RING, :], hidden_bank[i % 2][:, :], ACT.Silu)
                    last.then_inc(silu_done, 1)

        @block.vector
        def _(dve):
            for c in chunks_of(dve):
                dve.wait_ge(silu_done, c * HIDDEN + 2)
                if past(c * OUTS - 1):
                    dve.wait_ge(out_product, c * OUTS - 1)
                nc.vector.tensor_tensor(hidden[:, 1, :], gate[:, :], up[:, :], ALU.mult).then_inc(shared_done, 1)
                if isinstance(c, int):
                    choose_experts(dve)
                for k in range(OUTS):
                    dve.wait_ge(out_product, c * OUTS + (k + 1))
                    if past(c * OUTS + k):
                        dve.wait_ge(added, c * OUTS + k)
                    for j in range(TILES):
                        rows = x[:, bass.ds((c * TILES + j) * D, D)]
                        last = nc.vector.scalar_tensor_tensor(
                            out=rows, in0=out_bank[k % RING][:, j, :],
                            scalar=share[:, bass.ds(c * TILES + j, 1), expert_of(k):expert_of(k) + 1].rearrange("p n e -> p (n e)"),
                            in1=rows, op0=ALU.mult, op1=ALU.add)
                    last.then_inc(added, 1)


def route_tokens(nc, shared, mem, x_t, share):
    x, const, weight = (shared[k] for k in ("x", "const", "weight"))
    LAG_LN, LAG_TURN, LAG_LOGIT = 0, 1, 2
    PEEL, DEEPEST = 4, 2
    norm = shared["norm"]
    BATCH = 4
    BATCHES = GROUPS // BATCH
    xn = mem.sbuf("xn", [P, 2, BATCH, D])
    xn_done = mem.sem("xn_done")
    own_t = mem.sbuf("own_t", [P, 2, BATCH, P])
    logits = mem.sbuf("logits", [P, GROUPS, EXPERTS + 1])
    probs = mem.sbuf("probs", [P, GROUPS, EXPERTS])
    rest = mem.sbuf("rest", [P, GROUPS, EXPERTS])
    ranks = mem.sbuf("ranks", [P, GROUPS, EXPERTS])
    chosen = mem.sbuf("chosen", [P, GROUPS, EXPERTS])
    one = mem.sbuf("one", [P, GROUPS])
    half_tanh = mem.sbuf("half_tanh", [P, GROUPS])
    xt_bank, logit_bank = (mem.psum(k, [P, 512]) for k in ("xt_bank", "logit_bank"))
    (made, turned, own_copied, kept, logit_product, logit_copied, chain, exped, tanh_done) = (
        mem.sem(k) for k in ("made", "turned", "own_copied", "kept", "logit_product", "logit_copied",
                             "chain", "exped", "tanh_done"))
    whole = [P, GROUPS, EXPERTS]

    def wide(column_per_group):
        return column_per_group.rearrange("p (n o) -> p n o", o=1).broadcast_to(whole)

    with nc.Block() as block:

        @block.gpsimd
        def _(pool):
            clear_finished(nc, shared, mem)
            pool.wait_ge(made, 1)
            for piece in range(len(norm.PIECES)):
                norm.rstd_on_gpsimd(pool, piece, shared["minus_half"])
            for step in steps(pool, BATCHES, PEEL, DEEPEST):
                g, f = step.group(LAG_LN), step.group(LAG_TURN)
                if f:
                    pool.wait_ge(own_copied, f.n + 1)
                    pool.wait_ge(made, 1)
                    nc.gpsimd.tensor_copy(x_t[:, bass.ds(f.n * BATCH * P, BATCH * P)],
                                          own_t[:, f.parity, :, :].rearrange("p i k -> p (i k)")).then_inc(kept, 1)

        @block.tensor
        def _(pe):
            pe.wait_ge(made, 1)
            for step in steps(pe, BATCHES, PEEL, DEEPEST):
                f, n = step.group(LAG_TURN), step.group(LAG_LOGIT)
                if f:
                    pe.wait_ge(xn_done, f.n + 1)
                    if past(f.n):
                        pe.wait_ge(own_copied, f.n)
                    for i in range(BATCH):
                        mm = nc.tensor.transpose(xt_bank[:, i * P:(i + 1) * P], xn[:, f.parity, i, :], const["identity"])
                    mm.then_inc(turned, 1)
                if n:
                    pe.wait_ge(own_copied, n.n + 1)
                    if past(n.n):
                        pe.wait_ge(logit_copied, n.n)
                    for i in range(BATCH):
                        mm = nc.tensor.matmul(logit_bank[:, i * (EXPERTS + 1):(i + 1) * (EXPERTS + 1)],
                                              own_t[:, n.parity, i, :], shared["router"], start=True, stop=True)
                    mm.then_inc(logit_product, 1)

        @block.scalar
        def _(act):
            act.wait_ge(made, 1)
            for step in steps(act, BATCHES, PEEL, DEEPEST):
                f, n = step.group(LAG_TURN), step.group(LAG_LOGIT)
                if f:
                    act.wait_ge(turned, f.n + 1)
                    if past(f.n - 1):
                        act.wait_ge(logit_product, f.n - 1)
                        act.wait_ge(kept, f.n - 1)
                    nc.scalar.activation(own_t[:, f.parity, :, :].rearrange("p i k -> p (i k)"), xt_bank[:, :],
                                         ACT.Copy).then_inc(own_copied, 1)
                if n:
                    act.wait_ge(logit_product, n.n + 1)
                    act.wait_ge(made, 1)
                    nc.scalar.activation(logits[:, bass.ds(n.n * BATCH, BATCH), :].rearrange("p n e -> p (n e)"),
                                         logit_bank[:, 0:BATCH * (EXPERTS + 1)], ACT.Copy).then_inc(logit_copied, 1)
            act.wait_ge(logit_copied, BATCHES)
            nc.scalar.activation(half_tanh[:, :], logits[:, :, EXPERTS], ACT.Tanh, scale=0.5).then_inc(tanh_done, 1)
            act.wait_ge(chain, 2)
            nc.scalar.activation(probs[:, :, :], rest[:, :, :], ACT.Exp).then_inc(exped, 1)

        @block.vector
        def _(dve):
            dve.wait_ge(shared["loaded"], shared["loaded_count"])
            dve.wait_ge(shared["params"], shared["params_count"])
            dve.sem_inc(made, 1)
            norm.fold_on_vector(dve)
            for step in steps(dve, BATCHES, PEEL, DEEPEST):
                g = step.group(LAG_LN)
                if g:
                    if past(g.n - 1):
                        dve.wait_ge(turned, g.n - 1)
                    for i in range(BATCH):
                        last = norm.rows_on_vector(dve, xn[:, g.parity, i, :], x, g.n * BATCH + i,
                                                   PEEL * BATCH - 1)
                    last.then_inc(xn_done, 1)
            dve.wait_ge(logit_copied, BATCHES)
            nc.vector.tensor_reduce(one[:, :], logits[:, :, 0:EXPERTS], AXIS_X, ALU.max).then_inc(chain, 1)
            dve.wait_ge(chain, 1)
            nc.vector.tensor_tensor(rest[:, :, :], logits[:, :, 0:EXPERTS], wide(one[:, :]), ALU.subtract).then_inc(chain, 1)

    def choose_experts(dve):
        count = [2]

        def then(instruction):
            count[0] += 1
            instruction.then_inc(chain, 1)
            dve.wait_ge(chain, count[0])

        rank = const["expert_rank"].rearrange("p (o e) -> p o e", o=1).broadcast_to(whole)
        dve.wait_ge(exped, 1)
        then(nc.vector.tensor_reduce(one[:, :], probs[:, :, :], AXIS_X, ALU.add))
        then(nc.vector.reciprocal(one[:, :], one[:, :]))
        then(nc.vector.tensor_tensor(probs[:, :, :], probs[:, :, :], wide(one[:, :]), ALU.mult))
        then(nc.vector.tensor_copy(rest[:, :, :], probs[:, :, :]))
        for turn in range(2):
            then(nc.vector.tensor_reduce(one[:, :], rest[:, :, :], AXIS_X, ALU.max))
            then(nc.vector.tensor_tensor(ranks[:, :, :], rest[:, :, :], wide(one[:, :]), ALU.is_equal))
            then(nc.vector.tensor_tensor(ranks[:, :, :], ranks[:, :, :], rank, ALU.mult))
            then(nc.vector.tensor_reduce(one[:, :], ranks[:, :, :], AXIS_X, ALU.max))
            then(nc.vector.tensor_tensor(chosen[:, :, :], ranks[:, :, :], wide(one[:, :]), ALU.is_equal))
            if turn == 0:
                then(nc.vector.tensor_tensor(share[:, :, 0:EXPERTS], chosen[:, :, :], probs[:, :, :], ALU.mult))
                then(nc.vector.scalar_tensor_tensor(out=rest[:, :, :], in0=chosen[:, :, :], scalar=-2.0,
                                                    in1=rest[:, :, :], op0=ALU.mult, op1=ALU.add))
            else:
                then(nc.vector.tensor_tensor(chosen[:, :, :], chosen[:, :, :], probs[:, :, :], ALU.mult))
                then(nc.vector.tensor_tensor(share[:, :, 0:EXPERTS], share[:, :, 0:EXPERTS], chosen[:, :, :],
                                             ALU.add))
        dve.wait_ge(tanh_done, 1)
        then(nc.vector.tensor_scalar(share[:, :, EXPERTS], half_tanh[:, :], 0.5, 0.5, ALU.mult, ALU.add))

    return choose_experts


def program(nc, x_in, ctx_t, ctx_rows, ctx_last, mask, constants, matrices, columns, rows, window_bias, out):
    with ExitStack() as stack:
        mem = Memory(nc, stack, "all")
        matrix_at, matrix_width = offsets(MATRICES)
        column_at, column_width = offsets(COLUMNS)
        row_at, row_width = offsets(ROWS)
        const_at, const_width = offsets({k: CONST_WIDTH[k] for k in CONSTANTS})
        x = mem.sbuf("x", [P, GROUPS * D])
        const_sb = mem.sbuf("constants", [P, const_width])
        matrix_sb = mem.sbuf("matrices", [P, matrix_width])
        column_sb = mem.sbuf("columns", [P, column_width])
        row_sb = mem.sbuf("rows", [P, row_width])
        distance_bias = mem.sbuf("distance_bias", [P, H, S])
        minus_half = mem.sbuf("minus_half", [P, 1])
        PIECE = 8
        x_loaded = [mem.sem(f"x_loaded{i}") for i in range(GROUPS // PIECE)]
        params, rest_loaded, stored = mem.sem("params"), mem.sem("rest_loaded"), mem.sem("stored")

        def piece(tile, where):
            def get(name, part=None, width=D):
                at, whole = where[name]
                return tile[:, at:at + whole] if part is None else tile[:, at + part * width:at + (part + 1) * width]
            return get

        norm = Norm(nc, mem)
        shared = {"norm": norm, "finished": [], "x": x,
                  "weight": piece(matrix_sb, matrix_at), "column": piece(column_sb, column_at),
                  "row": piece(row_sb, row_at), "minus_half": minus_half,
                  "const": {k: const_sb[:, at:at + w] for k, (at, w) in const_at.items()},
                  "router": matrix_sb[:, matrix_at["moe_router"][0]:matrix_at["moe_gate_w"][0] + 1],
                  "loaded": x_loaded[-1], "loaded_count": 16, "params": params, "params_count": 16 * 4 + 1}
        first_width = matrix_at["sa_q"][0]
        x_pieces = [slice(i * PIECE, (i + 1) * PIECE) for i in range(GROUPS // PIECE)]
        x_rows = x_in.rearrange("(n b) q d -> (b q) n d", b=BG)
        out_rows = out.rearrange("(n b) q d -> (b q) n d", b=BG)

        def load_x(sp):
            for piece, done in zip(x_pieces, x_loaded):
                sp.dma_start(x[:, piece.start * D:piece.stop * D].rearrange("p (n d) -> p n d", d=D),
                             x_rows[:, piece, :]).then_inc(done, 16)

        def load_rest(sp):
            sp.dma_start(matrix_sb[:, first_width:], matrices[:, first_width:]).then_inc(rest_loaded, 16)
            for b in range(BG):
                sp.dma_start(distance_bias[b * S:(b + 1) * S, :, :].rearrange("p h k -> p (h k)"),
                             window_bias).then_inc(rest_loaded, 16)

        def load_params(act):
            act.dma_start(const_sb[:, :], constants).then_inc(params, 16)
            act.dma_start(matrix_sb[:, 0:first_width], matrices[:, 0:first_width]).then_inc(params, 16)
            act.dma_start(row_sb[:, :], rows.broadcast_to([P, row_width])).then_inc(params, 16)
            act.dma_start(column_sb[:, :], columns).then_inc(params, 16)

        def first_stats(dve):
            nc.vector.memset(minus_half[:, :], -0.5).then_inc(params, 1)
            for piece, done in zip(x_pieces, x_loaded):
                dve.wait_ge(done, 16)
                for n in range(piece.start, piece.stop):
                    norm.stats_on_vector(x, n)

        start = {"load_x": load_x, "load_rest": load_rest, "load_params": load_params, "first_stats": first_stats}
        cross_attention(nc, shared, ctx_t, mask, start, rest_loaded)
        norm.next_layer()
        self_attention(nc, shared, "sa", windowed=False)
        norm.next_layer()
        context = Context(mem, ctx_t, ctx_rows, ctx_last)
        channel_mix(nc, shared, context)
        norm.next_layer()
        similarity_attention(nc, shared, context)
        norm.next_layer()
        inner = mem.sbuf("inner", [P, GROUPS * D])
        self_attention(nc, shared, "wa", windowed=True, distance_bias=distance_bias, inner=inner)
        norm.next_layer()
        gelu_block(nc, shared, inner)
        norm.next_layer()
        mixture(nc, shared, out_rows, stored)


def kernel(**inputs):
    import numpy as _np
    import concourse.bacc as _bacc
    from concourse import mybir as _mybir
    from concourse.bass_utils import run_bass_kernel_spmd as _run

    a = {k: _np.asarray(v) for k, v in inputs.items()}

    def chunks(w):
        return w.reshape(-1, P, w.shape[-1]).transpose(1, 0, 2).reshape(P, -1)

    matrices = {
        "xa_q": a["L0_xattn_wq"].T, "xa_k": a["L0_xattn_wk"].T, "xa_v": a["L0_xattn_wv"].T,
        "xa_o": a["L0_xattn_wo"].T,
        "sa_q": a["L0_attn_Wq"], "sa_k": a["L0_attn_Wk"], "sa_v": a["L0_attn_Wv"], "sa_o": a["L0_attn_Wo"],
        "cm_r": a["L0_ffn_W_r"].T, "cm_k": a["L0_ffn_W_k"].T, "cm_v": a["L0_ffn_W_v"].T,
        "bi_qv": chunks(a["L1_xattn_W_qv"]),
        "wa_qkv": a["L1_attn_qkv_w"], "wa_gate": a["L1_attn_gate_w"], "wa_o": a["L1_attn_out_w"],
        "wa_fc1": a["L1_attn_fc1_w"], "wa_fc2": chunks(a["L1_attn_fc2_w"]),
        "moe_router": a["L1_ffn_router_w"], "moe_gate_w": a["L1_ffn_shared_gate_w"],
        "moe_w1": a["L1_ffn_w1"].transpose(1, 0, 2).reshape(P, -1),
        "moe_w2": a["L1_ffn_w2"].transpose(1, 0, 2).reshape(P, -1),
        "moe_gate_up": a["L1_ffn_shared_gate_up"], "moe_down": a["L1_ffn_shared_down"],
    }
    w_sim = a["L1_xattn_w_sim"].reshape(3, D)
    columns = {
        "xa_bq": a["L0_xattn_bq"], "xa_bk": a["L0_xattn_bk"], "xa_bv": a["L0_xattn_bv"],
        "sa_bq": a["L0_attn_bq"], "sa_bk": a["L0_attn_bk"], "sa_bv": a["L0_attn_bv"],
        "cm_mu_r": a["L0_ffn_mu_r"], "cm_mu_k": a["L0_ffn_mu_k"], "bi_w2": w_sim[1], "bi_w3": w_sim[2],
        "wa_g1": a["L1_attn_ln1_g"], "wa_b1": a["L1_attn_ln1_b"], "wa_bqkv": a["L1_attn_qkv_b"],
        "wa_bgate": a["L1_attn_gate_b"], "wa_g2": a["L1_attn_ln2_g"], "wa_b2": a["L1_attn_ln2_b"],
        "wa_bfc1": a["L1_attn_fc1_b"],
    }
    rows = {"xa_bo": a["L0_xattn_bo"], "sa_bo": a["L0_attn_bo"], "bi_w1": w_sim[0],
            "bi_bqv": a["L1_xattn_b_qv"], "wa_bo": a["L1_attn_out_b"], "wa_bfc2": a["L1_attn_fc2_b"],
            "bi_b": a["L1_xattn_b_sim"]}
    ctx = a["ctx_1024"]
    distance = _np.maximum(_np.arange(S)[:, None] - _np.arange(S)[None, :], 0)
    toeplitz = a["L1_attn_pos_bias"][distance].transpose(0, 2, 1).reshape(S, H * S)
    constants = shape_constants()
    arrays = {
        "x": a["x"],
        "ctx_t": ctx.transpose(2, 0, 1).reshape(D, B * KEYS),
        "ctx_rows": ctx[:, :LAST].reshape(B, CHUNKS, P, D).transpose(2, 0, 1, 3).reshape(P, B * CHUNKS * D),
        "ctx_last": ctx[:, LAST],
        "mask": a["mask_BxS2_ff1"].reshape(1, B * KEYS),
        "constants": _np.concatenate([constants[k] for k in CONSTANTS], axis=1),
        "matrices": _np.concatenate([matrices[k] for k in MATRICES], axis=1),
        "columns": _np.concatenate([columns[k].reshape(-1, P) for k in COLUMNS], axis=0).T,
        "rows": _np.concatenate([rows[k] for k in ROWS]).reshape(1, -1),
        "window_bias": toeplitz,
    }
    arrays = {f"in_{k}_dram": _np.ascontiguousarray(v) for k, v in arrays.items()}
    nc = _bacc.Bacc("TRN2", target_bir_lowering=False, num_devices=1)
    args = [nc.dram_tensor(k, v.shape, _mybir.dt.from_np(v.dtype), kind="ExternalInput").ap()
            for k, v in arrays.items()]
    out = nc.dram_tensor("out_dram", a["x"].shape, F32, kind="ExternalOutput").ap()
    program(nc, *args, out)
    r = _run(nc, [arrays], core_ids=[0])
    return r.results[0]["out_dram"]
```
